# Optimizing a Trainium2 kernel written in Bass

```python
import numpy as np
import jax
import jax.numpy as jnp

def _softmax(x, axis=-1):
    return jax.nn.softmax(x, axis=axis)

def _gelu(x):
    return jax.nn.gelu(x, approximate=True)

def _silu(x):
    return jax.nn.silu(x)

def _sigmoid(x):
    return jax.nn.sigmoid(x)

def _layernorm(x, axis=-1, eps=1e-05):
    m = jnp.mean(x, axis=axis, keepdims=True)
    v = jnp.var(x, axis=axis, keepdims=True)
    return (x - m) / jnp.sqrt(v + eps)

def _scatter_add(tgt, idx, src, axis=0):
    return tgt.at[idx].add(src)

def _segment_sum(src, seg, n):
    return jax.ops.segment_sum(src, seg, n)
kernel_name = 'mk_decoder_postln_d1_seqx_r4_be1f2b'

def setup_inputs(seed: int=0):
    np.random.seed(seed)
    _w = jnp.asarray

    def _rec_inputs():
        import jax
        import jax.numpy as jnp
        _rk = jax.random.key(seed)
        x = -0.0002928 + 1 * jax.random.normal(jax.random.fold_in(_rk, 1), (16, 128, 256), jnp.float32)
        _lenS = 128 - jax.random.randint(jax.random.fold_in(_rk, 7), (16,), 0, max(1, 128 // 4) + 1, jnp.int32)
        _lenS2 = 128 - jax.random.randint(jax.random.fold_in(_rk, 8), (16,), 0, max(1, 128 // 4) + 1, jnp.int32)
        _ctx_1024P = jax.random.normal(jax.random.fold_in(_rk, 11), (16, 16, 256), jnp.float32)
        _ctx_1024c = jax.random.dirichlet(jax.random.fold_in(_rk, 511), 0.3 * jnp.ones((16,), jnp.float32), (16, 128))
        _ctx_1024t = jnp.einsum('bsk,bkd->bsd', _ctx_1024c, _ctx_1024P)
        _ctx_1024t = _ctx_1024t * jax.lax.rsqrt(jnp.mean(jnp.square(_ctx_1024t)) + 1e-12) * 0.953939
        ctx_1024 = -1.39393e-06 + 0.999914 * (_ctx_1024t + 0.3 * jax.random.normal(jax.random.fold_in(_rk, 611), (16, 128, 256), jnp.float32))
        return (x, ctx_1024)
    x, ctx_1024 = _rec_inputs()

    def _L0_attn_setup():
        import jax, jax.numpy as jnp
        import numpy as np
        B, N, C, H = (4, 2048, 256, 16)
        D = C // H
        EPS = 1e-05
        key = jax.random.key(seed)
        ks = jax.random.split(key, 10)
        s = 1.0 / np.sqrt(C)
        return {'x': jax.random.normal(ks[0], (B, N, C), jnp.float32), 'Wq': jax.random.uniform(ks[1], (C, C), jnp.float32, -s, s), 'bq': jax.random.uniform(ks[2], (C,), jnp.float32, -s, s), 'Wk': jax.random.uniform(ks[3], (C, C), jnp.float32, -s, s), 'bk': jax.random.uniform(ks[4], (C,), jnp.float32, -s, s), 'Wv': jax.random.uniform(ks[5], (C, C), jnp.float32, -s, s), 'bv': jax.random.uniform(ks[6], (C,), jnp.float32, -s, s), 'Wo': jax.random.uniform(ks[7], (C, C), jnp.float32, -s, s), 'bo': jax.random.uniform(ks[8], (C,), jnp.float32, -s, s), 'ln_g': jnp.ones((C,), jnp.float32), 'ln_b': jnp.zeros((C,), jnp.float32)}
    _L0_attn_all = _L0_attn_setup()
    _L0_attn_in = {k: v for k, v in _L0_attn_all.items() if k in ('Wq', 'bq', 'Wk', 'bk', 'Wv', 'bv', 'Wo', 'bo', 'ln_g', 'ln_b')}
    del _L0_attn_all

    def _L0_xattn_setup():
        import jax, jax.numpy as jnp
        import numpy as np
        D_MODEL = 256
        N_HEADS = 16
        D_KEYS = D_MODEL // N_HEADS
        key = jax.random.key(seed)
        ks = jax.random.split(key, 11)
        B, L, S = (2, 512, 512)
        inp = {'queries': jax.random.normal(ks[0], (B, L, D_MODEL), dtype=jnp.float32), 'keys': jax.random.normal(ks[1], (B, S, D_MODEL), dtype=jnp.float32), 'values': jax.random.normal(ks[2], (B, S, D_MODEL), dtype=jnp.float32), 'Wq': jax.random.normal(ks[3], (D_MODEL, D_MODEL), dtype=jnp.float32) / np.sqrt(D_MODEL), 'bq': jax.random.normal(ks[4], (D_MODEL,), dtype=jnp.float32) / np.sqrt(D_MODEL), 'Wk': jax.random.normal(ks[5], (D_MODEL, D_MODEL), dtype=jnp.float32) / np.sqrt(D_MODEL), 'bk': jax.random.normal(ks[6], (D_MODEL,), dtype=jnp.float32) / np.sqrt(D_MODEL), 'Wv': jax.random.normal(ks[7], (D_MODEL, D_MODEL), dtype=jnp.float32) / np.sqrt(D_MODEL), 'bv': jax.random.normal(ks[8], (D_MODEL,), dtype=jnp.float32) / np.sqrt(D_MODEL), 'Wo': jax.random.normal(ks[9], (D_MODEL, D_MODEL), dtype=jnp.float32) / np.sqrt(D_MODEL), 'bo': jax.random.normal(ks[10], (D_MODEL,), dtype=jnp.float32) / np.sqrt(D_MODEL)}
        return inp
    _L0_xattn_all = _L0_xattn_setup()
    _L0_xattn_in = {k: v for k, v in _L0_xattn_all.items() if k in ('Wq', 'bq', 'Wk', 'bk', 'Wv', 'bv', 'Wo', 'bo')}
    del _L0_xattn_all

    def _L0_ffn_setup():
        import jax, jax.numpy as jnp
        import numpy as np
        B, S, D = (2, 256, 256)
        E, H, K, G = (8, 512, 2, 64)
        key = jax.random.key(seed)
        ks = jax.random.split(key, 5)
        return {'x': jax.random.normal(ks[0], (B, S, D), jnp.float32), 'wg1': jax.random.normal(ks[1], (D, G), jnp.float32) * 0.02, 'bg1': jnp.zeros((G,), jnp.float32), 'wg2': jax.random.normal(ks[2], (G, E), jnp.float32) * 0.02, 'w_in': jax.random.uniform(ks[3], (E, D, H), jnp.float32, -1.0 / D, 1.0 / D), 'w_out': jax.random.uniform(ks[4], (E, H, D), jnp.float32, -1.0 / H, 1.0 / H)}
    _L0_ffn_all = _L0_ffn_setup()
    _L0_ffn_in = {k: v for k, v in _L0_ffn_all.items() if k in ('wg1', 'bg1', 'wg2', 'w_in', 'w_out')}
    del _L0_ffn_all
    return {'x': x, 'ctx_1024': ctx_1024, 'L0_attn_Wq': _L0_attn_in['Wq'], 'L0_attn_bq': _L0_attn_in['bq'], 'L0_attn_Wk': _L0_attn_in['Wk'], 'L0_attn_bk': _L0_attn_in['bk'], 'L0_attn_Wv': _L0_attn_in['Wv'], 'L0_attn_bv': _L0_attn_in['bv'], 'L0_attn_Wo': _L0_attn_in['Wo'], 'L0_attn_bo': _L0_attn_in['bo'], 'L0_attn_ln_g': _L0_attn_in['ln_g'], 'L0_attn_ln_b': _L0_attn_in['ln_b'], 'L0_xattn_Wq': _L0_xattn_in['Wq'], 'L0_xattn_bq': _L0_xattn_in['bq'], 'L0_xattn_Wk': _L0_xattn_in['Wk'], 'L0_xattn_bk': _L0_xattn_in['bk'], 'L0_xattn_Wv': _L0_xattn_in['Wv'], 'L0_xattn_bv': _L0_xattn_in['bv'], 'L0_xattn_Wo': _L0_xattn_in['Wo'], 'L0_xattn_bo': _L0_xattn_in['bo'], 'L0_ffn_wg1': _L0_ffn_in['wg1'], 'L0_ffn_bg1': _L0_ffn_in['bg1'], 'L0_ffn_wg2': _L0_ffn_in['wg2'], 'L0_ffn_w_in': _L0_ffn_in['w_in'], 'L0_ffn_w_out': _L0_ffn_in['w_out']}

def reference(x, ctx_1024, L0_attn_Wq, L0_attn_bq, L0_attn_Wk, L0_attn_bk, L0_attn_Wv, L0_attn_bv, L0_attn_Wo, L0_attn_bo, L0_attn_ln_g, L0_attn_ln_b, L0_xattn_Wq, L0_xattn_bq, L0_xattn_Wk, L0_xattn_bk, L0_xattn_Wv, L0_xattn_bv, L0_xattn_Wo, L0_xattn_bo, L0_ffn_wg1, L0_ffn_bg1, L0_ffn_wg2, L0_ffn_w_in, L0_ffn_w_out):
    import jax
    import jax.numpy as jnp

    def _L0_attn_ref(x, Wq, bq, Wk, bk, Wv, bv, Wo, bo, ln_g, ln_b):
        import jax, jax.numpy as jnp
        import numpy as np
        B, N, C, H = (4, 2048, 256, 16)
        D = C // H
        EPS = 1e-05
        b, n, c = x.shape
        q = x @ Wq.T + bq
        k = x @ Wk.T + bk
        v = x @ Wv.T + bv
        split = lambda z: z.reshape(b, n, H, D).transpose(0, 2, 1, 3)
        q, k, v = (split(q), split(k), split(v))
        q = jax.nn.softmax(q, axis=-1)
        k = jax.nn.softmax(k, axis=-2)
        state = jnp.einsum('bhnd,bhne->bhde', k, v)
        out = jnp.einsum('bhnd,bhde->bhne', q, state)
        out = out.transpose(0, 2, 1, 3).reshape(b, n, c)
        mu = out.mean(-1, keepdims=True)
        var = out.var(-1, keepdims=True)
        out = (out - mu) * jax.lax.rsqrt(var + EPS) * ln_g + ln_b
        return out @ Wo.T + bo

    def _L0_xattn_ref(queries, keys, values, Wq, bq, Wk, bk, Wv, bv, Wo, bo):
        import jax, jax.numpy as jnp
        import numpy as np
        D_MODEL = 256
        N_HEADS = 16
        D_KEYS = D_MODEL // N_HEADS
        B, L, _ = queries.shape
        S = keys.shape[1]
        H, E = (N_HEADS, D_KEYS)
        scale = E ** (-0.5)
        q = (queries @ Wq.T + bq).reshape(B, L, H, E)
        k = (keys @ Wk.T + bk).reshape(B, S, H, E)
        v = (values @ Wv.T + bv).reshape(B, S, H, E)
        scores = jnp.einsum('blhe,bshe->bhls', q, k)
        attn = jax.nn.softmax(scores * scale, axis=-1)
        out = jnp.einsum('bhls,bshe->blhe', attn, v).reshape(B, L, H * E)
        return out @ Wo.T + bo

    def _L0_ffn_ref(x, wg1, bg1, wg2, w_in, w_out):
        import jax, jax.numpy as jnp
        import numpy as np
        B, S, D = (2, 256, 256)
        E, H, K, G = (8, 512, 2, 64)
        b, s, d = x.shape
        xt = x.reshape(-1, d)
        n = xt.shape[0]
        g = jax.nn.gelu(xt @ wg1 + bg1, approximate=False)
        logits = g @ wg2
        probs = jax.nn.softmax(logits, axis=-1)
        top_vals, top_idx = jax.lax.top_k(probs, K)
        gates = jnp.zeros_like(probs).at[jnp.arange(n)[:, None], top_idx].set(top_vals)
        h = jax.nn.gelu(jnp.einsum('nd,edh->enh', xt, w_in), approximate=False)
        o = jnp.einsum('enh,ehd->end', h, w_out)
        y = jnp.einsum('ne,end->nd', gates, o)
        return y.reshape(b, s, d)
    x = _layernorm(x + _L0_attn_ref(x, L0_attn_Wq, L0_attn_bq, L0_attn_Wk, L0_attn_bk, L0_attn_Wv, L0_attn_bv, L0_attn_Wo, L0_attn_bo, L0_attn_ln_g, L0_attn_ln_b), axis=-1)
    x = _layernorm(x + _L0_xattn_ref(x, ctx_1024, ctx_1024, L0_xattn_Wq, L0_xattn_bq, L0_xattn_Wk, L0_xattn_bk, L0_xattn_Wv, L0_xattn_bv, L0_xattn_Wo, L0_xattn_bo), axis=-1)
    x = _layernorm(x + _L0_ffn_ref(x, L0_ffn_wg1, L0_ffn_bg1, L0_ffn_wg2, L0_ffn_w_in, L0_ffn_w_out), axis=-1)
    return x

_drawn_inputs = setup_inputs


def setup_inputs(seed=0):
    import zlib

    import numpy as np

    out = dict(_drawn_inputs(seed))
    spreads = {'L0_attn_ln_g': (1.0, 0.2), 'L0_attn_ln_b': (0.0, 0.1), 'L0_ffn_bg1': (0.0, 2.0)}
    factors = {'L0_attn_bq': 8.0,
     'L0_attn_bk': 64.0,
     'L0_xattn_bq': 4.539,
     'L0_xattn_bk': 64.0,
     'L0_ffn_wg1': 26.192,
     'L0_ffn_wg2': 8.0,
     'L0_ffn_w_in': 8.0,
     'L0_ffn_w_out': 8.0}
    for name, (base, spread) in spreads.items():
        noise = np.random.default_rng([zlib.crc32(name.encode()), seed]).standard_normal(out[name].shape)
        drawn = base * np.exp(spread * noise) if base else spread * noise
        out[name] = jnp.asarray(drawn.astype(out[name].dtype))
    for name, factor in factors.items():
        out[name] = (out[name] * factor).astype(out[name].dtype)
    return out
```

```python
from contextlib import ExitStack

import numpy as np
import concourse.bass as bass
from concourse import mybir

f32 = mybir.dt.float32
f16 = mybir.dt.float16
bf16 = mybir.dt.bfloat16
ACT = mybir.ActivationFunctionType
ALU = mybir.AluOpType
AX = mybir.AxisListType

NB, S, D = 16, 128, 256
NH, DH = 16, 16
NE, HID, G = 8, 512, 64
P = 128
KC = D // P
HC = HID // P
WSCALE = 256.0
EPS = 1e-5
GT = 4
GW = GT * P
CQV, CK, CO, CQ2, CK2, CV2, CO2 = 0, 512, 768, 1024, 1280, 1536, 1792
NPW = 2048
RQV, RO, RV2, RO2, NROW = 0, 512, 768, 1024, 1280
VK, VK2, VQ2, VG, VB, NVEC = 0, 2, 4, 6, 8, 10


def decoder_layer(nc, x, ctx, wpack, rows, vecs, wg1, bg1, wg2, w_in, w_out, out):
    es = ExitStack()
    with es:
        def sb(name, shape, dt=f32):
            return es.enter_context(nc.sbuf_tensor(name, shape, dt))

        def pair(name, shape, dt=f32):
            return [sb(f"{name}{i}", shape, dt) for i in range(2)]

        def sem(name):
            return es.enter_context(nc.semaphore(name))

        ident = sb("ident", [P, P])
        identb = sb("identb", [P, P], bf16)
        blockmask = sb("blockmask", [P, P])
        evenodd = sb("evenodd", [P, 2])
        evenodd_s = sb("evenodd_s", [P, 2])
        pick = sb("pick", [P, 4, P], bf16)
        neghalf = sb("neghalf", [P, NB])
        rowb = sb("rowb", [P, NROW])
        vec = sb("vec", [P, NVEC])
        bq2s = sb("bq2s", [P, KC])
        bk2m = sb("bk2m", [P, 2, KC])
        lnb_rep = sb("lnb_rep", [P, KC, P])
        stage = sb("stage", [P, KC, NPW])
        wh = sb("wh", [P, KC, NPW], f16)
        wl = sb("wl", [P, KC, NPW], f16)
        X = pair("X", [P, D])
        C = pair("C", [P, D])
        XTh = pair("XTh", [P, KC, P], f16)
        XTl = pair("XTl", [P, KC, P], f16)
        QV = pair("QV", [P, 2 * D])
        qmax = pair("qmax", [P, NH])
        QS = pair("QS", [P, D])
        QE = pair("QE", [P, D])
        kmax = pair("kmax", [P, KC])
        knb = pair("knb", [P, KC])
        KE = pair("KE", [P, KC, P])
        ksum = pair("ksum", [P, KC])
        krec = pair("krec", [P, KC])
        QKT = pair("QKT", [P, 2 * KC, P])
        ST = pair("ST", [P, KC, P + 8])
        qrec = pair("qrec", [P, NH])
        ON = pair("ON", [P, D])
        OL = pair("OL", [P, D])
        OTh = pair("OTh", [P, KC, P], f16)
        OTl = pair("OTl", [P, KC, P], f16)
        XB = pair("XB", [P, D])
        bst = [pair(f"bst{n}_", [P, 6]) for n in range(3)]
        mv = [pair(f"mv{n}_", [P, 2]) for n in range(3)]
        nmu = [pair(f"nmu{n}_", [P, 1]) for n in range(3)]
        veps = [pair(f"veps{n}_", [P, 1]) for n in range(3)]
        rstd = [pair(f"rstd{n}_", [P, 1]) for n in range(3)]
        CTh = pair("CTh", [P, KC, P], f16)
        CTl = pair("CTl", [P, KC, P], f16)
        R1 = pair("R1", [P, D])
        X1 = pair("X1", [P, D])
        X1B = pair("X1B", [P, D])
        X1Th = pair("X1Th", [P, KC, P], f16)
        X1Tl = pair("X1Tl", [P, KC, P], f16)
        K2 = pair("K2", [P, KC, 2, P])
        Q2 = pair("Q2", [P, KC, P])
        V2 = pair("V2", [P, NH, DH + 1])
        NM = pair("NM", [P, 4, 32], bf16)
        MT = pair("MT", [P, P], bf16)
        EX = pair("EX", [P, 4, 4, P])
        r2 = pair("r2", [P, NH])
        O2 = pair("O2", [P, D])
        O2Th = pair("O2Th", [P, KC, P], f16)
        O2Tl = pair("O2Tl", [P, KC, P], f16)
        R2 = pair("R2", [P, D])
        X2 = pair("X2", [P, D])
        X2all = sb("X2all", [P, NB, D])
        X2Th = sb("X2Th", [P, KC, NB * P], f16)
        X2Tl = sb("X2Tl", [P, KC, NB * P], f16)
        x_v = x.rearrange("(i p) s d -> i p s d", p=2)
        ctx_v = ctx.rearrange("(i p) s d -> i p s d", p=2)
        X2all_v = X2all[:].rearrange("q (i p) d -> q i p d", p=2)
        X2Th_v = X2Th[:].rearrange("q c (i p t) -> q c i p t", p=2, t=P)
        X2Tl_v = X2Tl[:].rearrange("q c (i p t) -> q c i p t", p=2, t=P)
        w_in_v = w_in.rearrange("(i q) p k h -> i q p k h", q=2)
        w_out_v = w_out.rearrange("(i q) p k h -> i q p k h", q=2)
        wg1_f = sb("wg1_f", [P, KC, G])
        wg1h = sb("wg1h", [P, KC, G], f16)
        wg1l = sb("wg1l", [P, KC, G], f16)
        bg1_c = sb("bg1_c", [G, 1])
        wg2_f = sb("wg2_f", [G, NE])
        GG = sb("GG", [G, NB * P])
        L = sb("L", [P, NB, NE])
        lmax = sb("lmax", [P, NB])
        LE = sb("LE", [P, NB, NE])
        lsum = sb("lsum", [P, NB])
        lrec = sb("lrec", [P, NB])
        PR = sb("PR", [P, NB, NE])
        lower = sb("lower", [P, NE, NE])
        gates = sb("gates", [P, NB, NE])
        gates_v = gates[:].rearrange("p b (i q) -> p b i q", q=2)
        rank = sb("rank", [P, NB, NE])
        scratch = stage[:, :, :].rearrange("p k n -> p (k n)")
        CMP = scratch[:, 0:NB * NE * NE].rearrange("p (b e f) -> p b e f", b=NB, e=NE)
        CMQ = scratch[:, NB * NE * NE:2 * NB * NE * NE].rearrange("p (b e f) -> p b e f", b=NB, e=NE)
        EWF = pair("EWF", [P, 2048])
        EWH = pair("EWH", [P, 2048], f16)
        EWL = pair("EWL", [P, 2048], f16)
        HF = scratch[:, 2048:4096].rearrange("p (h t) -> p h t", h=HC)
        HH = [t[:, 0:2, :, :].rearrange("p u j t -> p (u j t)").bitcast(f16).rearrange("p (h t) -> p h t", h=HC)
              for t in EX]
        HL = [t[:, 2:4, :, :].rearrange("p u j t -> p (u j t)").bitcast(f16).rearrange("p (h t) -> p h t", h=HC)
              for t in EX]
        fst = sb("fst", [P, NB, 6])
        fmv = sb("fmv", [P, NB, 2])
        fnm = sb("fnm", [P, NB])
        fve = sb("fve", [P, NB])
        frs = sb("frs", [P, NB])

        bank = [es.enter_context(nc.psum_tensor(f"bank{i}", [P, 512], f32)) for i in range(8)]

        def chunks(t, n, w=P):
            return t[:, 0:n * w].rearrange("p (c w) -> p c w", c=n)

        s_w_ld = [sem(f"s_w_ld{q}") for q in range(4)]
        s_rows_ld, s_vec_ld, s_g_ld = sem("s_rows_ld"), sem("s_vec_ld"), sem("s_g_ld")
        s_cst, s_cstb = sem("s_cst"), sem("s_cstb")
        s_prep = sem("s_prep")
        s_lnb, s_bo_ps = sem("s_lnb"), sem("s_bo_ps")
        s_bo_fold, s_wo_fold = sem("s_bo_fold"), sem("s_wo_fold")
        s_wsp_h, s_wsp_l = sem("s_wsp_h"), sem("s_wsp_l")
        s_xld = [sem(f"s_xld{p}") for p in range(2)]
        s_cld = [sem(f"s_cld{p}") for p in range(2)]
        s_xT, s_xTh, s_xTl, s_xb = sem("s_xT"), sem("s_xTh"), sem("s_xTl"), sem("s_xb")
        s_qv_ps, s_k_ps, s_qv_sb, s_qmax = sem("s_qv_ps"), sem("s_k_ps"), sem("s_qv_sb"), sem("s_qmax")
        s_km, s_knb, s_ke, s_qs = sem("s_km"), sem("s_knb"), sem("s_ke"), sem("s_qs")
        s_qe, s_krec, s_qk_ps, s_qkT = sem("s_qe"), sem("s_krec"), sem("s_qk_ps"), sem("s_qkT")
        s_st_ps, s_st, s_o_ps, s_qrec = sem("s_st_ps"), sem("s_st"), sem("s_o_ps"), sem("s_qrec")
        s_on, s_ln0, s_onT, s_onTh = sem("s_on"), sem("s_ln0"), sem("s_onT"), sem("s_onTh")
        s_onTl = sem("s_onTl")
        s_bs = [sem(f"s_bs{n}") for n in range(3)]
        s_mv = [sem(f"s_mv{n}") for n in range(3)]
        s_nm = [sem(f"s_nm{n}") for n in range(3)]
        s_ve = [sem(f"s_ve{n}") for n in range(3)]
        s_rs = [sem(f"s_rs{n}") for n in range(3)]
        s_ao_ps, s_r1, s_x1, s_x1b = sem("s_ao_ps"), sem("s_r1"), sem("s_x1"), sem("s_x1b")
        s_cT, s_cTh, s_cTl, s_x1T = sem("s_cT"), sem("s_cTh"), sem("s_cTl"), sem("s_x1T")
        s_x1Th, s_x1Tl, s_k2_ps, s_k2 = sem("s_x1Th"), sem("s_x1Tl"), sem("s_k2_ps"), sem("s_k2")
        s_q2_ps, s_q2, s_v2_ps, s_v2 = sem("s_q2_ps"), sem("s_q2"), sem("s_v2_ps"), sem("s_v2")
        s_nat, s_mx, s_mT_ps, s_mT = sem("s_nat"), sem("s_mx"), sem("s_mT_ps"), sem("s_mT")
        s_sc, s_ex, s_pv, s_r2 = sem("s_sc"), sem("s_ex"), sem("s_pv"), sem("s_r2")
        s_o2, s_o2T, s_o2Th, s_o2Tl = sem("s_o2"), sem("s_o2T"), sem("s_o2Th"), sem("s_o2Tl")
        s_ao2, s_r2x, s_x2, s_x2T = sem("s_ao2"), sem("s_r2x"), sem("s_x2"), sem("s_x2T")
        s_x2Th, s_x2Tl = sem("s_x2Th"), sem("s_x2Tl")
        s_x2st = [sem(f"s_x2st{p}") for p in range(2)]
        s_g_ps, s_gg, s_l_ps, s_lsb = sem("s_g_ps"), sem("s_gg"), sem("s_l_ps"), sem("s_lsb")
        s_ewld = [sem(f"s_ewld{q}") for q in range(2)]
        s_ewh, s_ewl, s_up, s_hf = sem("s_ewh"), sem("s_ewl"), sem("s_up"), sem("s_hf")
        s_hh, s_hl, s_dn, s_acc = sem("s_hh"), sem("s_hl"), sem("s_dn"), sem("s_acc")
        s_fbs, s_fmv, s_fve, s_frs = sem("s_fbs"), sem("s_fmv"), sem("s_fve"), sem("s_frs")
        s_fy, s_outs = sem("s_fy"), sem("s_outs")

        def past(row, back):
            return not isinstance(row, int) or row >= back

        def split3(pe, dst, a_h, a_l, b_h, b_l, n=KC):
            for c in range(n):
                for i, (a, b) in enumerate(((a_h, b_h), (a_h, b_l), (a_l, b_h))):
                    last = pe.matmul(dst, a(c), b(c), start=(c == 0 and i == 0), stop=(c == n - 1 and i == 2))
            return last

        def pipeline(eng, order, emit, lag):
            def iteration(half, odd, live):
                for stream, step in order:
                    if stream in live:
                        at = odd - lag[stream]
                        emit(stream, step, 2 * half + at, at % 2, half + at // 2)

            def peeled(i):
                iteration(i // 2, i % 2, [st for st, back in lag.items() if 0 <= i - back < NB])
            for i in range(4):
                peeled(i)
            with eng.Fori(2, NB // 2) as half:
                for odd in range(2):
                    iteration(half, odd, list(lag))
            peeled(NB)
            peeled(NB + 1)

        LAG = {"A": 0, "B": 1, "C": 2}
        PE_ORDER = [("A", 0), ("B", 0), ("C", 0), ("A", 1), ("B", 1), ("C", 1), ("A", 2), ("B", 2), ("C", 2),
                    ("A", 3), ("B", 3), ("C", 3), ("A", 4), ("B", 4), ("C", 4), ("A", 5)]

        block = es.enter_context(nc.Block())

        @block.sync
        def _(sp):
            sp.dma_start(vec[:], vecs).then_inc(s_vec_ld, 16)
            for q in range(4):
                sp.dma_start(stage[:, :, 512 * q:512 * q + 512], wpack[:, :, 512 * q:512 * q + 512])\
                  .then_inc(s_w_ld[q], 16)
                if q == 0:
                    sp.dma_start(rowb[:], rows.partition_broadcast(P)).then_inc(s_rows_ld, 16)
            sp.dma_start(wg1_f[:], wg1).then_inc(s_g_ld, 16)
            sp.dma_start(bg1_c[:], bg1).then_inc(s_g_ld, 16)
            sp.dma_start(wg2_f[:], wg2).then_inc(s_g_ld, 16)

            def emit(stream, step, b, p, half):
                if stream == "A":
                    if past(b, 2):
                        sp.wait_ge(s_xb, b - 1)
                    if past(b, 2):
                        sp.wait_ge(s_xT, b - 1)
                    sp.dma_start(X[p][:], x_v[half, p]).then_inc(s_xld[p], 16)
                    if past(b, 2):
                        sp.wait_ge(s_cT, b - 1)
                    sp.dma_start(C[p][:], ctx_v[half, p]).then_inc(s_cld[p], 16)
                if stream == "C":
                    sp.wait_ge(s_x2, b + 1)
                    sp.dma_start(X2all_v[:, half, p, :], X2[p][:]).then_inc(s_x2st[p], 16)
            pipeline(sp, [("A", 0), ("C", 0)], emit, LAG)

            def expert_load(e, q, i=0):
                if not (isinstance(e, int) and e < 2):
                    sp.wait_ge(s_ewl, 8 * (e - 1))
                sp.dma_start(EWF[q][:, 0:1024].rearrange("p (k h) -> p k h", k=KC), w_in_v[i, q]).then_inc(s_ewld[q], 16)
                sp.dma_start(EWF[q][:, 1024:2048].rearrange("p (k h) -> p k h", k=HC), w_out_v[i, q]).then_inc(s_ewld[q], 16)
            expert_load(0, 0)
            expert_load(1, 1)
            with sp.Fori(1, NE // 2) as i:
                for q in range(2):
                    expert_load(2 * i + q, q, i)
            for g in range(NB // GT):
                sp.wait_ge(s_fy, GT * (g + 1))
                sp.dma_start(out.rearrange("b p d -> p b d")[:, GT * g:GT * g + GT, :],
                             X2all[:, GT * g:GT * g + GT, :]).then_inc(s_outs, 16)
            sp.wait_ge(s_outs, 16 * (NB // GT))

        @block.gpsimd
        def _(pool):
            pool.memset(ident[:], 0.0).then_inc(s_cst, 1)
            pool.memset(identb[:], 0.0).then_inc(s_cst, 1)
            pool.memset(blockmask[:], 1.0).then_inc(s_cst, 1)
            pool.memset(pick[:], 0.0).then_inc(s_cst, 1)
            pool.memset(lower[:], 1.0).then_inc(s_cst, 1)
            pool.memset(neghalf[:], -0.5).then_inc(s_cst, 1)
            for p in range(2):
                pool.memset(NM[p][:], 0.0).then_inc(s_cst, 1)
                pool.memset(V2[p][:], 1.0).then_inc(s_cst, 1)
            pool.wait_ge(s_cst, 10)
            for t in (ident, identb):
                pool.affine_select(out=t[:], in_=t[:], compare_op=ALU.not_equal, fill=1.0, base=0,
                                   pattern=[[-1, P]], channel_multiplier=1).then_inc(s_cstb, 1)
            bm = blockmask[:].rearrange("p (g d) -> p g d", g=8)
            pool.affine_select(out=bm, in_=bm, compare_op=ALU.is_ge, fill=0.0, base=0,
                               pattern=[[-DH, 8], [0, DH]], channel_multiplier=1).then_inc(s_cstb, 1)
            pool.wait_ge(s_cstb, 3)
            pool.affine_select(out=bm, in_=bm, compare_op=ALU.is_ge, fill=0.0, base=DH - 1,
                               pattern=[[DH, 8], [0, DH]], channel_multiplier=-1).then_inc(s_cstb, 1)
            for q in range(4):
                pool.affine_select(out=pick[:], in_=pick[:], compare_op=ALU.not_equal, fill=1.0, base=-32 * q,
                                   pattern=[[-1, 4], [0, P]], channel_multiplier=1).then_inc(s_cstb, 1)
                pool.wait_ge(s_cstb, 5 + q)
            pool.affine_select(out=lower[:], in_=lower[:], compare_op=ALU.is_ge, fill=0.0, base=-1,
                               pattern=[[1, NE], [-1, NE]], channel_multiplier=0).then_inc(s_cstb, 1)

            def norm(n, p, b, src, dst, signal):
                pool.wait_ge(s_ve[n], b + 1)
                pool.tensor_tensor(rstd[n][p][:], veps[n][p][:], neghalf[:, 0:1], ALU.pow).then_inc(s_rs[n], 1)
                pool.wait_ge(s_cstb, 9)
                pool.wait_ge(s_nm[n], b + 1)
                pool.wait_ge(s_rs[n], b + 1)
                pool.tensor_scalar(dst, src, nmu[n][p][:], rstd[n][p][:], ALU.add, ALU.mult).then_inc(signal, 1)

            def emit(stream, step, b, p, half):
                if (stream, step) == ("A", 0):
                    pool.wait_ge(s_bo_fold, 1)
                    pool.wait_ge(s_xld[p], 8 * b + 16 - 8 * p)
                    if past(b, 2):
                        pool.wait_ge(s_r1, b - 1)
                    pool.tensor_tensor(XB[p][:], X[p][:], rowb[:, RO:RO + D], ALU.add).then_inc(s_xb, 1)
                if (stream, step) == ("A", 1):
                    pool.wait_ge(s_qmax, b + 1)
                    if past(b, 2):
                        pool.wait_ge(s_qe, b - 1)
                    pool.tensor_tensor(QS[p][:].rearrange("p (h d) -> p h d", h=NH),
                                       QV[p][:, 0:D].rearrange("p (h d) -> p h d", h=NH),
                                       qmax[p][:].unsqueeze(2).to_broadcast([P, NH, DH]),
                                       ALU.subtract).then_inc(s_qs, 1)
                if (stream, step) == ("A", 4):
                    if past(b, 2):
                        pool.wait_ge(s_onT, b - 1)
                    norm(0, p, b, ON[p][:], OL[p][:], s_ln0)
                if (stream, step) == ("B", 0):
                    if past(b, 2):
                        pool.wait_ge(s_x1T, b - 1)
                    if past(b, 2):
                        pool.wait_ge(s_x1b, b - 1)
                    norm(1, p, b, R1[p][:], X1[p][:], s_x1)
                    pool.wait_ge(s_x1, b + 1)
                    if past(b, 2):
                        pool.wait_ge(s_r2x, b - 1)
                    pool.tensor_tensor(X1B[p][:], X1[p][:], rowb[:, RO2:RO2 + D], ALU.add).then_inc(s_x1b, 1)
                if (stream, step) == ("C", 3):
                    if past(b, 2):
                        pool.wait_ge(s_x2T, b - 1)
                    pool.wait_ge(s_x2st[p], 8 * b + -8 * p)
                    norm(2, p, b, R2[p][:], X2[p][:], s_x2)
            pipeline(pool, PE_ORDER, emit, LAG)

            for g in range(NB // GT):
                pool.wait_ge(s_fve, g + 1)
                pool.tensor_tensor(frs[:, GT * g:GT * g + GT], fve[:, GT * g:GT * g + GT],
                                   neghalf[:, 0:GT], ALU.pow).then_inc(s_frs, 1)

        @block.scalar
        def _(act):
            for q in range(4):
                act.wait_ge(s_w_ld[q], 16)
                if q == 1:
                    act.wait_ge(s_wo_fold, KC)
                act.activation(wh[:, :, 512 * q:512 * q + 512], stage[:, :, 512 * q:512 * q + 512],
                               ACT.Copy, scale=WSCALE).then_inc(s_wsp_h, 1)

            def copy(dst, src, signal):
                act.activation(dst, src, ACT.Copy).then_inc(signal, 1)

            def emit(stream, step, b, p, half):
                if (stream, step) == ("A", 0):
                    act.wait_ge(s_xT, b + 1)
                    if past(b, 2):
                        act.wait_ge(s_k_ps, b - 1)
                    copy(XTh[p][:], chunks(bank[0], KC), s_xTh)
                if (stream, step) == ("A", 1):
                    act.wait_ge(s_knb, b + 1)
                    if past(b, 2):
                        act.wait_ge(s_qk_ps, b - 1)
                    for c in range(KC):
                        act.activation(KE[p][:, c, :], bank[0][:, c * P:(c + 1) * P], ACT.Exp,
                                       bias=knb[p][:, c:c + 1], scale=1.0 / WSCALE,
                                       accum_out=ksum[p][:, c:c + 1]).then_inc(s_ke, 1)
                    act.wait_ge(s_qs, b + 1)
                    act.activation(QE[p][:], QS[p][:], ACT.Exp).then_inc(s_qe, 1)
                if (stream, step) == ("A", 2):
                    act.wait_ge(s_qk_ps, b + 1)
                    if past(b, 2):
                        act.wait_ge(s_o_ps, b - 1)
                    copy(QKT[p][:], chunks(bank[1], 2 * KC), s_qkT)
                if (stream, step) == ("A", 5):
                    act.wait_ge(s_onT, b + 1)
                    if past(b, 2):
                        act.wait_ge(s_ao_ps, b - 1)
                    copy(OTh[p][:], chunks(bank[0], KC), s_onTh)
                if (stream, step) == ("B", 0):
                    act.wait_ge(s_cT, b + 1)
                    if past(b, 2):
                        act.wait_ge(s_v2_ps, b - 1)
                    copy(CTh[p][:], chunks(bank[3], KC), s_cTh)
                if (stream, step) == ("B", 1):
                    act.wait_ge(s_x1T, b + 1)
                    if past(b, 2):
                        act.wait_ge(s_q2_ps, b - 1)
                    copy(X1Th[p][:], chunks(bank[2], KC), s_x1Th)
                if (stream, step) == ("B", 4):
                    act.wait_ge(s_mT_ps, b + 1)
                    if past(b, 2):
                        act.wait_ge(s_sc, 4 * b - 4)
                    copy(MT[p][:], bank[2][:, 0:P // 2].bitcast(bf16), s_mT)
                if (stream, step) == ("C", 0):
                    if past(b, 2):
                        act.wait_ge(s_pv, b - 1)
                    for u in range(4):
                        act.wait_ge(s_sc, 4 * b + u + 1)
                        act.activation(EX[p][:, u, :, :], chunks(bank[(5, 6, 7, 5)[u]], 4), ACT.Exp)\
                           .then_inc(s_ex, 1)
                if (stream, step) == ("C", 2):
                    act.wait_ge(s_o2T, b + 1)
                    if past(b, 2):
                        act.wait_ge(s_ao2, b - 1)
                    copy(O2Th[p][:], chunks(bank[4], KC), s_o2Th)
                if (stream, step) == ("C", 4):
                    act.wait_ge(s_x2T, b + 1)
                    copy(X2Th_v[:, :, half, p, :], chunks(bank[4], KC), s_x2Th)
            pipeline(act, PE_ORDER, emit, LAG)

            for g in range(4):
                act.wait_ge(s_g_ps, g + 1)
                act.activation(GG[:, 512 * g:512 * g + 512], bank[g][0:G, :], ACT.Gelu,
                               bias=bg1_c[:], scale=1.0 / WSCALE).then_inc(s_gg, 1)
            act.wait_ge(s_lsb, 2)
            act.activation(LE[:], L[:], ACT.Exp).then_inc(s_lsb, 1)

            def weights_high(e, q, part):
                act.wait_ge(s_ewld[q], 16 * e + 32 - 16 * q)
                if not (isinstance(e, int) and e < 2):
                    act.wait_ge(s_dn, 16 * (e - 1))
                for i in range(2):
                    lo = 1024 * i + 256 * part
                    act.activation(EWH[q][:, lo:lo + 256], EWF[q][:, lo:lo + 256], ACT.Copy,
                                   scale=WSCALE).then_inc(s_ewh, 1)
            for part in range(4):
                weights_high(0, 0, part)

            def expert(e, q, g, nxt):
                n = 4 * e + g
                for h in range(HC):
                    act.wait_ge(s_up, 4 * n + h + 1)
                    if not isinstance(n, int) or n > 0:
                        act.wait_ge(s_hl, 4 * n - 4 + h + 1)
                    act.activation(HF[:, h, :], bank[h][:, :], ACT.Gelu, scale=1.0 / WSCALE).then_inc(s_hf, 1)
                if nxt:
                    weights_high(e + 1, 1 - q, g)
            for q in range(2):
                for g in range(4):
                    expert(q, q, g, True)
            with act.Fori(1, NE // 2 - 1) as i:
                for q in range(2):
                    for g in range(4):
                        expert(2 * i + q, q, g, True)
            for q in range(2):
                for g in range(4):
                    expert(NE - 2 + q, q, g, q == 0)

        @block.vector
        def _(dve):
            chain = [0]

            def small(op):
                chain[0] += 1
                op.then_inc(s_prep, 1)
                dve.wait_ge(s_prep, chain[0])

            dve.wait_ge(s_cstb, 9)
            small(dve.tensor_reduce(evenodd[:, 0:1], blockmask[:, 0:P:2 * DH], AX.X, ALU.add))
            small(dve.tensor_scalar(evenodd[:, 1:2], evenodd[:, 0:1], -1.0, 1.0, ALU.mult, ALU.add))
            small(dve.tensor_scalar(evenodd_s[:], evenodd[:], 1.0 / WSCALE, None, ALU.mult))
            for p in range(2):
                for c in range(KC):
                    small(dve.tensor_copy(ST[p][:, c, P:P + 8], blockmask[:, 0:P:DH]))
            dve.wait_ge(s_vec_ld, 16)
            small(dve.tensor_scalar(bq2s[:], vec[:, VQ2:VQ2 + KC], DH ** -0.5, None, ALU.mult))
            for par in range(2):
                small(dve.tensor_scalar(bk2m[:, par, :], vec[:, VK2:VK2 + KC], evenodd[:, par:par + 1], None, ALU.mult))
            for c in range(KC):
                dve.tensor_copy(lnb_rep[:, c, :], vec[:, VB + c:VB + c + 1].to_broadcast([P, P]))\
                   .then_inc(s_lnb, 1)

            def weights_low(q):
                dve.wait_ge(s_wsp_h, q + 1)
                cols = slice(512 * q, 512 * q + 512)
                for c in range(KC):
                    dve.scalar_tensor_tensor(wl[:, c, cols], stage[:, c, cols], WSCALE, wh[:, c, cols],
                                             ALU.mult, ALU.subtract).then_inc(s_wsp_l, 1)
            weights_low(0)
            dve.wait_ge(s_bo_ps, 1)
            dve.wait_ge(s_rows_ld, 16)
            dve.tensor_tensor(rowb[:, RO:RO + D], bank[0][:, 0:D], rowb[:, RO:RO + D], ALU.add)\
               .then_inc(s_bo_fold, 1)
            for c in range(KC):
                dve.tensor_scalar(stage[:, c, CO:CO + D], stage[:, c, CO:CO + D], vec[:, VG + c:VG + c + 1],
                                  None, ALU.mult).then_inc(s_wo_fold, 1)
            for q in range(1, 4):
                weights_low(q)
            dve.wait_ge(s_g_ld, 48)
            small(dve.tensor_scalar(wg1h[:], wg1_f[:], WSCALE, None, ALU.mult))
            dve.scalar_tensor_tensor(wg1l[:], wg1_f[:], WSCALE, wg1h[:], ALU.mult, ALU.subtract)\
               .then_inc(s_wsp_l, 1)

            def low(dst, src, high, high_done, signal, row):
                dve.wait_ge(high_done, row + 1)
                dve.tensor_tensor(dst, src, high, ALU.subtract).then_inc(signal, 1)

            def stats(n, p, b, src, ready, parts=1):
                dve.wait_ge(ready, parts * b + parts)
                dve.bn_stats(bst[n][p][:], src).then_inc(s_bs[n], 1)
                dve.wait_ge(s_cstb, 9)
                dve.wait_ge(s_bs[n], b + 1)
                dve.bn_aggr(mv[n][p][:], bst[n][p][:]).then_inc(s_mv[n], 1)
                dve.wait_ge(s_mv[n], b + 1)
                if past(b, 2):
                    dve.wait_ge((s_ln0, s_x1, s_x2)[n], b - 1)
                dve.tensor_scalar(veps[n][p][:], mv[n][p][:, 1:2], EPS, None, ALU.add).then_inc(s_ve[n], 1)
                dve.tensor_scalar(nmu[n][p][:], mv[n][p][:, 0:1], -1.0, None, ALU.mult).then_inc(s_nm[n], 1)

            def emit(stream, step, b, p, half):
                if (stream, step) == ("A", 0):
                    low(XTl[p][:], chunks(bank[0], KC), XTh[p][:], s_xTh, s_xTl, b)
                if (stream, step) == ("A", 1):
                    dve.wait_ge(s_qv_ps, b + 1)
                    if past(b, 2):
                        dve.wait_ge(s_qs, b - 1)
                    if past(b, 2):
                        dve.wait_ge(s_st_ps, b - 1)
                    dve.scalar_tensor_tensor(QV[p][:], bank[1][:, :], 1.0 / WSCALE, rowb[:, RQV:RQV + 2 * D],
                                             ALU.mult, ALU.add).then_inc(s_qv_sb, 1)
                    dve.wait_ge(s_k_ps, b + 1)
                    dve.tensor_reduce(kmax[p][:], chunks(bank[0], KC), AX.X, ALU.max).then_inc(s_km, 1)
                    dve.wait_ge(s_km, 2 * b + 1)
                    dve.scalar_tensor_tensor(kmax[p][:], kmax[p][:], 1.0 / WSCALE, vec[:, VK:VK + KC],
                                             ALU.mult, ALU.add).then_inc(s_km, 1)
                    dve.wait_ge(s_km, 2 * b + 2)
                    if past(b, 2):
                        dve.wait_ge(s_ke, 2 * b - 2)
                    dve.tensor_tensor(knb[p][:], vec[:, VK:VK + KC], kmax[p][:], ALU.subtract).then_inc(s_knb, 1)
                    dve.wait_ge(s_qv_sb, b + 1)
                    dve.tensor_reduce(qmax[p][:], QV[p][:, 0:D].rearrange("p (h d) -> p h d", h=NH), AX.X,
                                      ALU.max).then_inc(s_qmax, 1)
                if (stream, step) == ("A", 3):
                    dve.wait_ge(s_ke, 2 * b + 2)
                    dve.reciprocal(krec[p][:], ksum[p][:]).then_inc(s_krec, 1)
                    dve.wait_ge(s_st_ps, b + 1)
                    dve.wait_ge(s_krec, b + 1)
                    if past(b, 2):
                        dve.wait_ge(s_o_ps, b - 1)
                    for c in range(KC):
                        dve.scalar_tensor_tensor(ST[p][:, c, 0:P], bank[0][:, c * P:(c + 1) * P],
                                                 krec[p][:, c:c + 1], blockmask[:], ALU.mult, ALU.mult)\
                           .then_inc(s_st, 1)
                if (stream, step) == ("A", 4):
                    dve.wait_ge(s_o_ps, b + 1)
                    o = chunks(bank[1], KC, P + 8)
                    dve.reciprocal(qrec[p][:].rearrange("p (c h) -> p c h", c=KC), o[:, :, P:P + 8])\
                       .then_inc(s_qrec, 1)
                    dve.wait_ge(s_qrec, b + 1)
                    if past(b, 2):
                        dve.wait_ge(s_ln0, b - 1)
                    for c in range(KC):
                        dve.tensor_tensor(ON[p][:, c * P:(c + 1) * P].rearrange("p (h d) -> p h d", d=DH),
                                          o[:, c, 0:P].rearrange("p (h d) -> p h d", d=DH),
                                          qrec[p][:, 8 * c:8 * c + 8].unsqueeze(2).to_broadcast([P, 8, DH]),
                                          ALU.mult).then_inc(s_on, 1)
                    stats(0, p, b, ON[p][:], s_on, 2)
                if (stream, step) == ("A", 5):
                    low(OTl[p][:], chunks(bank[0], KC), OTh[p][:], s_onTh, s_onTl, b)
                if (stream, step) == ("B", 0):
                    low(CTl[p][:], chunks(bank[3], KC), CTh[p][:], s_cTh, s_cTl, b)
                    dve.wait_ge(s_ao_ps, b + 1)
                    dve.wait_ge(s_xb, b + 1)
                    if past(b, 2):
                        dve.wait_ge(s_x1, b - 1)
                    dve.scalar_tensor_tensor(R1[p][:], bank[2][:, 0:D], 1.0 / WSCALE, XB[p][:], ALU.mult, ALU.add)\
                       .then_inc(s_r1, 1)
                    stats(1, p, b, R1[p][:], s_r1)
                if (stream, step) == ("B", 1):
                    dve.wait_ge(s_k2_ps, b + 1)
                    if past(b, 2):
                        dve.wait_ge(s_sc, 4 * b - 4)
                    for par in range(2):
                        dve.scalar_tensor_tensor(K2[p][:, :, par, :], chunks(bank[3], KC), evenodd_s[:, par:par + 1],
                                                 bk2m[:, par, :].unsqueeze(2).to_broadcast([P, KC, P]),
                                                 ALU.mult, ALU.add).then_inc(s_k2, 1)
                    low(X1Tl[p][:], chunks(bank[2], KC), X1Th[p][:], s_x1Th, s_x1Tl, b)
                if (stream, step) == ("B", 2):
                    dve.wait_ge(s_q2_ps, b + 1)
                    dve.scalar_tensor_tensor(Q2[p][:], chunks(bank[2], KC), DH ** -0.5 / WSCALE,
                                             bq2s[:].unsqueeze(2).to_broadcast([P, KC, P]),
                                             ALU.mult, ALU.add).then_inc(s_q2, 1)
                    dve.wait_ge(s_v2_ps, b + 1)
                    if past(b, 2):
                        dve.wait_ge(s_pv, b - 1)
                    dve.scalar_tensor_tensor(V2[p][:, :, 0:DH], bank[3][:, 0:D].rearrange("p (h d) -> p h d", h=NH),
                                             1.0 / WSCALE, rowb[:, RV2:RV2 + D].rearrange("p (h d) -> p h d", h=NH),
                                             ALU.mult, ALU.add).then_inc(s_v2, 1)
                if (stream, step) == ("B", 3):
                    if past(b, 2):
                        dve.wait_ge(s_mT_ps, b - 1)
                    for u in range(4):
                        dve.wait_ge(s_nat, 4 * b + u + 1)
                        dve.tensor_reduce(NM[p][:, u, 0:4], chunks(bank[(6, 7, 5, 6)[u]], 4), AX.X, ALU.max,
                                          negate=True).then_inc(s_mx, 1)
                if (stream, step) == ("C", 1):
                    dve.wait_ge(s_pv, b + 1)
                    pv = chunks(bank[4], NH, DH + 1)
                    dve.reciprocal(r2[p][:], pv[:, :, DH]).then_inc(s_r2, 1)
                    dve.wait_ge(s_r2, b + 1)
                    if past(b, 2):
                        dve.wait_ge(s_o2T, b - 1)
                    dve.tensor_tensor(O2[p][:].rearrange("p (h d) -> p h d", h=NH), pv[:, :, 0:DH],
                                      r2[p][:].unsqueeze(2).to_broadcast([P, NH, DH]), ALU.mult).then_inc(s_o2, 1)
                if (stream, step) == ("C", 2):
                    low(O2Tl[p][:], chunks(bank[4], KC), O2Th[p][:], s_o2Th, s_o2Tl, b)
                if (stream, step) == ("C", 3):
                    dve.wait_ge(s_ao2, b + 1)
                    dve.wait_ge(s_x1b, b + 1)
                    if past(b, 2):
                        dve.wait_ge(s_x2, b - 1)
                    dve.scalar_tensor_tensor(R2[p][:], bank[4][:, 0:D], 1.0 / WSCALE, X1B[p][:], ALU.mult, ALU.add)\
                       .then_inc(s_r2x, 1)
                    stats(2, p, b, R2[p][:], s_r2x)
                if (stream, step) == ("C", 4):
                    low(X2Tl_v[:, :, half, p, :], chunks(bank[4], KC), X2Th_v[:, :, half, p, :], s_x2Th, s_x2Tl, b)
            pipeline(dve, PE_ORDER, emit, LAG)

            dve.wait_ge(s_l_ps, 1)
            logits = bank[4][:, 0:NB * NE].rearrange("p (b e) -> p b e", b=NB)
            dve.tensor_reduce(lmax[:], logits, AX.X, ALU.max).then_inc(s_lsb, 1)
            dve.wait_ge(s_lsb, 1)
            dve.tensor_tensor(L[:], logits, lmax[:].unsqueeze(2).to_broadcast([P, NB, NE]), ALU.subtract)\
               .then_inc(s_lsb, 1)
            dve.wait_ge(s_lsb, 3)
            small(dve.tensor_reduce(lsum[:], LE[:], AX.X, ALU.add))
            small(dve.reciprocal(lrec[:], lsum[:]))
            small(dve.tensor_tensor(PR[:], LE[:], lrec[:].unsqueeze(2).to_broadcast([P, NB, NE]), ALU.mult))
            mine = PR[:].unsqueeze(3).to_broadcast([P, NB, NE, NE])
            for b in range(NB):
                small(dve.tensor_copy(CMQ[:, b, :, :], PR[:, b, :].unsqueeze(1).to_broadcast([P, NE, NE])))
            small(dve.tensor_tensor(CMP, CMQ, mine, ALU.is_equal))
            for b in range(NB):
                small(dve.tensor_tensor(CMP[:, b, :, :], CMP[:, b, :, :], lower[:], ALU.mult))
            small(dve.tensor_tensor(CMQ, CMQ, mine, ALU.is_gt))
            small(dve.tensor_tensor(CMP, CMP, CMQ, ALU.add))
            small(dve.tensor_reduce(rank[:], CMP, AX.X, ALU.add))
            small(dve.tensor_scalar(rank[:], rank[:], 1.5, 1.0 / WSCALE, ALU.is_lt, ALU.mult))
            small(dve.tensor_tensor(gates[:], PR[:], rank[:], ALU.mult))
            for p in range(2):
                dve.wait_ge(s_x2st[p], 8 * NB)

            def weights_low_e(e, q, part):
                if not (isinstance(e, int) and e < 2):
                    dve.wait_ge(s_dn, 16 * (e - 1))
                for i in range(2):
                    dve.wait_ge(s_ewh, 8 * e + 2 * part + i + 1)
                    lo = 1024 * i + 256 * part
                    dve.scalar_tensor_tensor(EWL[q][:, lo:lo + 256], EWF[q][:, lo:lo + 256], WSCALE,
                                             EWH[q][:, lo:lo + 256], ALU.mult, ALU.subtract).then_inc(s_ewl, 1)
            for part in range(4):
                weights_low_e(0, 0, part)

            def split_hidden(e, q, g, n, first):
                for h in range(HC):
                    dve.wait_ge(s_hf, 4 * n + h + 1)
                    if not first:
                        dve.wait_ge(s_dn, 4 * (n - 1))
                    dve.tensor_copy(HH[n_par(g)][:, h, :], HF[:, h, :]).then_inc(s_hh, 1)
                    dve.wait_ge(s_hh, 4 * n + h + 1)
                    dve.tensor_tensor(HL[n_par(g)][:, h, :], HF[:, h, :], HH[n_par(g)][:, h, :], ALU.subtract)\
                       .then_inc(s_hl, 1)

            def n_par(g):
                return g % 2

            def accumulate(i, q, g, n):
                for t in range(GT):
                    b = GT * g + t
                    dve.wait_ge(s_dn, 4 * n + t + 1)
                    if not isinstance(n, int) or n >= 4:
                        dve.wait_ge(s_acc, 4 * (n - 4) + t + 1)
                    dve.scalar_tensor_tensor(X2all[:, b, :], bank[4 + t][:, 0:D], gates_v[:, b, i, q:q + 1],
                                             X2all[:, b, :], ALU.mult, ALU.add).then_inc(s_acc, 1)

            def step(i, q, g, nxt):
                e = 2 * i + q
                n = 4 * e + g
                first = isinstance(n, int) and n < 2
                split_hidden(e, q, g, n, first)
                if not isinstance(n, int) or n > 0:
                    if g:
                        accumulate(i, q, g - 1, n - 1)
                    else:
                        accumulate(i + (q - 1) // 2, 1 - q, 3, n - 1)
                if nxt:
                    weights_low_e(e + 1, 1 - q, g)
            for q in range(2):
                for g in range(4):
                    step(0, q, g, True)
            with dve.Fori(1, NE // 2 - 1) as i:
                for q in range(2):
                    for g in range(4):
                        step(i, q, g, True)
            for q in range(2):
                for g in range(4):
                    step(NE // 2 - 1, q, g, q == 0)
            accumulate(NE // 2 - 1, 1, 3, 4 * NE - 1)

            for g in range(NB // GT):
                rows4 = range(GT * g, GT * g + GT)
                for b in rows4:
                    if b % GT == 0:
                        dve.wait_ge(s_acc, 4 * (4 * (NE - 1) + g + 1))
                    dve.bn_stats(fst[:, b, :], X2all[:, b, :]).then_inc(s_fbs, 1)
                for b in rows4:
                    dve.wait_ge(s_fbs, b + 1)
                    dve.bn_aggr(fmv[:, b, :], fst[:, b, :]).then_inc(s_fmv, 1)
                dve.wait_ge(s_fmv, GT * (g + 1))
                dve.tensor_scalar(fve[:, GT * g:GT * g + GT], fmv[:, GT * g:GT * g + GT, 1], EPS, None, ALU.add)\
                   .then_inc(s_fve, 1)
            for b in range(NB):
                if b % GT == 0:
                    dve.wait_ge(s_frs, b // GT + 1)
                dve.tensor_scalar(X2all[:, b, :], X2all[:, b, :], fmv[:, b, 0:1], frs[:, b:b + 1],
                                  ALU.subtract, ALU.mult).then_inc(s_fy, 1)

        @block.tensor
        def _(pe):
            pe.wait_ge(s_cstb, 9)
            pe.wait_ge(s_w_ld[1], 16)
            pe.wait_ge(s_lnb, KC)
            for c in range(KC):
                last = pe.matmul(bank[0][:, 0:D], lnb_rep[:, c, :], stage[:, c, CO:CO + D],
                                 start=(c == 0), stop=(c == KC - 1))
            last.then_inc(s_bo_ps, 1)
            pe.wait_ge(s_wsp_l, 4 * KC + 1)

            def w(t, col, width):
                return lambda c: t[:, c, col:col + width]

            def feature_major(dst, col, th, tl, signal):
                for f in range(KC):
                    last = split3(pe, dst[:, f * P:(f + 1) * P],
                                  w(wh, col + f * P, P), w(wl, col + f * P, P),
                                  lambda c: th[:, c, :], lambda c: tl[:, c, :])
                last.then_inc(signal, 1)

            def token_major(dst, col, width, th, tl, signal):
                split3(pe, dst, lambda c: th[:, c, :], lambda c: tl[:, c, :],
                       w(wh, col, width), w(wl, col, width)).then_inc(signal, 1)

            def turn(dst, src, n, signal):
                for c in range(n):
                    last = pe.transpose(dst[:, c * P:(c + 1) * P], src(c), ident[:])
                last.then_inc(signal, 1)

            def emit(stream, step, b, p, half):
                if (stream, step) == ("A", 0):
                    pe.wait_ge(s_xld[p], 8 * b + 16 - 8 * p)
                    if past(b, 1):
                        pe.wait_ge(s_onTl, b)
                    turn(bank[0], lambda c: X[p][:, c * P:(c + 1) * P], KC, s_xT)
                if (stream, step) == ("A", 1):
                    pe.wait_ge(s_xTl, b + 1)
                    if past(b, 1):
                        pe.wait_ge(s_on, 2 * b)
                    token_major(bank[1][:, :], CQV, 2 * D, XTh[p], XTl[p], s_qv_ps)
                    feature_major(bank[0], CK, XTh[p], XTl[p], s_k_ps)
                if (stream, step) == ("A", 2):
                    pe.wait_ge(s_qe, b + 1)
                    pe.wait_ge(s_ke, 2 * b + 2)
                    pe.wait_ge(s_qv_sb, b + 1)
                    for c in range(KC):
                        pe.transpose(bank[1][:, c * P:(c + 1) * P], QE[p][:, c * P:(c + 1) * P], ident[:])
                    turn(bank[1][:, D:2 * D], lambda c: KE[p][:, c, :], KC, s_qk_ps)
                if (stream, step) == ("A", 3):
                    pe.wait_ge(s_qkT, b + 1)
                    for c in range(KC):
                        last = pe.matmul(bank[0][:, c * P:(c + 1) * P], QKT[p][:, KC + c, :],
                                         QV[p][:, D + c * P:D + (c + 1) * P], start=True, stop=True)
                    last.then_inc(s_st_ps, 1)
                if (stream, step) == ("A", 4):
                    pe.wait_ge(s_st, 2 * b + 2)
                    o = chunks(bank[1], KC, P + 8)
                    for c in range(KC):
                        last = pe.matmul(o[:, c, :], QKT[p][:, c, :], ST[p][:, c, :], start=True, stop=True)
                    last.then_inc(s_o_ps, 1)
                if (stream, step) == ("A", 5):
                    pe.wait_ge(s_ln0, b + 1)
                    turn(bank[0], lambda c: OL[p][:, c * P:(c + 1) * P], KC, s_onT)
                if (stream, step) == ("B", 0):
                    pe.wait_ge(s_onTl, b + 1)
                    if past(b, 1):
                        pe.wait_ge(s_mT, b)
                    token_major(bank[2][:, 0:D], CO, D, OTh[p], OTl[p], s_ao_ps)
                    pe.wait_ge(s_cld[p], 8 * b + 16 - 8 * p)
                    if past(b, 1):
                        pe.wait_ge(s_v2, b)
                    turn(bank[3], lambda c: C[p][:, c * P:(c + 1) * P], KC, s_cT)
                if (stream, step) == ("B", 1):
                    pe.wait_ge(s_cTl, b + 1)
                    feature_major(bank[3], CK2, CTh[p], CTl[p], s_k2_ps)
                    pe.wait_ge(s_x1, b + 1)
                    turn(bank[2], lambda c: X1[p][:, c * P:(c + 1) * P], KC, s_x1T)
                if (stream, step) == ("B", 2):
                    pe.wait_ge(s_k2, 2 * b + 2)
                    token_major(bank[3][:, 0:D], CV2, D, CTh[p], CTl[p], s_v2_ps)
                    pe.wait_ge(s_x1Tl, b + 1)
                    feature_major(bank[2], CQ2, X1Th[p], X1Tl[p], s_q2_ps)
                if (stream, step) == ("B", 3):
                    pe.wait_ge(s_q2, b + 1)
                    for u in range(4):
                        rows32 = slice(32 * u, 32 * u + 32)
                        if u < 3:
                            if not (isinstance(b, int) and b == 0):
                                pe.wait_ge(s_ex, 4 * b + u + 2 - 4)
                        else:
                            pe.wait_ge(s_mx, 4 * b + 1)
                        for c in range(KC):
                            last = pe.matmul(bank[(6, 7, 5, 6)[u]][:, c * 2 * P:(c + 1) * 2 * P],
                                             Q2[p][rows32, c, :].bitcast(bf16)[:, 1::2],
                                             K2[p][rows32, c, :, :].rearrange("p a t -> p (a t)").bitcast(bf16)[:, 1::2],
                                             start=True, stop=True)
                        last.then_inc(s_nat, 1)
                if (stream, step) == ("B", 4):
                    pe.wait_ge(s_mx, 4 * b + 4)
                    pe.transpose(bank[2][:, 0:P // 2].bitcast(bf16), NM[p][:].rearrange("p s j -> p (s j)"),
                                 identb[:]).then_inc(s_mT_ps, 1)
                if (stream, step) == ("C", 0):
                    pe.wait_ge(s_mT, b + 1)
                    for u in range(4):
                        rows32 = slice(32 * u, 32 * u + 32)
                        if u < 3:
                            pe.wait_ge(s_mx, 4 * b + min(3 + u, 4))
                        else:
                            pe.wait_ge(s_ex, 4 * b + 1)
                        dst = bank[(5, 6, 7, 5)[u]]
                        for j in range(4):
                            c, par = j // 2, j % 2
                            o = dst[:, j * P:(j + 1) * P]
                            pe.matmul(o, pick[rows32, j, :], MT[p][rows32, :], start=True, stop=False)
                            last = pe.matmul(o, K2[p][rows32, c, par, :], Q2[p][rows32, c, :], start=False, stop=True)
                        last.then_inc(s_sc, 1)
                if (stream, step) == ("C", 1):
                    if past(b, 1):
                        pe.wait_ge(s_x2Tl, b)
                    for u in range(4):
                        pe.wait_ge(s_ex, 4 * b + u + 1)
                        for j in range(4):
                            h = 8 * (j // 2) + 2 * u + j % 2
                            last = pe.matmul(bank[4][:, h * (DH + 1):(h + 1) * (DH + 1)], EX[p][:, u, j, :],
                                             V2[p][:, h, :], start=True, stop=True)
                    last.then_inc(s_pv, 1)
                if (stream, step) == ("C", 2):
                    pe.wait_ge(s_o2, b + 1)
                    turn(bank[4], lambda c: O2[p][:, c * P:(c + 1) * P], KC, s_o2T)
                if (stream, step) == ("C", 3):
                    pe.wait_ge(s_o2Tl, b + 1)
                    token_major(bank[4][:, 0:D], CO2, D, O2Th[p], O2Tl[p], s_ao2)
                if (stream, step) == ("C", 4):
                    pe.wait_ge(s_x2, b + 1)
                    turn(bank[4], lambda c: X2[p][:, c * P:(c + 1) * P], KC, s_x2T)
            pipeline(pe, PE_ORDER, emit, LAG)

            pe.wait_ge(s_x2Tl, NB)
            pe.wait_ge(s_ex, 4 * NB)
            for g in range(4):
                cols = slice(512 * g, 512 * g + 512)
                split3(pe, bank[g][0:G, :], lambda c: wg1h[:, c, :], lambda c: wg1l[:, c, :],
                       lambda c: X2Th[:, c, cols], lambda c: X2Tl[:, c, cols]).then_inc(s_g_ps, 1)
            for b in range(NB):
                if b % 4 == 0:
                    pe.wait_ge(s_gg, b // 4 + 1)
                last = pe.matmul(bank[4][:, b * NE:(b + 1) * NE], GG[:, b * P:(b + 1) * P], wg2_f[:],
                                 start=True, stop=True)
            last.then_inc(s_l_ps, 1)

            def up(e, q, g, n):
                pe.wait_ge(s_ewl, 8 * (e + 1))
                cols = slice(GW * g, GW * g + GW)
                wi_h = EWH[q][:, 0:1024].rearrange("p (k h) -> p k h", k=KC)
                wi_l = EWL[q][:, 0:1024].rearrange("p (k h) -> p k h", k=KC)
                for h in range(HC):
                    if not isinstance(n, int) or n > 0:
                        pe.wait_ge(s_hf, 4 * (n - 1) + h + 1)
                    split3(pe, bank[h][:, :],
                           lambda c: wi_h[:, c, h * P:(h + 1) * P], lambda c: wi_l[:, c, h * P:(h + 1) * P],
                           lambda c: X2Th[:, c, cols], lambda c: X2Tl[:, c, cols]).then_inc(s_up, 1)

            def down(e, q, g, n):
                wo_h = EWH[q][:, 1024:2048].rearrange("p (k d) -> p k d", k=HC)
                wo_l = EWL[q][:, 1024:2048].rearrange("p (k d) -> p k d", k=HC)
                pe.wait_ge(s_hl, 4 * (n + 1))
                for t in range(GT):
                    if isinstance(n, int) and n == 0:
                        pe.wait_ge(s_lsb, 2)
                    else:
                        pe.wait_ge(s_acc, 4 * (n - 1) + t + 1)
                    split3(pe, bank[4 + t][:, 0:D],
                           lambda c: HH[g % 2][:, c, t * P:(t + 1) * P], lambda c: HL[g % 2][:, c, t * P:(t + 1) * P],
                           lambda c: wo_h[:, c, :], lambda c: wo_l[:, c, :], HC).then_inc(s_dn, 1)

            def step(e, q, g):
                n = 4 * e + g
                up(e, q, g, n)
                if not isinstance(n, int) or n > 0:
                    if g:
                        down(e, q, g - 1, n - 1)
                    else:
                        down(e - 1, 1 - q, 3, n - 1)
            for q in range(2):
                for g in range(4):
                    step(q, q, g)
            with pe.Fori(1, NE // 2) as i:
                for q in range(2):
                    for g in range(4):
                        step(2 * i + q, q, g)
            down(NE - 1, 1, 3, 4 * NE - 1)


def kernel(**inputs):
    import concourse.bacc as bacc
    from concourse.bass_utils import run_bass_kernel_spmd

    a = {k: np.asarray(v) for k, v in inputs.items()}

    def chunked(m):
        return m.reshape(-1, P, m.shape[-1]).transpose(1, 0, 2)

    order = ["attn_Wq", "attn_Wv", "attn_Wk", "attn_Wo", "xattn_Wq", "xattn_Wk", "xattn_Wv", "xattn_Wo"]
    wpack = chunked(np.concatenate([a["L0_" + n].T for n in order], axis=1))
    rows = np.concatenate([a["L0_" + n] for n in ("attn_bq", "attn_bv", "attn_bo", "xattn_bv", "xattn_bo")])
    vecs = np.concatenate([a["L0_" + n].reshape(KC, P).T
                           for n in ("attn_bk", "xattn_bk", "xattn_bq", "attn_ln_g", "attn_ln_b")], axis=1)
    arrays = {
        "x": a["x"],
        "ctx": a["ctx_1024"],
        "wpack": wpack,
        "rows": rows,
        "vecs": vecs,
        "wg1": chunked(a["L0_ffn_wg1"]),
        "bg1": a["L0_ffn_bg1"].reshape(G, 1),
        "wg2": a["L0_ffn_wg2"],
        "w_in": a["L0_ffn_w_in"].reshape(NE, KC, P, HID).transpose(0, 2, 1, 3),
        "w_out": a["L0_ffn_w_out"].reshape(NE, HC, P, D).transpose(0, 2, 1, 3),
    }
    arrays = {k: np.ascontiguousarray(v) for k, v in arrays.items()}
    nc = bacc.Bacc("TRN2", target_bir_lowering=False, num_devices=1)
    args = [nc.dram_tensor(k, v.shape, mybir.dt.from_np(v.dtype), kind="ExternalInput").ap()
            for k, v in arrays.items()]
    out = nc.dram_tensor("out", (NB, S, D), f32, kind="ExternalOutput").ap()
    decoder_layer(nc, *args, out)
    r = run_bass_kernel_spmd(nc, [arrays], core_ids=[0])
    return r.results[0]["out"]
```

```python
from contextlib import ExitStack

import numpy as np
import concourse.bass as bass
from concourse import mybir

f32 = mybir.dt.float32
f16 = mybir.dt.float16
bf16 = mybir.dt.bfloat16
ACT = mybir.ActivationFunctionType
ALU = mybir.AluOpType
AX = mybir.AxisListType

NB, S, D = 16, 128, 256
NH, DH = 16, 16
NE, HID, G = 8, 512, 64
P = 128
KC = D // P
HC = HID // P
WSCALE = 256.0
PSCALE = 64.0
EPS = 1e-5
GT = 4
GW = GT * P
CQV, CK, CO, CQ2, CK2, CV2, CO2 = 0, 512, 768, 1024, 1280, 1536, 1792
NPW = 2048
RQV, RO, RV2, RO2, NROW = 0, 512, 768, 1024, 1280
VK, VK2, VQ2, VG, VB, NVEC = 0, 2, 4, 6, 8, 10


def decoder_layer(nc, x, ctx, wpack, rows, vecs, wg1, bg1, wg2, w_in, w_out, out):
    es = ExitStack()
    with es:
        def sb(name, shape, dt=f32):
            return es.enter_context(nc.sbuf_tensor(name, shape, dt))

        def pair(name, shape, dt=f32):
            return [sb(f"{name}{i}", shape, dt) for i in range(2)]

        def sem(name):
            return es.enter_context(nc.semaphore(name))

        ident = sb("ident", [P, P])
        identb = sb("identb", [P, P], bf16)
        blockmask = sb("blockmask", [P, P])
        mask4 = sb("mask4", [P, 4])
        pick = sb("pick", [P, 8, P], bf16)
        neghalf = sb("neghalf", [P, NB])
        rowb = sb("rowb", [P, NROW])
        vec = sb("vec", [P, NVEC])
        bq2s = sb("bq2s", [P, KC])
        bk2s = sb("bk2s", [P, KC])
        lnb_rep = sb("lnb_rep", [P, KC, P])
        stage = sb("stage", [P, KC, NPW])
        wh = sb("wh", [P, KC, NPW], f16)
        wl = sb("wl", [P, KC, NPW], f16)
        X = pair("X", [P, D])
        C = pair("C", [P, D])
        XTh = pair("XTh", [P, KC, P], f16)
        XTl = pair("XTl", [P, KC, P], f16)
        QV = pair("QV", [P, 2 * D])
        qmax = pair("qmax", [P, NH])
        QS = pair("QS", [P, D])
        QE = pair("QE", [P, D])
        kmax = pair("kmax", [P, KC])
        knb = pair("knb", [P, KC])
        KE = pair("KE", [P, KC, P])
        ksum = pair("ksum", [P, KC])
        krec = pair("krec", [P, KC])
        QKT = pair("QKT", [P, 2 * KC, P])
        ST = pair("ST", [P, KC, P + 8])
        qrec = pair("qrec", [P, NH])
        ON = pair("ON", [P, D])
        OL = pair("OL", [P, D])
        OTh = pair("OTh", [P, KC, P], f16)
        OTl = pair("OTl", [P, KC, P], f16)
        XB = pair("XB", [P, D])
        bst = [pair(f"bst{n}_", [P, 6]) for n in range(3)]
        mv = [pair(f"mv{n}_", [P, 2]) for n in range(3)]
        nmu = [pair(f"nmu{n}_", [P, 1]) for n in range(3)]
        veps = [pair(f"veps{n}_", [P, 1]) for n in range(3)]
        rstd = [pair(f"rstd{n}_", [P, 1]) for n in range(3)]
        CTh = pair("CTh", [P, KC, P], f16)
        CTl = pair("CTl", [P, KC, P], f16)
        R1 = pair("R1", [P, D])
        X1 = pair("X1", [P, D])
        X1Th = pair("X1Th", [P, KC, P], f16)
        X1Tl = pair("X1Tl", [P, KC, P], f16)
        K2h = pair("K2h", [P, KC, P], f16)
        K2l = pair("K2l", [P, KC, P], f16)
        Q2h = pair("Q2h", [P, KC, P], f16)
        Q2l = pair("Q2l", [P, KC, P], f16)
        QMh = pair("QMh", [P, KC, 4, P], f16)
        QMl = pair("QMl", [P, KC, 4, P], f16)
        V2 = pair("V2", [P, NH, DH + 1])
        V2h = pair("V2h", [P, NH, DH + 1], f16)
        V2l = pair("V2l", [P, NH, DH + 1], f16)
        NM = pair("NM", [P, 2, 64], bf16)
        MT = pair("MT", [P, P], bf16)
        EX = pair("EX", [P, 4, P])
        EXh = pair("EXh", [P, 4, 4, P], f16)
        EXl = pair("EXl", [P, 4, 4, P], f16)
        r2 = pair("r2", [P, NH])
        O2 = pair("O2", [P, D])
        O2Th = pair("O2Th", [P, KC, P], f16)
        O2Tl = pair("O2Tl", [P, KC, P], f16)
        R2 = pair("R2", [P, D])
        X2 = pair("X2", [P, D])
        X2all = sb("X2all", [P, NB, D])
        X2Th = sb("X2Th", [P, KC, NB * P], f16)
        X2Tl = sb("X2Tl", [P, KC, NB * P], f16)
        x_v = x.rearrange("(i p) s d -> i p s d", p=2)
        ctx_v = ctx.rearrange("(i p) s d -> i p s d", p=2)
        X2all_v = X2all[:].rearrange("q (i p) d -> q i p d", p=2)
        X2Th_v = X2Th[:].rearrange("q c (i p t) -> q c i p t", p=2, t=P)
        X2Tl_v = X2Tl[:].rearrange("q c (i p t) -> q c i p t", p=2, t=P)
        w_in_v = w_in.rearrange("(i q) p k h -> i q p k h", q=2)
        w_out_v = w_out.rearrange("(i q) p k h -> i q p k h", q=2)
        wg1_f = sb("wg1_f", [P, KC, G])
        wg1h = sb("wg1h", [P, KC, G], f16)
        wg1l = sb("wg1l", [P, KC, G], f16)
        bg1_c = sb("bg1_c", [G, 1])
        wg2_f = sb("wg2_f", [G, NE])
        GG = sb("GG", [G, NB * P])
        L = sb("L", [P, NB, NE])
        lmax = sb("lmax", [P, NB])
        LE = sb("LE", [P, NB, NE])
        lsum = sb("lsum", [P, NB])
        lrec = sb("lrec", [P, NB])
        PR = sb("PR", [P, NB, NE])
        lower = sb("lower", [P, NE, NE])
        gates = sb("gates", [P, NB, NE])
        gates_v = gates[:].rearrange("p b (i q) -> p b i q", q=2)
        rank = sb("rank", [P, NB, NE])
        scratch = stage[:, :, :].rearrange("p k n -> p (k n)")
        CMP = scratch[:, 0:NB * NE * NE].rearrange("p (b e f) -> p b e f", b=NB, e=NE)
        CMQ = scratch[:, NB * NE * NE:2 * NB * NE * NE].rearrange("p (b e f) -> p b e f", b=NB, e=NE)
        EWF = pair("EWF", [P, 2048])
        EWH = pair("EWH", [P, 2048], f16)
        EWL = pair("EWL", [P, 2048], f16)
        HF = scratch[:, 2048:4096].rearrange("p (h t) -> p h t", h=HC)
        HH = [t[:].rearrange("p u j t -> p u (j t)") for t in EXh]
        HL = [t[:].rearrange("p u j t -> p u (j t)") for t in EXl]
        fst = sb("fst", [P, NB, 6])
        fmv = sb("fmv", [P, NB, 2])
        fnm = sb("fnm", [P, NB])
        fve = sb("fve", [P, NB])
        frs = sb("frs", [P, NB])

        bank = [es.enter_context(nc.psum_tensor(f"bank{i}", [P, 512], f32)) for i in range(8)]

        def chunks(t, n, w=P):
            return t[:, 0:n * w].rearrange("p (c w) -> p c w", c=n)

        s_w_ld = [sem(f"s_w_ld{q}") for q in range(4)]
        s_rows_ld, s_vec_ld, s_g_ld = sem("s_rows_ld"), sem("s_vec_ld"), sem("s_g_ld")
        s_cst, s_cstb = sem("s_cst"), sem("s_cstb")
        s_prep = sem("s_prep")
        s_lnb, s_bo_ps = sem("s_lnb"), sem("s_bo_ps")
        s_bo_fold, s_wo_fold = sem("s_bo_fold"), sem("s_wo_fold")
        s_wsp_h, s_wsp_l = sem("s_wsp_h"), sem("s_wsp_l")
        s_xld = [sem(f"s_xld{p}") for p in range(2)]
        s_cld = [sem(f"s_cld{p}") for p in range(2)]
        s_xT, s_xTh, s_xTl, s_xb = sem("s_xT"), sem("s_xTh"), sem("s_xTl"), sem("s_xb")
        s_qv_ps, s_k_ps, s_qv_sb, s_qmax = sem("s_qv_ps"), sem("s_k_ps"), sem("s_qv_sb"), sem("s_qmax")
        s_km, s_knb, s_ke, s_qs = sem("s_km"), sem("s_knb"), sem("s_ke"), sem("s_qs")
        s_qe, s_krec, s_qk_ps, s_qkT = sem("s_qe"), sem("s_krec"), sem("s_qk_ps"), sem("s_qkT")
        s_st_ps, s_st, s_o_ps, s_qrec = sem("s_st_ps"), sem("s_st"), sem("s_o_ps"), sem("s_qrec")
        s_on, s_ln0, s_onT, s_onTh = sem("s_on"), sem("s_ln0"), sem("s_onT"), sem("s_onTh")
        s_onTl = sem("s_onTl")
        s_bs = [sem(f"s_bs{n}") for n in range(3)]
        s_mv = [sem(f"s_mv{n}") for n in range(3)]
        s_nm = [sem(f"s_nm{n}") for n in range(3)]
        s_ve = [sem(f"s_ve{n}") for n in range(3)]
        s_rs = [sem(f"s_rs{n}") for n in range(3)]
        s_ao_ps, s_r1, s_x1, s_x1b = sem("s_ao_ps"), sem("s_r1"), sem("s_x1"), sem("s_x1b")
        s_cT, s_cTh, s_cTl, s_x1T = sem("s_cT"), sem("s_cTh"), sem("s_cTl"), sem("s_x1T")
        s_x1Th, s_x1Tl, s_k2_ps, s_k2h = sem("s_x1Th"), sem("s_x1Tl"), sem("s_k2_ps"), sem("s_k2h")
        s_q2_ps, s_q2h, s_v2_ps, s_v2 = sem("s_q2_ps"), sem("s_q2h"), sem("s_v2_ps"), sem("s_v2")
        s_k2l, s_q2l, s_qmh, s_qml = sem("s_k2l"), sem("s_q2l"), sem("s_qmh"), sem("s_qml")
        s_nat, s_mx, s_mT_ps, s_mT = sem("s_nat"), sem("s_mx"), sem("s_mT_ps"), sem("s_mT")
        s_sc, s_ex, s_exh, s_exl = sem("s_sc"), sem("s_ex"), sem("s_exh"), sem("s_exl")
        s_v2h, s_v2l, s_pv, s_r2 = sem("s_v2h"), sem("s_v2l"), sem("s_pv"), sem("s_r2")
        s_o2, s_o2T, s_o2Th, s_o2Tl = sem("s_o2"), sem("s_o2T"), sem("s_o2Th"), sem("s_o2Tl")
        s_ao2, s_r2x, s_x2, s_x2T = sem("s_ao2"), sem("s_r2x"), sem("s_x2"), sem("s_x2T")
        s_x2Th, s_x2Tl = sem("s_x2Th"), sem("s_x2Tl")
        s_x2st = [sem(f"s_x2st{p}") for p in range(2)]
        s_g_ps, s_gg, s_l_ps, s_lsb = sem("s_g_ps"), sem("s_gg"), sem("s_l_ps"), sem("s_lsb")
        s_ewld = [sem(f"s_ewld{q}") for q in range(2)]
        s_ewh, s_ewl, s_up, s_hf = sem("s_ewh"), sem("s_ewl"), sem("s_up"), sem("s_hf")
        s_hh, s_hl, s_dn, s_acc = sem("s_hh"), sem("s_hl"), sem("s_dn"), sem("s_acc")
        s_fbs, s_fmv, s_fve, s_frs = sem("s_fbs"), sem("s_fmv"), sem("s_fve"), sem("s_frs")
        s_fy, s_outs = sem("s_fy"), sem("s_outs")

        SC_BANK, NAT_BANK = (6, 0, 1, 5), (4, 5, 3, 7)

        def past(row, back):
            return not isinstance(row, int) or row >= back

        def split3(pe, dst, a_h, a_l, b_h, b_l, n=KC):
            for c in range(n):
                for i, (a, b) in enumerate(((a_h, b_h), (a_h, b_l), (a_l, b_h))):
                    last = pe.matmul(dst, a(c), b(c), start=(c == 0 and i == 0), stop=(c == n - 1 and i == 2))
            return last

        def upto(n):
            return min(n, NB) if isinstance(n, int) else n

        def pipeline(eng, order, emit):
            steps = [(word[:-2], int(word[-1])) for word in order.split()]

            def iteration(half, odd, live):
                for step, lag in steps:
                    if lag in live:
                        at = odd - lag
                        emit(step, 2 * half + at, at % 2, half + at // 2)

            def peeled(i):
                iteration(i // 2, i % 2, [lag for lag in range(4) if 0 <= i - lag < NB])
            for i in range(6):
                peeled(i)
            with eng.Fori(3, NB // 2) as half:
                for odd in range(2):
                    iteration(half, odd, range(4))
            for i in range(NB, NB + 3):
                peeled(i)

        block = es.enter_context(nc.Block())

        @block.sync
        def _(sp):
            sp.dma_start(vec[:], vecs).then_inc(s_vec_ld, 16)
            for q in range(4):
                sp.dma_start(stage[:, :, 512 * q:512 * q + 512], wpack[:, :, 512 * q:512 * q + 512])\
                  .then_inc(s_w_ld[q], 16)
                if q == 0:
                    sp.dma_start(rowb[:], rows.partition_broadcast(P)).then_inc(s_rows_ld, 16)
            sp.dma_start(wg1_f[:], wg1).then_inc(s_g_ld, 16)
            sp.dma_start(bg1_c[:], bg1).then_inc(s_g_ld, 16)
            sp.dma_start(wg2_f[:], wg2).then_inc(s_g_ld, 16)

            def expert_load(e, q, i=0):
                if not (isinstance(e, int) and e < 2):
                    sp.wait_ge(s_ewl, 8 * (e - 1))
                sp.dma_start(EWF[q][:, 0:1024].rearrange("p (k h) -> p k h", k=KC), w_in_v[i, q]).then_inc(s_ewld[q], 16)
                sp.dma_start(EWF[q][:, 1024:2048].rearrange("p (k h) -> p k h", k=HC), w_out_v[i, q]).then_inc(s_ewld[q], 16)
            expert_load(0, 0)
            expert_load(1, 1)

            def emit(step, b, p, half):
                if step == "load":
                    if past(b, 2):
                        sp.wait_ge(s_xb, b - 1)
                    if past(b, 2):
                        sp.wait_ge(s_xT, b - 1)
                    sp.dma_start(X[p][:], x_v[half, p]).then_inc(s_xld[p], 16)
                    if past(b, 2):
                        sp.wait_ge(s_cT, b - 1)
                    sp.dma_start(C[p][:], ctx_v[half, p]).then_inc(s_cld[p], 16)
                if step == "keep":
                    sp.wait_ge(s_x2, b + 1)
                    sp.dma_start(X2all_v[:, half, p, :], X2[p][:]).then_inc(s_x2st[p], 16)
            pipeline(sp, "load/0 keep/3", emit)

            with sp.Fori(1, NE // 2) as i:
                for q in range(2):
                    expert_load(2 * i + q, q, i)
            for g in range(NB // GT):
                sp.wait_ge(s_fy, GT * (g + 1))
                sp.dma_start(out.rearrange("b p d -> p b d")[:, GT * g:GT * g + GT, :],
                             X2all[:, GT * g:GT * g + GT, :]).then_inc(s_outs, 16)
            sp.wait_ge(s_outs, 16 * (NB // GT))

        @block.gpsimd
        def _(pool):
            pool.memset(ident[:], 0.0).then_inc(s_cst, 1)
            pool.memset(identb[:], 0.0).then_inc(s_cst, 1)
            pool.memset(blockmask[:], 1.0).then_inc(s_cst, 1)
            pool.memset(pick[:], 0.0).then_inc(s_cst, 1)
            pool.memset(lower[:], 1.0).then_inc(s_cst, 1)
            pool.memset(neghalf[:], -0.5).then_inc(s_cst, 1)
            for p in range(2):
                pool.memset(NM[p][:], 0.0).then_inc(s_cst, 1)
                pool.memset(V2[p][:], 1.0).then_inc(s_cst, 1)
            pool.wait_ge(s_cst, 10)
            for t in (ident, identb):
                pool.affine_select(out=t[:], in_=t[:], compare_op=ALU.not_equal, fill=1.0, base=0,
                                   pattern=[[-1, P]], channel_multiplier=1).then_inc(s_cstb, 1)
            bm = blockmask[:].rearrange("p (g d) -> p g d", g=8)
            pool.affine_select(out=bm, in_=bm, compare_op=ALU.is_ge, fill=0.0, base=0,
                               pattern=[[-DH, 8], [0, DH]], channel_multiplier=1).then_inc(s_cstb, 1)
            pool.wait_ge(s_cstb, 3)
            pool.affine_select(out=bm, in_=bm, compare_op=ALU.is_ge, fill=0.0, base=DH - 1,
                               pattern=[[DH, 8], [0, DH]], channel_multiplier=-1).then_inc(s_cstb, 1)
            for q in range(2):
                pool.affine_select(out=pick[:], in_=pick[:], compare_op=ALU.not_equal, fill=1.0, base=-64 * q,
                                   pattern=[[-1, 8], [0, P]], channel_multiplier=1).then_inc(s_cstb, 1)
                pool.wait_ge(s_cstb, 5 + q)
            pool.affine_select(out=lower[:], in_=lower[:], compare_op=ALU.is_ge, fill=0.0, base=-1,
                               pattern=[[1, NE], [-1, NE]], channel_multiplier=0).then_inc(s_cstb, 1)

            def norm(n, p, b, src, dst, signal):
                pool.wait_ge(s_ve[n], b + 1)
                pool.tensor_tensor(rstd[n][p][:], veps[n][p][:], neghalf[:, 0:1], ALU.pow).then_inc(s_rs[n], 1)
                pool.wait_ge(s_cstb, 7)
                pool.wait_ge(s_nm[n], b + 1)
                pool.wait_ge(s_rs[n], b + 1)
                pool.tensor_scalar(dst, src, nmu[n][p][:], rstd[n][p][:], ALU.add, ALU.mult).then_inc(signal, 1)

            def emit(step, b, p, half):
                if step == "xb":
                    pool.wait_ge(s_bo_fold, 1)
                    pool.wait_ge(s_xld[p], 8 * b + 16 - 8 * p)
                    if past(b, 2):
                        pool.wait_ge(s_r1, b - 1)
                    pool.tensor_tensor(XB[p][:], X[p][:], rowb[:, RO:RO + D], ALU.add).then_inc(s_xb, 1)
                if step == "qs":
                    pool.wait_ge(s_qmax, b + 1)
                    if past(b, 2):
                        pool.wait_ge(s_qe, b - 1)
                    pool.tensor_tensor(QS[p][:].rearrange("p (h d) -> p h d", h=NH),
                                       QV[p][:, 0:D].rearrange("p (h d) -> p h d", h=NH),
                                       qmax[p][:].unsqueeze(2).to_broadcast([P, NH, DH]),
                                       ALU.subtract).then_inc(s_qs, 1)
                if step == "norm0":
                    if past(b, 2):
                        pool.wait_ge(s_onT, b - 1)
                    norm(0, p, b, ON[p][:], OL[p][:], s_ln0)
                if step == "norm1":
                    if past(b, 2):
                        pool.wait_ge(s_x1T, b - 1)
                    if past(b, 2):
                        pool.wait_ge(s_x1b, b - 1)
                    norm(1, p, b, R1[p][:], X1[p][:], s_x1)
                if step == "x1b":
                    pool.wait_ge(s_x1, b + 1)
                    pool.tensor_tensor(X2all_v[:, half, p, :], X1[p][:], rowb[:, RO2:RO2 + D], ALU.add)\
                        .then_inc(s_x1b, 1)
                if step[:-1] == "exl":
                    u = int(step[-1])
                    pool.wait_ge(s_exh, 4 * b + u + 1)
                    if past(b, 2):
                        pool.wait_ge(s_pv, 4 * b - 7 + u)
                    pool.tensor_tensor(EXl[p][:, u, :, :], EX[u % 2][:], EXh[p][:, u, :, :], ALU.subtract)\
                        .then_inc(s_exl, 1)
                if step == "norm2":
                    if past(b, 2):
                        pool.wait_ge(s_x2T, b - 1)
                    if past(b, 2):
                        pool.wait_ge(s_x2st[p], 8 * b - 8 * p)
                    norm(2, p, b, R2[p][:], X2[p][:], s_x2)
            pipeline(pool, "exl3/2 qs/0 xb/0 norm0/0 exl0/1 norm2/3 exl1/1 norm1/0 x1b/0 exl2/1", emit)

            for g in range(NB // GT):
                pool.wait_ge(s_fve, g + 1)
                pool.tensor_tensor(frs[:, GT * g:GT * g + GT], fve[:, GT * g:GT * g + GT],
                                   neghalf[:, 0:GT], ALU.pow).then_inc(s_frs, 1)

        @block.scalar
        def _(act):
            for q in range(4):
                act.wait_ge(s_w_ld[q], 16)
                if q == 1:
                    act.wait_ge(s_wo_fold, KC)
                act.activation(wh[:, :, 512 * q:512 * q + 512], stage[:, :, 512 * q:512 * q + 512],
                               ACT.Copy, scale=PSCALE).then_inc(s_wsp_h, 1)

            def copy(dst, src, signal):
                act.activation(dst, src, ACT.Copy).then_inc(signal, 1)

            def emit(step, b, p, half):
                if step == "XTh":
                    act.wait_ge(s_xT, b + 1)
                    if past(b, 2):
                        act.wait_ge(s_k_ps, b - 1)
                    copy(XTh[p][:], chunks(bank[0], KC), s_xTh)
                if step == "ke":
                    act.wait_ge(s_knb, b + 1)
                    if past(b, 2):
                        act.wait_ge(s_qk_ps, b - 1)
                    for c in range(KC):
                        act.activation(KE[p][:, c, :], bank[2][:, c * P:(c + 1) * P], ACT.Exp,
                                       bias=knb[p][:, c:c + 1], scale=1.0 / PSCALE,
                                       accum_out=ksum[p][:, c:c + 1]).then_inc(s_ke, 1)
                if step == "qe":
                    act.wait_ge(s_qs, b + 1)
                    if past(b, 2):
                        act.wait_ge(s_qk_ps, b - 1)
                    act.activation(QE[p][:], QS[p][:], ACT.Exp).then_inc(s_qe, 1)
                if step == "qkT":
                    act.wait_ge(s_qk_ps, b + 1)
                    if past(b, 2):
                        act.wait_ge(s_o_ps, b - 1)
                    copy(QKT[p][:], chunks(bank[2], 2 * KC), s_qkT)
                if step == "OTh":
                    act.wait_ge(s_onT, b + 1)
                    if past(b, 2):
                        act.wait_ge(s_ao_ps, b - 1)
                    copy(OTh[p][:], chunks(bank[3], KC), s_onTh)
                if step == "CTh":
                    act.wait_ge(s_cT, b + 1)
                    if past(b, 2):
                        act.wait_ge(s_v2_ps, b - 1)
                    copy(CTh[p][:], chunks(bank[6], KC), s_cTh)
                if step == "X1Th":
                    act.wait_ge(s_x1T, b + 1)
                    if past(b, 2):
                        act.wait_ge(s_q2_ps, b - 1)
                    copy(X1Th[p][:], chunks(bank[2], KC), s_x1Th)
                if step == "MT":
                    act.wait_ge(s_mT_ps, b + 1)
                    if past(b, 2):
                        act.wait_ge(s_sc, 4 * b - 4)
                    copy(MT[p][:], bank[7][:, 0:P // 2].bitcast(bf16), s_mT)
                if step[:-1] == "ex":
                    u = int(step[-1])
                    act.wait_ge(s_sc, 4 * b + u + 1)
                    if past(4 * b + u, 2):
                        act.wait_ge(s_exl, 4 * b + u - 1)
                    act.activation(EX[u % 2][:], chunks(bank[SC_BANK[u]], 4), ACT.Exp,
                                   scale=DH ** -0.5 / PSCALE ** 2).then_inc(s_ex, 1)
                    if past(b, 2):
                        act.wait_ge(s_pv, 4 * b - 7 + u)
                    act.activation(EXh[p][:, u, :, :], chunks(bank[SC_BANK[u]], 4), ACT.Exp,
                                   scale=DH ** -0.5 / PSCALE ** 2).then_inc(s_exh, 1)
                if step == "k2h":
                    act.wait_ge(s_k2_ps, b + 1)
                    if past(b, 2):
                        act.wait_ge(s_sc, 4 * b - 4)
                    for c in range(KC):
                        act.activation(K2h[p][:, c, :], bank[6][:, c * P:(c + 1) * P], ACT.Identity,
                                       bias=bk2s[:, c:c + 1]).then_inc(s_k2h, 1)
                if step == "q2h":
                    act.wait_ge(s_q2_ps, b + 1)
                    if past(b, 2):
                        act.wait_ge(s_qmh, 4 * b - 4)
                    if past(b, 2):
                        act.wait_ge(s_q2l, 2 * b - 2)
                    for c in range(KC):
                        act.activation(Q2h[p][:, c, :], bank[1][:, c * P:(c + 1) * P], ACT.Identity,
                                       bias=bq2s[:, c:c + 1]).then_inc(s_q2h, 1)
                if step == "qml":
                    act.wait_ge(s_q2l, 2 * b + 2)
                    if past(b, 2):
                        act.wait_ge(s_sc, 4 * b - 4)
                    for j in range(4):
                        act.activation(QMl[p][:, :, j, :], Q2l[p][:], ACT.Copy, scale=mask4[:, j:j + 1])\
                           .then_inc(s_qml, 1)
                if step == "v2h":
                    act.wait_ge(s_v2, b + 1)
                    if past(b, 2):
                        act.wait_ge(s_pv, 4 * b - 4)
                    copy(V2h[p][:], V2[p][:], s_v2h)
                if step == "O2Th":
                    act.wait_ge(s_o2T, b + 1)
                    if past(b, 2):
                        act.wait_ge(s_ao2, b - 1)
                    copy(O2Th[p][:], chunks(bank[5], KC), s_o2Th)
                if step == "X2Th":
                    act.wait_ge(s_x2T, b + 1)
                    copy(X2Th_v[:, :, half, p, :], chunks(bank[4], KC), s_x2Th)
            pipeline(act, "XTh/0 q2h/1 ex3/2 ke/0 qe/0 qkT/0 qml/1 MT/1 ex0/1 O2Th/2 OTh/0 CTh/0 ex1/1 k2h/0 ex2/1 "
                          "v2h/0 X2Th/3 X1Th/0", emit)

            for g in range(4):
                act.wait_ge(s_g_ps, g + 1)
                act.activation(GG[:, 512 * g:512 * g + 512], bank[g][0:G, :], ACT.Gelu,
                               bias=bg1_c[:], scale=1.0 / WSCALE).then_inc(s_gg, 1)
            act.wait_ge(s_lsb, 2)
            act.activation(LE[:], L[:], ACT.Exp).then_inc(s_lsb, 1)

            def weights_high(e, q, part):
                act.wait_ge(s_ewld[q], 16 * e + 32 - 16 * q)
                if not (isinstance(e, int) and e < 2):
                    act.wait_ge(s_dn, 16 * (e - 1))
                for i in range(2):
                    lo = 1024 * i + 256 * part
                    act.activation(EWH[q][:, lo:lo + 256], EWF[q][:, lo:lo + 256], ACT.Copy,
                                   scale=WSCALE).then_inc(s_ewh, 1)
            for part in range(4):
                weights_high(0, 0, part)

            def expert(e, q, g, nxt):
                n = 4 * e + g
                for h in range(HC):
                    act.wait_ge(s_up, 4 * n + h + 1)
                    if not isinstance(n, int) or n > 0:
                        act.wait_ge(s_hl, 4 * n - 4 + h + 1)
                    act.activation(HF[:, h, :], bank[h][:, :], ACT.Gelu, scale=1.0 / WSCALE).then_inc(s_hf, 1)
                if nxt:
                    weights_high(e + 1, 1 - q, g)
            for q in range(2):
                for g in range(4):
                    expert(q, q, g, True)
            with act.Fori(1, NE // 2 - 1) as i:
                for q in range(2):
                    for g in range(4):
                        expert(2 * i + q, q, g, True)
            for q in range(2):
                for g in range(4):
                    expert(NE - 2 + q, q, g, q == 0)

        @block.vector
        def _(dve):
            chain = [0]

            def small(op):
                chain[0] += 1
                op.then_inc(s_prep, 1)
                dve.wait_ge(s_prep, chain[0])

            dve.wait_ge(s_cstb, 7)
            small(dve.tensor_tensor(mask4[:], blockmask[:, 0:P // 2:DH], blockmask[:, P // 2:P:DH], ALU.add))
            for p in range(2):
                for c in range(KC):
                    small(dve.tensor_copy(ST[p][:, c, P:P + 8], blockmask[:, 0:P:DH]))
            dve.wait_ge(s_vec_ld, 16)
            small(dve.tensor_scalar(bq2s[:], vec[:, VQ2:VQ2 + KC], PSCALE, None, ALU.mult))
            small(dve.tensor_scalar(bk2s[:], vec[:, VK2:VK2 + KC], PSCALE, None, ALU.mult))
            for c in range(KC):
                dve.tensor_copy(lnb_rep[:, c, :], vec[:, VB + c:VB + c + 1].to_broadcast([P, P]))\
                   .then_inc(s_lnb, 1)

            def weights_low(q):
                dve.wait_ge(s_wsp_h, q + 1)
                cols = slice(512 * q, 512 * q + 512)
                for c in range(KC):
                    dve.scalar_tensor_tensor(wl[:, c, cols], stage[:, c, cols], PSCALE, wh[:, c, cols],
                                             ALU.mult, ALU.subtract).then_inc(s_wsp_l, 1)
            weights_low(0)
            dve.wait_ge(s_bo_ps, 1)
            dve.wait_ge(s_rows_ld, 16)
            dve.tensor_tensor(rowb[:, RO:RO + D], bank[0][:, 0:D], rowb[:, RO:RO + D], ALU.add)\
               .then_inc(s_bo_fold, 1)
            for c in range(KC):
                dve.tensor_scalar(stage[:, c, CO:CO + D], stage[:, c, CO:CO + D], vec[:, VG + c:VG + c + 1],
                                  None, ALU.mult).then_inc(s_wo_fold, 1)
            for q in range(1, 4):
                weights_low(q)
            dve.wait_ge(s_g_ld, 48)
            small(dve.tensor_scalar(wg1h[:], wg1_f[:], WSCALE, None, ALU.mult))
            dve.scalar_tensor_tensor(wg1l[:], wg1_f[:], WSCALE, wg1h[:], ALU.mult, ALU.subtract)\
               .then_inc(s_wsp_l, 1)

            def low(dst, src, high, high_done, signal, row):
                dve.wait_ge(high_done, row + 1)
                dve.tensor_tensor(dst, src, high, ALU.subtract).then_inc(signal, 1)

            def stats(n, p, b, src, ready, parts=1):
                dve.wait_ge(ready, parts * b + parts)
                dve.bn_stats(bst[n][p][:], src).then_inc(s_bs[n], 1)
                dve.wait_ge(s_cstb, 7)
                dve.wait_ge(s_bs[n], b + 1)
                dve.bn_aggr(mv[n][p][:], bst[n][p][:]).then_inc(s_mv[n], 1)
                dve.wait_ge(s_mv[n], b + 1)
                if past(b, 2):
                    dve.wait_ge((s_ln0, s_x1, s_x2)[n], b - 1)
                dve.tensor_scalar(veps[n][p][:], mv[n][p][:, 1:2], EPS, None, ALU.add).then_inc(s_ve[n], 1)
                dve.tensor_scalar(nmu[n][p][:], mv[n][p][:, 0:1], -1.0, None, ALU.mult).then_inc(s_nm[n], 1)

            def emit(step, b, p, half):
                if step == "XTl":
                    low(XTl[p][:], chunks(bank[0], KC), XTh[p][:], s_xTh, s_xTl, b)
                if step == "qvsb":
                    dve.wait_ge(s_qv_ps, b + 1)
                    if past(b, 2):
                        dve.wait_ge(s_qs, b - 1)
                    if past(b, 2):
                        dve.wait_ge(s_st_ps, b - 1)
                    dve.scalar_tensor_tensor(QV[p][:], bank[0][:, :], 1.0 / PSCALE, rowb[:, RQV:RQV + 2 * D],
                                             ALU.mult, ALU.add).then_inc(s_qv_sb, 1)
                if step == "kmax":
                    dve.wait_ge(s_k_ps, b + 1)
                    dve.tensor_reduce(kmax[p][:], chunks(bank[2], KC), AX.X, ALU.max).then_inc(s_km, 1)
                    dve.wait_ge(s_km, 2 * b + 1)
                    dve.scalar_tensor_tensor(kmax[p][:], kmax[p][:], 1.0 / PSCALE, vec[:, VK:VK + KC],
                                             ALU.mult, ALU.add).then_inc(s_km, 1)
                    dve.wait_ge(s_km, 2 * b + 2)
                    if past(b, 2):
                        dve.wait_ge(s_ke, 2 * b - 2)
                    dve.tensor_tensor(knb[p][:], vec[:, VK:VK + KC], kmax[p][:], ALU.subtract).then_inc(s_knb, 1)
                if step == "qmax":
                    dve.wait_ge(s_qv_sb, b + 1)
                    dve.tensor_reduce(qmax[p][:], QV[p][:, 0:D].rearrange("p (h d) -> p h d", h=NH), AX.X,
                                      ALU.max).then_inc(s_qmax, 1)
                if step == "krec":
                    dve.wait_ge(s_ke, 2 * b + 2)
                    dve.reciprocal(krec[p][:], ksum[p][:]).then_inc(s_krec, 1)
                if step == "ST":
                    dve.wait_ge(s_st_ps, b + 1)
                    dve.wait_ge(s_krec, b + 1)
                    if past(b, 2):
                        dve.wait_ge(s_o_ps, b - 1)
                    for c in range(KC):
                        dve.scalar_tensor_tensor(ST[p][:, c, 0:P], bank[1][:, c * P:(c + 1) * P],
                                                 krec[p][:, c:c + 1], blockmask[:], ALU.mult, ALU.mult)\
                           .then_inc(s_st, 1)
                if step == "on":
                    dve.wait_ge(s_o_ps, b + 1)
                    o = chunks(bank[2], KC, P + 8)
                    dve.reciprocal(qrec[p][:].rearrange("p (c h) -> p c h", c=KC), o[:, :, P:P + 8])\
                       .then_inc(s_qrec, 1)
                    dve.wait_ge(s_qrec, b + 1)
                    if past(b, 2):
                        dve.wait_ge(s_ln0, b - 1)
                    for c in range(KC):
                        dve.tensor_tensor(ON[p][:, c * P:(c + 1) * P].rearrange("p (h d) -> p h d", d=DH),
                                          o[:, c, 0:P].rearrange("p (h d) -> p h d", d=DH),
                                          qrec[p][:, 8 * c:8 * c + 8].unsqueeze(2).to_broadcast([P, 8, DH]),
                                          ALU.mult).then_inc(s_on, 1)
                if step == "stats0":
                    stats(0, p, b, ON[p][:], s_on, 2)
                if step == "OTl":
                    low(OTl[p][:], chunks(bank[3], KC), OTh[p][:], s_onTh, s_onTl, b)
                if step == "CTl":
                    low(CTl[p][:], chunks(bank[6], KC), CTh[p][:], s_cTh, s_cTl, b)
                if step == "R1":
                    dve.wait_ge(s_ao_ps, b + 1)
                    dve.wait_ge(s_xb, b + 1)
                    if past(b, 2):
                        dve.wait_ge(s_x1, b - 1)
                    dve.scalar_tensor_tensor(R1[p][:], bank[3][:, 0:D], 1.0 / PSCALE, XB[p][:], ALU.mult, ALU.add)\
                       .then_inc(s_r1, 1)
                    stats(1, p, b, R1[p][:], s_r1)
                if step == "X1Tl":
                    low(X1Tl[p][:], chunks(bank[2], KC), X1Th[p][:], s_x1Th, s_x1Tl, b)
                if step == "v2sb":
                    dve.wait_ge(s_v2_ps, b + 1)
                    if past(b, 2):
                        dve.wait_ge(s_v2l, b - 1)
                    dve.scalar_tensor_tensor(V2[p][:, :, 0:DH], bank[0][:, 0:D].rearrange("p (h d) -> p h d", h=NH),
                                             1.0 / PSCALE, rowb[:, RV2:RV2 + D].rearrange("p (h d) -> p h d", h=NH),
                                             ALU.mult, ALU.add).then_inc(s_v2, 1)
                if step == "k2l":
                    if past(b, 2):
                        dve.wait_ge(s_sc, 4 * b - 4)
                    dve.wait_ge(s_k2h, 2 * b + 2)
                    for c in range(KC):
                        dve.scalar_tensor_tensor(K2l[p][:, c, :], bank[6][:, c * P:(c + 1) * P], bk2s[:, c:c + 1],
                                                 K2h[p][:, c, :], ALU.add, ALU.subtract).then_inc(s_k2l, 1)
                if step == "qmh":
                    dve.wait_ge(s_q2h, 2 * b + 2)
                    if past(b, 2):
                        dve.wait_ge(s_sc, 4 * b - 4)
                    for j in range(4):
                        dve.tensor_scalar(QMh[p][:, :, j, :], Q2h[p][:], mask4[:, j:j + 1], None, ALU.mult)\
                           .then_inc(s_qmh, 1)
                if step == "q2l":
                    dve.wait_ge(s_q2h, 2 * b + 2)
                    if past(b, 2):
                        dve.wait_ge(s_qml, 4 * b - 4)
                    for c in range(KC):
                        dve.scalar_tensor_tensor(Q2l[p][:, c, :], bank[1][:, c * P:(c + 1) * P], bq2s[:, c:c + 1],
                                                 Q2h[p][:, c, :], ALU.add, ALU.subtract).then_inc(s_q2l, 1)
                if step == "v2l":
                    dve.wait_ge(s_v2h, b + 1)
                    if past(b, 2):
                        dve.wait_ge(s_pv, 4 * b - 4)
                    dve.tensor_tensor(V2l[p][:], V2[p][:], V2h[p][:], ALU.subtract).then_inc(s_v2l, 1)
                if step == "mx":
                    if past(b, 2):
                        dve.wait_ge(s_mT_ps, b - 1)
                    for u in range(4):
                        dve.wait_ge(s_nat, 4 * b + u + 1)
                        dve.tensor_reduce(NM[p][:, u % 2, 4 * (u // 2):4 * (u // 2) + 4], chunks(bank[NAT_BANK[u]], 4), AX.X, ALU.max,
                                          negate=True).then_inc(s_mx, 1)
                if step == "o2":
                    dve.wait_ge(s_pv, 4 * b + 4)
                    pv = chunks(bank[6], NH, DH + 1)
                    dve.reciprocal(r2[p][:], pv[:, :, DH]).then_inc(s_r2, 1)
                    dve.wait_ge(s_r2, b + 1)
                    if past(b, 2):
                        dve.wait_ge(s_o2T, b - 1)
                    dve.tensor_tensor(O2[p][:].rearrange("p (h d) -> p h d", h=NH), pv[:, :, 0:DH],
                                      r2[p][:].unsqueeze(2).to_broadcast([P, NH, DH]), ALU.mult).then_inc(s_o2, 1)
                if step == "O2Tl":
                    low(O2Tl[p][:], chunks(bank[5], KC), O2Th[p][:], s_o2Th, s_o2Tl, b)
                if step == "R2":
                    dve.wait_ge(s_ao2, b + 1)
                    dve.wait_ge(s_x1b, b + 1)
                    if past(b, 2):
                        dve.wait_ge(s_x2, b - 1)
                    dve.scalar_tensor_tensor(R2[p][:], bank[3][:, 0:D], 1.0 / PSCALE, X2all_v[:, half, p, :], ALU.mult, ALU.add)\
                       .then_inc(s_r2x, 1)
                    stats(2, p, b, R2[p][:], s_r2x)
                if step == "X2Tl":
                    low(X2Tl_v[:, :, half, p, :], chunks(bank[4], KC), X2Th_v[:, :, half, p, :], s_x2Th, s_x2Tl, b)
            pipeline(dve, "X1Tl/1 XTl/0 qmh/1 qvsb/0 kmax/0 qmax/0 q2l/1 krec/0 mx/1 ST/0 o2/2 on/0 stats0/0 R2/3 O2Tl/2 "
                          "OTl/0 CTl/0 R1/0 k2l/0 v2sb/0 v2l/0 X2Tl/3", emit)

            dve.wait_ge(s_l_ps, 1)
            logits = bank[4][:, 0:NB * NE].rearrange("p (b e) -> p b e", b=NB)
            dve.tensor_reduce(lmax[:], logits, AX.X, ALU.max).then_inc(s_lsb, 1)
            dve.wait_ge(s_lsb, 1)
            dve.tensor_tensor(L[:], logits, lmax[:].unsqueeze(2).to_broadcast([P, NB, NE]), ALU.subtract)\
               .then_inc(s_lsb, 1)
            dve.wait_ge(s_lsb, 3)
            small(dve.tensor_reduce(lsum[:], LE[:], AX.X, ALU.add))
            small(dve.reciprocal(lrec[:], lsum[:]))
            small(dve.tensor_tensor(PR[:], LE[:], lrec[:].unsqueeze(2).to_broadcast([P, NB, NE]), ALU.mult))
            mine = PR[:].unsqueeze(3).to_broadcast([P, NB, NE, NE])
            for b in range(NB):
                small(dve.tensor_copy(CMQ[:, b, :, :], PR[:, b, :].unsqueeze(1).to_broadcast([P, NE, NE])))
            small(dve.tensor_tensor(CMP, CMQ, mine, ALU.is_equal))
            for b in range(NB):
                small(dve.tensor_tensor(CMP[:, b, :, :], CMP[:, b, :, :], lower[:], ALU.mult))
            small(dve.tensor_tensor(CMQ, CMQ, mine, ALU.is_gt))
            small(dve.tensor_tensor(CMP, CMP, CMQ, ALU.add))
            small(dve.tensor_reduce(rank[:], CMP, AX.X, ALU.add))
            small(dve.tensor_scalar(rank[:], rank[:], 1.5, 1.0 / WSCALE, ALU.is_lt, ALU.mult))
            small(dve.tensor_tensor(gates[:], PR[:], rank[:], ALU.mult))
            for p in range(2):
                dve.wait_ge(s_x2st[p], 8 * NB)

            def weights_low_e(e, q, part):
                if not (isinstance(e, int) and e < 2):
                    dve.wait_ge(s_dn, 16 * (e - 1))
                for i in range(2):
                    dve.wait_ge(s_ewh, 8 * e + 2 * part + i + 1)
                    lo = 1024 * i + 256 * part
                    dve.scalar_tensor_tensor(EWL[q][:, lo:lo + 256], EWF[q][:, lo:lo + 256], WSCALE,
                                             EWH[q][:, lo:lo + 256], ALU.mult, ALU.subtract).then_inc(s_ewl, 1)
            for part in range(4):
                weights_low_e(0, 0, part)

            def split_hidden(e, q, g, n, first):
                for h in range(HC):
                    dve.wait_ge(s_hf, 4 * n + h + 1)
                    if not first:
                        dve.wait_ge(s_dn, 4 * (n - 1))
                    dve.tensor_copy(HH[n_par(g)][:, h, :], HF[:, h, :]).then_inc(s_hh, 1)
                    dve.wait_ge(s_hh, 4 * n + h + 1)
                    dve.tensor_tensor(HL[n_par(g)][:, h, :], HF[:, h, :], HH[n_par(g)][:, h, :], ALU.subtract)\
                       .then_inc(s_hl, 1)

            def n_par(g):
                return g % 2

            def accumulate(i, q, g, n):
                for t in range(GT):
                    b = GT * g + t
                    dve.wait_ge(s_dn, 4 * n + t + 1)
                    if not isinstance(n, int) or n >= 4:
                        dve.wait_ge(s_acc, 4 * (n - 4) + t + 1)
                    dve.scalar_tensor_tensor(X2all[:, b, :], bank[4 + t][:, 0:D], gates_v[:, b, i, q:q + 1],
                                             X2all[:, b, :], ALU.mult, ALU.add).then_inc(s_acc, 1)

            def step(i, q, g, nxt):
                e = 2 * i + q
                n = 4 * e + g
                first = isinstance(n, int) and n < 2
                split_hidden(e, q, g, n, first)
                if not isinstance(n, int) or n > 0:
                    if g:
                        accumulate(i, q, g - 1, n - 1)
                    else:
                        accumulate(i + (q - 1) // 2, 1 - q, 3, n - 1)
                if nxt:
                    weights_low_e(e + 1, 1 - q, g)
            for q in range(2):
                for g in range(4):
                    step(0, q, g, True)
            with dve.Fori(1, NE // 2 - 1) as i:
                for q in range(2):
                    for g in range(4):
                        step(i, q, g, True)
            for q in range(2):
                for g in range(4):
                    step(NE // 2 - 1, q, g, q == 0)
            accumulate(NE // 2 - 1, 1, 3, 4 * NE - 1)

            for g in range(NB // GT):
                rows4 = range(GT * g, GT * g + GT)
                for b in rows4:
                    if b % GT == 0:
                        dve.wait_ge(s_acc, 4 * (4 * (NE - 1) + g + 1))
                    dve.bn_stats(fst[:, b, :], X2all[:, b, :]).then_inc(s_fbs, 1)
                for b in rows4:
                    dve.wait_ge(s_fbs, b + 1)
                    dve.bn_aggr(fmv[:, b, :], fst[:, b, :]).then_inc(s_fmv, 1)
                dve.wait_ge(s_fmv, GT * (g + 1))
                dve.tensor_scalar(fve[:, GT * g:GT * g + GT], fmv[:, GT * g:GT * g + GT, 1], EPS, None, ALU.add)\
                   .then_inc(s_fve, 1)
            for b in range(NB):
                if b % GT == 0:
                    dve.wait_ge(s_frs, b // GT + 1)
                dve.tensor_scalar(X2all[:, b, :], X2all[:, b, :], fmv[:, b, 0:1], frs[:, b:b + 1],
                                  ALU.subtract, ALU.mult).then_inc(s_fy, 1)

        @block.tensor
        def _(pe):
            pe.wait_ge(s_cstb, 7)
            pe.wait_ge(s_w_ld[1], 16)
            pe.wait_ge(s_lnb, KC)
            for c in range(KC):
                last = pe.matmul(bank[0][:, 0:D], lnb_rep[:, c, :], stage[:, c, CO:CO + D],
                                 start=(c == 0), stop=(c == KC - 1))
            last.then_inc(s_bo_ps, 1)
            pe.wait_ge(s_wsp_l, 4 * KC + 1)

            def w(t, col, width):
                return lambda c: t[:, c, col:col + width]

            def feature_major(dst, col, th, tl, signal):
                for f in range(KC):
                    last = split3(pe, dst[:, f * P:(f + 1) * P],
                                  w(wh, col + f * P, P), w(wl, col + f * P, P),
                                  lambda c: th[:, c, :], lambda c: tl[:, c, :])
                last.then_inc(signal, 1)

            def token_major(dst, col, width, th, tl, signal):
                split3(pe, dst, lambda c: th[:, c, :], lambda c: tl[:, c, :],
                       w(wh, col, width), w(wl, col, width)).then_inc(signal, 1)

            def turn(dst, src, n, signal):
                for c in range(n):
                    last = pe.transpose(dst[:, c * P:(c + 1) * P], src(c), ident[:])
                last.then_inc(signal, 1)

            def emit(step, b, p, half):
                if step == "xT":
                    pe.wait_ge(s_xld[p], 8 * b + 16 - 8 * p)
                    if past(b, 1):
                        pe.wait_ge(s_v2, b)
                    turn(bank[0], lambda c: X[p][:, c * P:(c + 1) * P], KC, s_xT)
                if step == "qv":
                    pe.wait_ge(s_xTl, b + 1)
                    token_major(bank[0][:, :], CQV, 2 * D, XTh[p], XTl[p], s_qv_ps)
                if step == "v2":
                    pe.wait_ge(s_cTl, b + 1)
                    pe.wait_ge(s_qv_sb, b + 1)
                    if past(b, 1):
                        pe.wait_ge(s_exh, 4 * b - 2)
                    token_major(bank[0][:, 0:D], CV2, D, CTh[p], CTl[p], s_v2_ps)
                if step == "kk":
                    pe.wait_ge(s_xTl, b + 1)
                    if past(b, 1):
                        pe.wait_ge(s_x1Tl, b)
                    feature_major(bank[2], CK, XTh[p], XTl[p], s_k_ps)
                if step == "qk":
                    pe.wait_ge(s_qe, b + 1)
                    pe.wait_ge(s_ke, 2 * b + 2)
                    for c in range(KC):
                        pe.transpose(bank[2][:, c * P:(c + 1) * P], QE[p][:, c * P:(c + 1) * P], ident[:])
                    turn(bank[2][:, D:2 * D], lambda c: KE[p][:, c, :], KC, s_qk_ps)
                if step == "o":
                    pe.wait_ge(s_qkT, b + 1)
                    pe.wait_ge(s_st, 2 * b + 2)
                    o = chunks(bank[2], KC, P + 8)
                    for c in range(KC):
                        last = pe.matmul(o[:, c, :], QKT[p][:, c, :], ST[p][:, c, :], start=True, stop=True)
                    last.then_inc(s_o_ps, 1)
                if step == "x1T":
                    pe.wait_ge(s_x1, b + 1)
                    pe.wait_ge(s_on, 2 * b + 2)
                    turn(bank[2], lambda c: X1[p][:, c * P:(c + 1) * P], KC, s_x1T)
                if step == "q2":
                    pe.wait_ge(s_x1Tl, b + 1)
                    pe.wait_ge(s_st, 2 * b + 2)
                    if past(b, 1):
                        pe.wait_ge(s_exh, 4 * b - 1)
                    feature_major(bank[1], CQ2, X1Th[p], X1Tl[p], s_q2_ps)
                if step == "st":
                    pe.wait_ge(s_qkT, b + 1)
                    if past(b, 1):
                        pe.wait_ge(s_q2l, 2 * b)
                    for c in range(KC):
                        last = pe.matmul(bank[1][:, c * P:(c + 1) * P], QKT[p][:, KC + c, :],
                                         QV[p][:, D + c * P:D + (c + 1) * P], start=True, stop=True)
                    last.then_inc(s_st_ps, 1)
                if step == "onT":
                    pe.wait_ge(s_ln0, b + 1)
                    if past(b, 3):
                        pe.wait_ge(s_r2x, b - 2)
                    elif past(b, 1):
                        pe.wait_ge(s_mx, 4 * b - 1)
                    turn(bank[3], lambda c: OL[p][:, c * P:(c + 1) * P], KC, s_onT)
                if step == "ao":
                    pe.wait_ge(s_onTl, b + 1)
                    token_major(bank[3][:, 0:D], CO, D, OTh[p], OTl[p], s_ao_ps)
                if step == "ao2":
                    pe.wait_ge(s_o2Tl, b + 1)
                    pe.wait_ge(s_mx, 4 * upto(b + 3) - 1)
                    token_major(bank[3][:, 0:D], CO2, D, O2Th[p], O2Tl[p], s_ao2)
                if step == "cT":
                    pe.wait_ge(s_cld[p], 8 * b + 16 - 8 * p)
                    if past(b, 1):
                        pe.wait_ge(s_exh, 4 * b - 3)
                    turn(bank[6], lambda c: C[p][:, c * P:(c + 1) * P], KC, s_cT)
                if step == "k2":
                    pe.wait_ge(s_cTl, b + 1)
                    feature_major(bank[6], CK2, CTh[p], CTl[p], s_k2_ps)
                if step == "pv":
                    pe.wait_ge(s_v2l, b + 1)
                    pe.wait_ge(s_k2l, 2 * upto(b + 2))
                    for u in range(4):
                        pe.wait_ge(s_exl, 4 * b + u + 1)
                        for j in range(4):
                            h = 4 * u + j
                            last = split3(pe, bank[6][:, h * (DH + 1):(h + 1) * (DH + 1)],
                                          lambda c: EXh[p][:, u, j, :], lambda c: EXl[p][:, u, j, :],
                                          lambda c: V2h[p][:, h, :], lambda c: V2l[p][:, h, :], 1)
                        last.then_inc(s_pv, 1)
                if step == "mT":
                    pe.wait_ge(s_mx, 4 * b + 4)
                    pe.transpose(bank[7][:, 0:P // 2].bitcast(bf16), NM[p][:].rearrange("p s m -> p (s m)"),
                                 identb[:]).then_inc(s_mT_ps, 1)
                if step == "o2T":
                    pe.wait_ge(s_o2, b + 1)
                    pe.wait_ge(s_mx, 4 * upto(b + 2) - 2)
                    turn(bank[5], lambda c: O2[p][:, c * P:(c + 1) * P], KC, s_o2T)
                if step == "x2T":
                    pe.wait_ge(s_x2, b + 1)
                    pe.wait_ge(s_mx, 4 * upto(b + 3) - 3)
                    turn(bank[4], lambda c: X2[p][:, c * P:(c + 1) * P], KC, s_x2T)
                if step == "nat":
                    pe.wait_ge(s_k2h, 2 * b + 2)
                    pe.wait_ge(s_qmh, 4 * b + 4)
                    for u in range(4):
                        c, rows64 = u // 2, slice(64 * (u % 2), 64 * (u % 2) + 64)
                        if u == 0 and past(b, 3):
                            pe.wait_ge(s_x2Tl, b - 2)
                        if u == 1 and past(b, 1):
                            pe.wait_ge(s_exh, 4 * b)
                        if u == 2:
                            pe.wait_ge(s_r1, b + 1)
                        if u == 3 and past(b, 1):
                            pe.wait_ge(s_mT, b)
                        for j in range(4):
                            last = pe.matmul(bank[NAT_BANK[u]][:, j * P:(j + 1) * P], QMh[p][rows64, c, j, :],
                                             K2h[p][rows64, c, :], start=True, stop=True)
                        last.then_inc(s_nat, 1)
                if step[:-1] == "sc":
                    u = int(step[-1])
                    c, rows64 = u // 2, slice(64 * (u % 2), 64 * (u % 2) + 64)
                    pe.wait_ge(s_mT, b + 1)
                    pe.wait_ge(s_k2l, 2 * b + 2)
                    pe.wait_ge(s_qml, 4 * b + 4)
                    if u == 0 and past(b, 1):
                        pe.wait_ge(s_o2, b)
                    if u == 1:
                        pe.wait_ge(s_v2, b + 1)
                        pe.wait_ge(s_qv_sb, upto(b + 2))
                    if u == 2:
                        pe.wait_ge(s_st, 2 * upto(b + 2))
                    if u == 3 and past(b, 1):
                        pe.wait_ge(s_o2Tl, b)
                    dst = bank[SC_BANK[u]]
                    for j in range(4):
                        pe.matmul(dst[:, j * P:(j + 1) * P], pick[rows64, 4 * c + j, :], MT[p][rows64, :],
                                  start=(j == 0), stop=False)
                    for k, q in ((K2h, QMh), (K2h, QMl), (K2l, QMh)):
                        last = pe.matmul(dst[:, :], k[p][rows64, c, :],
                                         q[p][rows64, c, :, :].rearrange("p j t -> p (j t)"),
                                         start=False, stop=(k is K2l))
                    last.then_inc(s_sc, 1)
            pipeline(pe, "xT/0 q2/1 qv/0 kk/0 nat/1 pv/2 qk/0 st/0 mT/1 ao2/3 o/0 sc0/1 sc1/1 sc2/1 o2T/2 onT/0 "
                         "cT/0 ao/0 k2/0 v2/0 sc3/1 x2T/3 x1T/0", emit)

            pe.wait_ge(s_x2Tl, NB)
            pe.wait_ge(s_o2, NB)
            for g in range(4):
                cols = slice(512 * g, 512 * g + 512)
                split3(pe, bank[g][0:G, :], lambda c: wg1h[:, c, :], lambda c: wg1l[:, c, :],
                       lambda c: X2Th[:, c, cols], lambda c: X2Tl[:, c, cols]).then_inc(s_g_ps, 1)
            for b in range(NB):
                if b % 4 == 0:
                    pe.wait_ge(s_gg, b // 4 + 1)
                last = pe.matmul(bank[4][:, b * NE:(b + 1) * NE], GG[:, b * P:(b + 1) * P], wg2_f[:],
                                 start=True, stop=True)
            last.then_inc(s_l_ps, 1)

            def up(e, q, g, n):
                pe.wait_ge(s_ewl, 8 * (e + 1))
                cols = slice(GW * g, GW * g + GW)
                wi_h = EWH[q][:, 0:1024].rearrange("p (k h) -> p k h", k=KC)
                wi_l = EWL[q][:, 0:1024].rearrange("p (k h) -> p k h", k=KC)
                for h in range(HC):
                    if not isinstance(n, int) or n > 0:
                        pe.wait_ge(s_hf, 4 * (n - 1) + h + 1)
                    split3(pe, bank[h][:, :],
                           lambda c: wi_h[:, c, h * P:(h + 1) * P], lambda c: wi_l[:, c, h * P:(h + 1) * P],
                           lambda c: X2Th[:, c, cols], lambda c: X2Tl[:, c, cols]).then_inc(s_up, 1)

            def down(e, q, g, n):
                wo_h = EWH[q][:, 1024:2048].rearrange("p (k d) -> p k d", k=HC)
                wo_l = EWL[q][:, 1024:2048].rearrange("p (k d) -> p k d", k=HC)
                pe.wait_ge(s_hl, 4 * (n + 1))
                for t in range(GT):
                    if isinstance(n, int) and n == 0:
                        pe.wait_ge(s_lsb, 2)
                    else:
                        pe.wait_ge(s_acc, 4 * (n - 1) + t + 1)
                    split3(pe, bank[4 + t][:, 0:D],
                           lambda c: HH[g % 2][:, c, t * P:(t + 1) * P], lambda c: HL[g % 2][:, c, t * P:(t + 1) * P],
                           lambda c: wo_h[:, c, :], lambda c: wo_l[:, c, :], HC).then_inc(s_dn, 1)

            def step(e, q, g):
                n = 4 * e + g
                up(e, q, g, n)
                if not isinstance(n, int) or n > 0:
                    if g:
                        down(e, q, g - 1, n - 1)
                    else:
                        down(e - 1, 1 - q, 3, n - 1)
            for q in range(2):
                for g in range(4):
                    step(q, q, g)
            with pe.Fori(1, NE // 2) as i:
                for q in range(2):
                    for g in range(4):
                        step(2 * i + q, q, g)
            down(NE - 1, 1, 3, 4 * NE - 1)


def kernel(**inputs):
    import concourse.bacc as bacc
    from concourse.bass_utils import run_bass_kernel_spmd

    a = {k: np.asarray(v) for k, v in inputs.items()}

    def chunked(m):
        return m.reshape(-1, P, m.shape[-1]).transpose(1, 0, 2)

    order = ["attn_Wq", "attn_Wv", "attn_Wk", "attn_Wo", "xattn_Wq", "xattn_Wk", "xattn_Wv", "xattn_Wo"]
    wpack = chunked(np.concatenate([a["L0_" + n].T for n in order], axis=1))
    rows = np.concatenate([a["L0_" + n] for n in ("attn_bq", "attn_bv", "attn_bo", "xattn_bv", "xattn_bo")])
    vecs = np.concatenate([a["L0_" + n].reshape(KC, P).T
                           for n in ("attn_bk", "xattn_bk", "xattn_bq", "attn_ln_g", "attn_ln_b")], axis=1)
    arrays = {
        "x": a["x"],
        "ctx": a["ctx_1024"],
        "wpack": wpack,
        "rows": rows,
        "vecs": vecs,
        "wg1": chunked(a["L0_ffn_wg1"]),
        "bg1": a["L0_ffn_bg1"].reshape(G, 1),
        "wg2": a["L0_ffn_wg2"],
        "w_in": a["L0_ffn_w_in"].reshape(NE, KC, P, HID).transpose(0, 2, 1, 3),
        "w_out": a["L0_ffn_w_out"].reshape(NE, HC, P, D).transpose(0, 2, 1, 3),
    }
    arrays = {k: np.ascontiguousarray(v) for k, v in arrays.items()}
    nc = bacc.Bacc("TRN2", target_bir_lowering=False, num_devices=1)
    args = [nc.dram_tensor(k, v.shape, mybir.dt.from_np(v.dtype), kind="ExternalInput").ap()
            for k, v in arrays.items()]
    out = nc.dram_tensor("out", (NB, S, D), f32, kind="ExternalOutput").ap()
    decoder_layer(nc, *args, out)
    r = run_bass_kernel_spmd(nc, [arrays], core_ids=[0])
    return r.results[0]["out"]
```

```python
from contextlib import ExitStack

import numpy as np
import concourse.bass as bass
from concourse import mybir

f32 = mybir.dt.float32
f16 = mybir.dt.float16
bf16 = mybir.dt.bfloat16
ACT = mybir.ActivationFunctionType
ALU = mybir.AluOpType
AX = mybir.AxisListType

NB, S, D = 16, 128, 256
NH, DH = 16, 16
NE, HID, G = 8, 512, 64
P = 128
KC = D // P
HC = HID // P
WSCALE = 256.0
PSCALE = 64.0
EPS = 1e-5
GT = 4
HALVES = 2
TW = HALVES * P
MAXT = (2 * NB * S + NE * (TW - 1)) // TW
TR = 4
MAXI = -(-MAXT // TR)
MAXC = MAXI * TR * HALVES
SPARE = TW
MAGIC = 1.5 * 2 ** 23
CQV, CK, CO, CQ2, CK2, CV2, CO2 = 0, 512, 768, 1024, 1280, 1536, 1792
NPW = 2048
RQV, RO, RV2, RO2, NROW = 0, 512, 768, 1024, 1280
VK, VK2, VQ2, VG, VB, NVEC = 0, 2, 4, 6, 8, 10


def decoder_layer(nc, x, ctx, wpack, rows, vecs, wg1, bg1, wg2, w_in, w_out, out):
    x2d = nc.dram_tensor("x2d", (NB * S + SPARE, D), f32).ap()
    tokens = nc.dram_tensor("tokens", (NB * S + SPARE, D), f32).ap()
    es = ExitStack()
    with es:
        def sb(name, shape, dt=f32):
            return es.enter_context(nc.sbuf_tensor(name, shape, dt))

        def pair(name, shape, dt=f32):
            return [sb(f"{name}{i}", shape, dt) for i in range(2)]

        def sem(name):
            return es.enter_context(nc.semaphore(name))

        ident = sb("ident", [P, P])
        identb = sb("identb", [P, P], bf16)
        blockmask = sb("blockmask", [P, P])
        mask4 = sb("mask4", [P, 4])
        pick = sb("pick", [P, 8, P], bf16)
        neghalf = sb("neghalf", [P, NB])
        rowb = sb("rowb", [P, NROW])
        vec = sb("vec", [P, NVEC])
        bq2s = sb("bq2s", [P, KC])
        bk2s = sb("bk2s", [P, KC])
        lnb_rep = sb("lnb_rep", [P, KC, P])
        stage = sb("stage", [P, KC, NPW])
        wh = sb("wh", [P, KC, NPW], f16)
        wl = sb("wl", [P, KC, NPW], f16)
        X = pair("X", [P, D])
        C = pair("C", [P, D])
        XTh = pair("XTh", [P, KC, P], f16)
        XTl = pair("XTl", [P, KC, P], f16)
        QV = pair("QV", [P, 2 * D])
        qmax = pair("qmax", [P, NH])
        QS = pair("QS", [P, D])
        QE = pair("QE", [P, D])
        kmax = pair("kmax", [P, KC])
        knb = pair("knb", [P, KC])
        KE = pair("KE", [P, KC, P])
        ksum = pair("ksum", [P, KC])
        krec = pair("krec", [P, KC])
        QKT = pair("QKT", [P, 2 * KC, P])
        ST = pair("ST", [P, KC, P + 8])
        qrec = pair("qrec", [P, NH])
        ON = pair("ON", [P, D])
        OL = pair("OL", [P, D])
        OTh = pair("OTh", [P, KC, P], f16)
        OTl = pair("OTl", [P, KC, P], f16)
        XB = pair("XB", [P, D])
        bst = [pair(f"bst{n}_", [P, 6]) for n in range(3)]
        mv = [pair(f"mv{n}_", [P, 2]) for n in range(3)]
        nmu = [pair(f"nmu{n}_", [P, 1]) for n in range(3)]
        veps = [pair(f"veps{n}_", [P, 1]) for n in range(3)]
        rstd = [pair(f"rstd{n}_", [P, 1]) for n in range(3)]
        CTh = pair("CTh", [P, KC, P], f16)
        CTl = pair("CTl", [P, KC, P], f16)
        R1 = pair("R1", [P, D])
        X1 = pair("X1", [P, D])
        X1Th = pair("X1Th", [P, KC, P], f16)
        X1Tl = pair("X1Tl", [P, KC, P], f16)
        K2h = pair("K2h", [P, KC, P], f16)
        K2l = pair("K2l", [P, KC, P], f16)
        Q2h = pair("Q2h", [P, KC, P], f16)
        Q2l = pair("Q2l", [P, KC, P], f16)
        EW = sb("EW", [P, NE, 2, 2048], f16)
        QMh = [EW[:, 5, 0, 1024 * p:1024 * p + 1024].rearrange("q (c j t) -> q c j t", c=KC, j=4) for p in range(2)]
        QMl = [EW[:, 5, 1, 1024 * p:1024 * p + 1024].rearrange("q (c j t) -> q c j t", c=KC, j=4) for p in range(2)]
        V2 = pair("V2", [P, NH, DH + 1])
        V2h = pair("V2h", [P, NH, DH + 1], f16)
        V2l = pair("V2l", [P, NH, DH + 1], f16)
        NM = pair("NM", [P, 2, 64], bf16)
        MT = pair("MT", [P, P], bf16)
        EX = pair("EX", [P, 4, P])
        EXh = [EW[:, 6, p, :].rearrange("q (u j t) -> q u j t", u=4, j=4) for p in range(2)]
        EXl = [EW[:, 7, p, :].rearrange("q (u j t) -> q u j t", u=4, j=4) for p in range(2)]
        r2 = pair("r2", [P, NH])
        O2 = pair("O2", [P, D])
        O2Th = pair("O2Th", [P, KC, P], f16)
        O2Tl = pair("O2Tl", [P, KC, P], f16)
        R2 = pair("R2", [P, D])
        X2 = pair("X2", [P, D])
        rows_all = sb("rows_all", [P, NB, D])
        X2Th = pair("X2Th", [P, KC, P], f16)
        X2Tl = pair("X2Tl", [P, KC, P], f16)
        x_v = x.rearrange("(i p) s d -> i p s d", p=2)
        ctx_v = ctx.rearrange("(i p) s d -> i p s d", p=2)
        rows_v = rows_all[:].rearrange("q (i p) d -> q i p d", p=2)
        tokens_v = tokens[0:NB * S].rearrange("(i p s) d -> i p s d", p=2, s=S)
        x2d_v = x2d[0:NB * S].rearrange("(i p s) d -> i p s d", p=2, s=S)
        wg1_f = sb("wg1_f", [P, KC, G])
        wg1h = sb("wg1h", [P, KC, G], f16)
        wg1l = sb("wg1l", [P, KC, G], f16)
        bg1_c = sb("bg1_c", [G, 1])
        wg2_f = sb("wg2_f", [G, NE])
        scratch = stage[:, :, :].rearrange("p k n -> p (k n)")
        GG = scratch[0:G, 0:NB * P]
        GG_v = GG.rearrange("g (i p t) -> g i p t", p=2, t=P)
        L = sb("L", [P, NB, NE])
        lmax = sb("lmax", [P, NB])
        LE = sb("LE", [P, NB, NE])
        lsum = sb("lsum", [P, NB])
        lrec = sb("lrec", [P, NB])
        PR = sb("PR", [P, NB, NE])
        lower = sb("lower", [P, NE, NE])
        number = sb("number", [P, NB], mybir.dt.int32)
        number_f = sb("number_f", [P, NB])
        along_i = sb("along_i", [P, P], mybir.dt.int32)
        along = sb("along", [P, P])
        spare_i = sb("spare_i", [P, MAXI * TR, HALVES], mybir.dt.int32)
        spare_f = sb("spare_f", [P, MAXC])
        down8 = sb("down8", [P, NE])
        down8_i = sb("down8_i", [P, NE], mybir.dt.int32)
        before = sb("before", [P, P], f16)
        ones = sb("ones", [P, P], f16)
        blank = sb("blank", [P, HALVES, D])
        top = sb("top", [P, 2, NB])
        rest = sb("rest", [P, NB, NE])
        score = sb("score", [P, NB, NE])
        best = sb("best", [P, NB])
        sel = sb("sel", [P, 2, NB, NE])
        selh = sb("selh", [P, NB + 1, NE], f16)
        counts = sb("counts", [P, NE])
        over = sb("over", [P, NE, NB])
        ntile = sb("ntile", [P, NE])
        ahead = sb("ahead", [P, NE, NE])
        start = sb("start", [P, NE])
        end = sb("end", [P, NE])
        SL = sb("SL", [P, NB, NE])
        spick = sb("spick", [P, 2, NB, NE])
        slot_f = sb("slot_f", [P, 2, NB])
        column = sb("column", [P, 2, NB])
        place_in = sb("place_in", [P, 2, NB])
        odd_col = sb("odd_col", [P, 2, NB])
        shift = sb("shift", [P, 2, NB])
        table = sb("table", [P, MAXC])
        home = sb("home", [P, MAXC], mybir.dt.int32)
        gate = sb("gate", [P, MAXC])
        passed = sb("passed", [P, MAXI * TR, NE])
        texp_f = sb("texp_f", [P, MAXI * TR])
        texp = sb("texp", [P, MAXI * TR], mybir.dt.int32)
        EW_v = EW[:].rearrange("q e l (p n) -> q e l p n", p=2)
        EWF = [scratch[:, 2048 + 1024 * p:3072 + 1024 * p] for p in range(2)]
        TX = [sb(f"TX{k}", [P, HALVES, D]) for k in range(TR)]
        TXh = [t[:].bitcast(f16).rearrange("p (c t) -> p c t", c=KC) for t in (QS[0], QS[1])]
        TXl = [t[:].bitcast(f16).rearrange("p (c t) -> p c t", c=KC) for t in (XB[0], XB[1])]
        HF = [scratch[:, 1024 * k:1024 * k + 1024].rearrange("p (h t) -> p h t", h=HC) for k in range(2)]
        HH = [t[:].bitcast(f16).rearrange("p (h t) -> p h t", h=HC) for t in QV]
        HL = [t[:].rearrange("p j t -> p (j t)").bitcast(f16).rearrange("p (h t) -> p h t", h=HC) for t in EX]
        Y = [t[:].rearrange("p c t -> p (c t)").rearrange("p (f d) -> p f d", f=HALVES) for t in QKT]
        HOT = [t[:].rearrange("p k n -> p (k n)").bitcast(f32).rearrange("p (b t) -> p b t", b=NB) for t in (wh, wl)]
        COLS = rows_all[:].rearrange("p b d -> p (b d)")[:, 0:2 * NB * 2 * MAXC]\
            .rearrange("p (k b v c) -> p k b v c", k=2, b=NB, v=2)
        HOTC = scratch[:, 0:2 * NB * MAXC].rearrange("p (k b c) -> p k b c", k=2, b=NB)
        from_rows = [sb(f"from_rows{k}", [P, HALVES], mybir.dt.int32) for k in range(TR)]
        to_rows = [sb(f"to_rows{k}", [P, HALVES], mybir.dt.int32) for k in range(TR)]
        home_v = home[:].rearrange("q (i k f) -> q i k f", k=TR, f=HALVES)
        gate_v = gate[:].rearrange("q (i k f) -> q i k f", k=TR, f=HALVES)
        texp_v = texp[0:1, :].rearrange("q (i k) -> q i k", k=TR)
        fst = sb("fst", [P, NB, 6])
        fmv = sb("fmv", [P, NB, 2])
        fnm = sb("fnm", [P, NB])
        fve = sb("fve", [P, NB])
        frs = sb("frs", [P, NB])

        bank = [es.enter_context(nc.psum_tensor(f"bank{i}", [P, 512], f32)) for i in range(8)]

        def chunks(t, n, w=P):
            return t[:, 0:n * w].rearrange("p (c w) -> p c w", c=n)

        s_w_ld = [sem(f"s_w_ld{q}") for q in range(4)]
        s_rows_ld, s_vec_ld, s_g_ld = sem("s_rows_ld"), sem("s_vec_ld"), sem("s_g_ld")
        s_cst, s_cstb = sem("s_cst"), sem("s_cstb")
        s_prep = sem("s_prep")
        s_lnb, s_bo_ps = sem("s_lnb"), sem("s_bo_ps")
        s_bo_fold, s_wo_fold = sem("s_bo_fold"), sem("s_wo_fold")
        s_wsp_h, s_wsp_l = sem("s_wsp_h"), sem("s_wsp_l")
        s_xld = [sem(f"s_xld{p}") for p in range(2)]
        s_cld = [sem(f"s_cld{p}") for p in range(2)]
        s_xT, s_xTh, s_xTl, s_xb = sem("s_xT"), sem("s_xTh"), sem("s_xTl"), sem("s_xb")
        s_qv_ps, s_k_ps, s_qv_sb, s_qmax = sem("s_qv_ps"), sem("s_k_ps"), sem("s_qv_sb"), sem("s_qmax")
        s_km, s_knb, s_ke, s_qs = sem("s_km"), sem("s_knb"), sem("s_ke"), sem("s_qs")
        s_qe, s_krec, s_qk_ps, s_qkT = sem("s_qe"), sem("s_krec"), sem("s_qk_ps"), sem("s_qkT")
        s_st_ps, s_st, s_o_ps, s_qrec = sem("s_st_ps"), sem("s_st"), sem("s_o_ps"), sem("s_qrec")
        s_on, s_ln0, s_onT, s_onTh = sem("s_on"), sem("s_ln0"), sem("s_onT"), sem("s_onTh")
        s_onTl = sem("s_onTl")
        s_bs = [sem(f"s_bs{n}") for n in range(3)]
        s_mv = [sem(f"s_mv{n}") for n in range(3)]
        s_nm = [sem(f"s_nm{n}") for n in range(3)]
        s_ve = [sem(f"s_ve{n}") for n in range(3)]
        s_rs = [sem(f"s_rs{n}") for n in range(3)]
        s_ao_ps, s_r1, s_x1, s_x1b = sem("s_ao_ps"), sem("s_r1"), sem("s_x1"), sem("s_x1b")
        s_cT, s_cTh, s_cTl, s_x1T = sem("s_cT"), sem("s_cTh"), sem("s_cTl"), sem("s_x1T")
        s_x1Th, s_x1Tl, s_k2_ps, s_k2h = sem("s_x1Th"), sem("s_x1Tl"), sem("s_k2_ps"), sem("s_k2h")
        s_q2_ps, s_q2h, s_v2_ps, s_v2 = sem("s_q2_ps"), sem("s_q2h"), sem("s_v2_ps"), sem("s_v2")
        s_k2l, s_q2l, s_qmh, s_qml = sem("s_k2l"), sem("s_q2l"), sem("s_qmh"), sem("s_qml")
        s_nat, s_mx, s_mT_ps, s_mT = sem("s_nat"), sem("s_mx"), sem("s_mT_ps"), sem("s_mT")
        s_sc, s_ex, s_exh, s_exl = sem("s_sc"), sem("s_ex"), sem("s_exh"), sem("s_exl")
        s_v2h, s_v2l, s_pv, s_r2 = sem("s_v2h"), sem("s_v2l"), sem("s_pv"), sem("s_r2")
        s_o2, s_o2T, s_o2Th, s_o2Tl = sem("s_o2"), sem("s_o2T"), sem("s_o2Th"), sem("s_o2Tl")
        s_ao2, s_r2x, s_x2, s_x2T = sem("s_ao2"), sem("s_r2x"), sem("s_x2"), sem("s_x2T")
        s_x2Th, s_x2Tl = sem("s_x2Th"), sem("s_x2Tl")
        s_x2st = [sem(f"s_x2st{p}") for p in range(2)]
        s_gg, s_l_ps, s_lsb = sem("s_gg"), sem("s_l_ps"), sem("s_lsb")
        s_gh, s_gcp = sem("s_gh"), sem("s_gcp")
        s_ewld = [sem(f"s_ewld{q}") for q in range(2)]
        s_tok = [sem(f"s_tok{q}") for q in range(2)]
        s_cnt_sel = sem("s_cnt_sel")
        s_spare, s_cnt_ps, s_slot = sem("s_spare"), sem("s_cnt_ps"), sem("s_slot")
        s_from, s_to = sem("s_from"), sem("s_to")
        s_hot, s_cols, s_tab_ps, s_table = sem("s_hot"), sem("s_cols"), sem("s_tab_ps"), sem("s_table")
        s_tld = [[sem(f"s_tld{k}{f}") for f in range(HALVES)] for k in range(TR)]
        s_tT, s_tTh, s_tTl = sem("s_tT"), sem("s_tTh"), sem("s_tTl")
        s_y, s_texp = sem("s_y"), sem("s_texp")
        s_yld4 = [sem(f"s_yld{g}") for g in range(NB // GT)]
        s_blank = sem("s_blank")
        s_ewh, s_ewl, s_up, s_hf = sem("s_ewh"), sem("s_ewl"), sem("s_up"), sem("s_hf")
        s_hh, s_hl, s_dn, s_accs = sem("s_hh"), sem("s_hl"), sem("s_dn"), [sem(f"s_acc{f}") for f in range(HALVES)]
        s_acc0, s_acc1 = s_accs
        s_fbs, s_fmv, s_fve, s_frs = sem("s_fbs"), sem("s_fmv"), sem("s_fve"), sem("s_frs")
        s_fy, s_outs = sem("s_fy"), sem("s_outs")

        SC_BANK, NAT_BANK = (6, 0, 1, 5), (4, 5, 3, 7)

        def past(row, back):
            return not isinstance(row, int) or row >= back

        def split3(pe, dst, a_h, a_l, b_h, b_l, n=KC):
            for c in range(n):
                for i, (a, b) in enumerate(((a_h, b_h), (a_h, b_l), (a_l, b_h))):
                    last = pe.matmul(dst, a(c), b(c), start=(c == 0 and i == 0), stop=(c == n - 1 and i == 2))
            return last

        def within(t):
            return not isinstance(t, int) or t < MAXT

        def upto(n):
            return min(n, NB) if isinstance(n, int) else n

        def pipeline(eng, order, emit):
            steps = [(word[:-2], int(word[-1])) for word in order.split()]

            def iteration(half, odd, live):
                for step, lag in steps:
                    if lag in live:
                        at = odd - lag
                        emit(step, 2 * half + at, at % 2, half + at // 2)

            def peeled(i):
                iteration(i // 2, i % 2, [lag for lag in range(5) if 0 <= i - lag < NB])
            for i in range(6):
                peeled(i)
            with eng.Fori(3, NB // 2) as half:
                for odd in range(2):
                    iteration(half, odd, range(5))
            for i in range(NB, NB + 4):
                peeled(i)

        block = es.enter_context(nc.Block())

        @block.sync
        def _(sp):
            sp.dma_start(vec[:], vecs).then_inc(s_vec_ld, 16)
            for q in range(4):
                sp.dma_start(stage[:, :, 512 * q:512 * q + 512], wpack[:, :, 512 * q:512 * q + 512])\
                  .then_inc(s_w_ld[q], 16)
                if q == 0:
                    sp.dma_start(rowb[:], rows.partition_broadcast(P)).then_inc(s_rows_ld, 16)
            sp.dma_start(wg1_f[:], wg1).then_inc(s_g_ld, 16)
            sp.dma_start(bg1_c[:], bg1).then_inc(s_g_ld, 16)
            sp.dma_start(wg2_f[:], wg2).then_inc(s_g_ld, 16)

            sp.wait_ge(s_blank, 2)
            for dst in (x2d, tokens):
                sp.dma_start(dst[NB * S:NB * S + SPARE, :].rearrange("(f s) d -> s f d", f=HALVES), blank[:])\
                  .then_inc(s_spare, 16)
            def expert_part(e, p, piece):
                if piece >= 2:
                    sp.wait_ge(s_ewl, piece - 1)
                sp.dma_start(EWF[p].rearrange("p (k n) -> p k n", k=(KC, HC)[p]), (w_in, w_out)[p][e])\
                  .then_inc(s_ewld[p], 16)

            def emit(step, b, p, half):
                if step == "load":
                    if past(b, 2):
                        sp.wait_ge(s_xb, b - 1)
                    if past(b, 2):
                        sp.wait_ge(s_xT, b - 1)
                    sp.dma_start(X[p][:], x_v[half, p]).then_inc(s_xld[p], 16)
                    if past(b, 2):
                        sp.wait_ge(s_cT, b - 1)
                    sp.dma_start(C[p][:], ctx_v[half, p]).then_inc(s_cld[p], 16)
                if step == "weights" and isinstance(b, int) and b in (2, 3):
                    sp.wait_ge(s_wsp_l, 4 * KC + 1)
                    expert_part(0, p, p)
                if step == "weights" and not isinstance(b, int):
                    sp.wait_ge(s_ewl, b - 5)
                    sp.dma_start(EWF[p].rearrange("p (k n) -> p k n", k=(KC, HC)[p]), (w_in, w_out)[p][half - 2])\
                      .then_inc(s_ewld[p], 16)
                if step == "keep":
                    sp.wait_ge(s_x2, b + 1)
                    sp.dma_start(tokens_v[half, p], X2[p][:]).then_inc(s_tok[p], 16)
                    sp.dma_start(x2d_v[half, p], X2[p][:]).then_inc(s_x2st[p], 16)
            pipeline(sp, "load/0 weights/0 keep/3", emit)
            for piece in range(12, 2 * NE):
                expert_part(piece // 2, piece % 2, piece)

            sp.wait_ge(s_acc0, 16 * MAXT)
            sp.wait_ge(s_acc1, 16 * MAXT)
            for g in range(NB // GT):
                sp.dma_start(rows_all[:, GT * g:GT * g + GT, :],
                             tokens[0:NB * S].rearrange("(b s) d -> s b d", s=S)[:, GT * g:GT * g + GT, :])\
                  .then_inc(s_yld4[g], 16)
            for g in range(NB // GT):
                sp.wait_ge(s_fy, GT * (g + 1))
                sp.dma_start(out.rearrange("b p d -> p b d")[:, GT * g:GT * g + GT, :],
                             rows_all[:, GT * g:GT * g + GT, :]).then_inc(s_outs, 16)
            sp.wait_ge(s_outs, 16 * (NB // GT))

        @block.gpsimd
        def _(pool):
            pool.memset(ident[:], 0.0).then_inc(s_cst, 1)
            pool.memset(identb[:], 0.0).then_inc(s_cst, 1)
            pool.memset(blockmask[:], 1.0).then_inc(s_cst, 1)
            pool.memset(pick[:], 0.0).then_inc(s_cst, 1)
            pool.memset(lower[:], 1.0).then_inc(s_cst, 1)
            pool.memset(neghalf[:], -0.5).then_inc(s_cst, 1)
            for p in range(2):
                pool.memset(NM[p][:], 0.0).then_inc(s_cst, 1)
                pool.memset(V2[p][:], 1.0).then_inc(s_cst, 1)
            pool.memset(before[:], 1.0).then_inc(s_cst, 1)
            pool.memset(ones[:], 1.0).then_inc(s_cst, 1)
            pool.memset(selh[:], 0.0).then_inc(s_blank, 1)
            pool.memset(blank[:], 0.0).then_inc(s_blank, 1)
            pool.iota(number[:], [[P, NB]], base=0, channel_multiplier=1).then_inc(s_cst, 1)
            pool.iota(along_i[:], [[1, P]], base=0, channel_multiplier=0).then_inc(s_cst, 1)
            pool.iota(spare_i[:], [[0, MAXI * TR], [P, HALVES]], base=NB * S, channel_multiplier=1).then_inc(s_cst, 1)
            pool.iota(down8_i[:], [[-1, NE]], base=NE, channel_multiplier=0).then_inc(s_cst, 1)
            pool.wait_ge(s_cst, 16)
            for t in (ident, identb):
                pool.affine_select(out=t[:], in_=t[:], compare_op=ALU.not_equal, fill=1.0, base=0,
                                   pattern=[[-1, P]], channel_multiplier=1).then_inc(s_cstb, 1)
            bm = blockmask[:].rearrange("p (g d) -> p g d", g=8)
            pool.affine_select(out=bm, in_=bm, compare_op=ALU.is_ge, fill=0.0, base=0,
                               pattern=[[-DH, 8], [0, DH]], channel_multiplier=1).then_inc(s_cstb, 1)
            pool.wait_ge(s_cstb, 3)
            pool.affine_select(out=bm, in_=bm, compare_op=ALU.is_ge, fill=0.0, base=DH - 1,
                               pattern=[[DH, 8], [0, DH]], channel_multiplier=-1).then_inc(s_cstb, 1)
            for q in range(2):
                pool.affine_select(out=pick[:], in_=pick[:], compare_op=ALU.not_equal, fill=1.0, base=-64 * q,
                                   pattern=[[-1, 8], [0, P]], channel_multiplier=1).then_inc(s_cstb, 1)
                pool.wait_ge(s_cstb, 5 + q)
            pool.affine_select(out=before[:], in_=before[:], compare_op=ALU.is_ge, fill=0.0, base=-1,
                               pattern=[[1, P]], channel_multiplier=-1).then_inc(s_cstb, 1)
            pool.affine_select(out=lower[:], in_=lower[:], compare_op=ALU.is_ge, fill=0.0, base=-1,
                               pattern=[[1, NE], [-1, NE]], channel_multiplier=0).then_inc(s_cstb, 1)

            def norm(n, p, b, src, dst, signal):
                pool.wait_ge(s_ve[n], b + 1)
                pool.tensor_tensor(rstd[n][p][:], veps[n][p][:], neghalf[:, 0:1], ALU.pow).then_inc(s_rs[n], 1)
                pool.wait_ge(s_cstb, 8)
                pool.wait_ge(s_nm[n], b + 1)
                pool.wait_ge(s_rs[n], b + 1)
                pool.tensor_scalar(dst, src, nmu[n][p][:], rstd[n][p][:], ALU.add, ALU.mult).then_inc(signal, 1)

            def emit(step, b, p, half):
                if step == "xb":
                    pool.wait_ge(s_bo_fold, 1)
                    pool.wait_ge(s_xld[p], 8 * b + 16 - 8 * p)
                    if past(b, 2):
                        pool.wait_ge(s_r1, b - 1)
                    pool.tensor_tensor(XB[p][:], X[p][:], rowb[:, RO:RO + D], ALU.add).then_inc(s_xb, 1)
                if step == "qs":
                    pool.wait_ge(s_qmax, b + 1)
                    if past(b, 2):
                        pool.wait_ge(s_qe, b - 1)
                    pool.tensor_tensor(QS[p][:].rearrange("p (h d) -> p h d", h=NH),
                                       QV[p][:, 0:D].rearrange("p (h d) -> p h d", h=NH),
                                       qmax[p][:].unsqueeze(2).to_broadcast([P, NH, DH]),
                                       ALU.subtract).then_inc(s_qs, 1)
                if step == "norm0":
                    if past(b, 2):
                        pool.wait_ge(s_onT, b - 1)
                    norm(0, p, b, ON[p][:], OL[p][:], s_ln0)
                if step == "norm1":
                    if past(b, 2):
                        pool.wait_ge(s_x1T, b - 1)
                    if past(b, 2):
                        pool.wait_ge(s_x1b, b - 1)
                    norm(1, p, b, R1[p][:], X1[p][:], s_x1)
                if step == "x1b":
                    pool.wait_ge(s_x1, b + 1)
                    pool.tensor_tensor(rows_v[:, half, p, :], X1[p][:], rowb[:, RO2:RO2 + D], ALU.add)\
                        .then_inc(s_x1b, 1)
                if step[:-1] == "exl":
                    u = int(step[-1])
                    pool.wait_ge(s_exh, 4 * b + u + 1)
                    if past(b, 2):
                        pool.wait_ge(s_pv, 4 * b - 7 + u)
                    pool.tensor_tensor(EXl[p][:, u, :, :], EX[u % 2][:], EXh[p][:, u, :, :], ALU.subtract)\
                        .then_inc(s_exl, 1)
                if step == "norm2":
                    if past(b, 2):
                        pool.wait_ge(s_x2T, b - 1)
                    if past(b, 2):
                        pool.wait_ge(s_x2st[p], 8 * b - 8 * p)
                    if past(b, 2):
                        pool.wait_ge(s_tok[p], 8 * b - 8 * p)
                    norm(2, p, b, R2[p][:], X2[p][:], s_x2)
            pipeline(pool, "xb/0 exl3/2 qs/0 norm0/0 exl0/1 norm2/3 exl1/1 norm1/0 x1b/0 exl2/1", emit)

            def gather(i, k):
                if past(i, 1):
                    pool.wait_ge(s_tT, TR * (i - 1) + k + 1)
                pool.tensor_copy(from_rows[k][:], home_v[:, i, k, :]).then_inc(s_from, 1)
                pool.wait_ge(s_from, TR * i + k + 1)
                for f in range(HALVES):
                    pool.nop(nofuse=True)
                    pool.indirect_dma_start(TX[k][:, f, :], None, x2d,
                                            bass.IndirectOffsetOnAxis(ap=from_rows[k][:, f:f + 1], axis=0))\
                        .then_inc(s_tld[k][f], 16)

            def add_up(i, k):
                t = TR * i + k
                pool.wait_ge(s_y, 2 * t + 2)
                if past(t, 1):
                    pool.wait_ge(s_acc0, 16 * t)
                if past(t, 1):
                    pool.wait_ge(s_acc1, 16 * t)
                pool.tensor_copy(to_rows[k % 2][:], home_v[:, i, k, :]).then_inc(s_to, 1)
                pool.wait_ge(s_to, t + 1)
                for f in range(HALVES):
                    pool.nop(nofuse=True)
                    pool.indirect_dma_start(tokens, bass.IndirectOffsetOnAxis(ap=to_rows[k % 2][:, f:f + 1], axis=0),
                                            Y[k % 2][:, f, :], None, compute_op=ALU.add).then_inc(s_accs[f], 16)
            pool.wait_ge(s_spare, 32)
            for p in range(2):
                pool.wait_ge(s_x2st[p], 8 * NB)
                pool.wait_ge(s_tok[p], 8 * NB)
            pool.wait_ge(s_table, 2)
            for k in range(TR):
                gather(0, k)

            def tiles(i):
                for k in range(TR):
                    gather(i + 1, k)
                    add_up(i, k)
            tiles(0)
            with pool.Fori(1, MAXI - 2) as i:
                tiles(i)
            for i in range(MAXI - 2, MAXI):
                for k in range(TR):
                    if TR * (i + 1) + k < MAXT:
                        gather(i + 1, k)
                    if TR * i + k < MAXT:
                        add_up(i, k)

            for g in range(NB // GT):
                pool.wait_ge(s_fve, g + 1)
                pool.tensor_tensor(frs[:, GT * g:GT * g + GT], fve[:, GT * g:GT * g + GT],
                                   neghalf[:, 0:GT], ALU.pow).then_inc(s_frs, 1)

        @block.scalar
        def _(act):
            for q in range(4):
                act.wait_ge(s_w_ld[q], 16)
                if q == 1:
                    act.wait_ge(s_wo_fold, KC)
                act.activation(wh[:, :, 512 * q:512 * q + 512], stage[:, :, 512 * q:512 * q + 512],
                               ACT.Copy, scale=PSCALE).then_inc(s_wsp_h, 1)

            def gate_hidden(g):
                act.wait_ge(s_gcp, 4 * g + 4)
                act.activation(GG[:, 512 * g:512 * g + 512], GG[:, 512 * g:512 * g + 512], ACT.Gelu,
                               bias=bg1_c[:], scale=1.0 / WSCALE).then_inc(s_gg, 1)

            def copy(dst, src, signal):
                act.activation(dst, src, ACT.Copy).then_inc(signal, 1)

            def emit(step, b, p, half):
                if step == "XTh":
                    act.wait_ge(s_xT, b + 1)
                    if past(b, 2):
                        act.wait_ge(s_k_ps, b - 1)
                    copy(XTh[p][:], chunks(bank[0], KC), s_xTh)
                if step == "ke":
                    act.wait_ge(s_knb, b + 1)
                    if past(b, 2):
                        act.wait_ge(s_qk_ps, b - 1)
                    for c in range(KC):
                        act.activation(KE[p][:, c, :], bank[2][:, c * P:(c + 1) * P], ACT.Exp,
                                       bias=knb[p][:, c:c + 1], scale=1.0 / PSCALE,
                                       accum_out=ksum[p][:, c:c + 1]).then_inc(s_ke, 1)
                if step == "qe":
                    act.wait_ge(s_qs, b + 1)
                    if past(b, 2):
                        act.wait_ge(s_qk_ps, b - 1)
                    act.activation(QE[p][:], QS[p][:], ACT.Exp).then_inc(s_qe, 1)
                if step == "qkT":
                    act.wait_ge(s_qk_ps, b + 1)
                    if past(b, 2):
                        act.wait_ge(s_o_ps, b - 1)
                    copy(QKT[p][:], chunks(bank[2], 2 * KC), s_qkT)
                if step == "OTh":
                    act.wait_ge(s_onT, b + 1)
                    if past(b, 2):
                        act.wait_ge(s_ao_ps, b - 1)
                    copy(OTh[p][:], chunks(bank[3], KC), s_onTh)
                if step == "CTh":
                    act.wait_ge(s_cT, b + 1)
                    if past(b, 2):
                        act.wait_ge(s_v2_ps, b - 1)
                    copy(CTh[p][:], chunks(bank[6], KC), s_cTh)
                if step == "X1Th":
                    act.wait_ge(s_x1T, b + 1)
                    if past(b, 2):
                        act.wait_ge(s_q2_ps, b - 1)
                    copy(X1Th[p][:], chunks(bank[2], KC), s_x1Th)
                if step == "MT":
                    act.wait_ge(s_mT_ps, b + 1)
                    if past(b, 2):
                        act.wait_ge(s_sc, 4 * b - 4)
                    copy(MT[p][:], bank[7][:, 0:P // 2].bitcast(bf16), s_mT)
                if step[:-1] == "ex":
                    u = int(step[-1])
                    act.wait_ge(s_sc, 4 * b + u + 1)
                    if past(4 * b + u, 2):
                        act.wait_ge(s_exl, 4 * b + u - 1)
                    act.activation(EX[u % 2][:], chunks(bank[SC_BANK[u]], 4), ACT.Exp,
                                   scale=DH ** -0.5 / PSCALE ** 2).then_inc(s_ex, 1)
                    if past(b, 2):
                        act.wait_ge(s_pv, 4 * b - 7 + u)
                    act.activation(EXh[p][:, u, :, :], chunks(bank[SC_BANK[u]], 4), ACT.Exp,
                                   scale=DH ** -0.5 / PSCALE ** 2).then_inc(s_exh, 1)
                if step == "k2h":
                    act.wait_ge(s_k2_ps, b + 1)
                    if past(b, 2):
                        act.wait_ge(s_sc, 4 * b - 4)
                    for c in range(KC):
                        act.activation(K2h[p][:, c, :], bank[6][:, c * P:(c + 1) * P], ACT.Identity,
                                       bias=bk2s[:, c:c + 1]).then_inc(s_k2h, 1)
                if step == "q2h":
                    act.wait_ge(s_q2_ps, b + 1)
                    if past(b, 2):
                        act.wait_ge(s_qmh, 4 * b - 4)
                    if past(b, 2):
                        act.wait_ge(s_q2l, 2 * b - 2)
                    for c in range(KC):
                        act.activation(Q2h[p][:, c, :], bank[1][:, c * P:(c + 1) * P], ACT.Identity,
                                       bias=bq2s[:, c:c + 1]).then_inc(s_q2h, 1)
                if step == "qml":
                    act.wait_ge(s_q2l, 2 * b + 2)
                    if past(b, 2):
                        act.wait_ge(s_sc, 4 * b - 4)
                    for j in range(4):
                        act.activation(QMl[p][:, :, j, :], Q2l[p][:], ACT.Copy, scale=mask4[:, j:j + 1])\
                           .then_inc(s_qml, 1)
                if step == "v2h":
                    act.wait_ge(s_v2, b + 1)
                    if past(b, 2):
                        act.wait_ge(s_pv, 4 * b - 4)
                    copy(V2h[p][:], V2[p][:], s_v2h)
                if step == "O2Th":
                    act.wait_ge(s_o2T, b + 1)
                    if past(b, 2):
                        act.wait_ge(s_ao2, b - 1)
                    copy(O2Th[p][:], chunks(bank[5], KC), s_o2Th)
                if step == "ewh" and not isinstance(b, int):
                    act.wait_ge(s_ewld[p], 8 * b - 32 - 8 * p)
                    act.activation(EW_v[:, half - 3, 0, p, :], EWF[p], ACT.Copy, scale=WSCALE).then_inc(s_ewh, 1)
                if step == "X2Th":
                    act.wait_ge(s_x2T, b + 1)
                    if past(b, 2):
                        act.wait_ge(s_gh, b - 1)
                    copy(X2Th[p][:], chunks(bank[4], KC), s_x2Th)
                    if isinstance(b, int) and b == NB - 2:
                        for g in range(3):
                            gate_hidden(g)
            pipeline(act, "ewh/0 XTh/0 q2h/1 ex3/2 ke/0 qe/0 qkT/0 qml/1 MT/1 ex0/1 O2Th/2 OTh/0 CTh/0 ex1/1 "
                          "k2h/0 ex2/1 v2h/0 X2Th/3 X1Th/0", emit)

            gate_hidden(3)
            act.wait_ge(s_lsb, 2)
            act.activation(LE[:], L[:], ACT.Exp).then_inc(s_lsb, 1)
            act.wait_ge(s_pv, 4 * NB)
            for piece in range(10, 2 * NE):
                e, p = piece // 2, piece % 2
                act.wait_ge(s_ewld[p], 16 * e + 16)
                act.activation(EW_v[:, e, 0, p, :], EWF[p], ACT.Copy, scale=WSCALE).then_inc(s_ewh, 1)

            def tile_high(t, k):
                act.wait_ge(s_tT, t + 1)
                if past(t, 2):
                    act.wait_ge(s_up, t - 1)
                copy(TXh[k % 2][:], bank[6 + k % 2][:, :].rearrange("p (c t) -> p c t", c=KC), s_tTh)

            def hidden(t, k):
                act.wait_ge(s_up, t + 1)
                if past(t, 2):
                    act.wait_ge(s_hl, 2 * (t - 1))
                for g in range(2):
                    act.activation(HF[k % 2][:, 2 * g:2 * g + 2, :],
                                   bank[2 * (k % 2) + g][:, :].rearrange("p (h t) -> p h t", h=2),
                                   ACT.Gelu, scale=1.0 / WSCALE).then_inc(s_hf, 1)

            def gated(i, k):
                t = TR * i + k
                act.wait_ge(s_dn, t + 1)
                if past(t, 2):
                    act.wait_ge(s_acc0, 16 * (t - 1))
                if past(t, 2):
                    act.wait_ge(s_acc1, 16 * (t - 1))
                for f in range(HALVES):
                    act.activation(Y[k % 2][:, f, :], bank[4 + k % 2][:, f * D:(f + 1) * D], ACT.Copy,
                                   scale=gate_v[:, i, k, f:f + 1]).then_inc(s_y, 1)
            act.wait_ge(s_table, 2)
            tile_high(0, 0)
            tile_high(1, 1)
            hidden(0, 0)

            def tiles(i, n=TR):
                for k in range(n):
                    if within(TR * i + k + 2):
                        tile_high(TR * i + k + 2, k + 2)
                    if within(TR * i + k + 1):
                        hidden(TR * i + k + 1, k + 1)
                    gated(i, k)
            tiles(0)
            with act.Fori(1, MAXI - 1) as i:
                tiles(i)
            tiles(MAXI - 1, MAXT - TR * (MAXI - 1))

        @block.vector
        def _(dve):
            chain = [0]

            def small(op):
                chain[0] += 1
                op.then_inc(s_prep, 1)
                dve.wait_ge(s_prep, chain[0])

            dve.wait_ge(s_vec_ld, 16)
            for c in range(KC):
                dve.tensor_copy(lnb_rep[:, c, :], vec[:, VB + c:VB + c + 1].to_broadcast([P, P]))\
                   .then_inc(s_lnb, 1)

            def weights_low(q):
                dve.wait_ge(s_wsp_h, q + 1)
                cols = slice(512 * q, 512 * q + 512)
                for c in range(KC):
                    dve.scalar_tensor_tensor(wl[:, c, cols], stage[:, c, cols], PSCALE, wh[:, c, cols],
                                             ALU.mult, ALU.subtract).then_inc(s_wsp_l, 1)
            weights_low(0)
            dve.wait_ge(s_bo_ps, 1)
            dve.wait_ge(s_rows_ld, 16)
            dve.tensor_tensor(rowb[:, RO:RO + D], bank[0][:, 0:D], rowb[:, RO:RO + D], ALU.add)\
               .then_inc(s_bo_fold, 1)
            for c in range(KC):
                dve.tensor_scalar(stage[:, c, CO:CO + D], stage[:, c, CO:CO + D], vec[:, VG + c:VG + c + 1],
                                  None, ALU.mult).then_inc(s_wo_fold, 1)
            dve.wait_ge(s_cstb, 8)
            small(dve.tensor_tensor(mask4[:], blockmask[:, 0:P // 2:DH], blockmask[:, P // 2:P:DH], ALU.add))
            for p in range(2):
                for c in range(KC):
                    small(dve.tensor_copy(ST[p][:, c, P:P + 8], blockmask[:, 0:P:DH]))
            small(dve.tensor_copy(number_f[:], number[:]))
            small(dve.tensor_copy(along[:], along_i[:]))
            small(dve.tensor_copy(spare_f[:], spare_i[:].rearrange("p t f -> p (t f)")))
            small(dve.tensor_copy(down8[:], down8_i[:]))
            small(dve.tensor_scalar(bq2s[:], vec[:, VQ2:VQ2 + KC], PSCALE, None, ALU.mult))
            small(dve.tensor_scalar(bk2s[:], vec[:, VK2:VK2 + KC], PSCALE, None, ALU.mult))
            for q in range(1, 4):
                weights_low(q)
            dve.wait_ge(s_g_ld, 48)
            small(dve.tensor_scalar(wg1h[:], wg1_f[:], WSCALE, None, ALU.mult))
            dve.scalar_tensor_tensor(wg1l[:], wg1_f[:], WSCALE, wg1h[:], ALU.mult, ALU.subtract)\
               .then_inc(s_wsp_l, 1)

            def low(dst, src, high, high_done, signal, row):
                dve.wait_ge(high_done, row + 1)
                dve.tensor_tensor(dst, src, high, ALU.subtract).then_inc(signal, 1)

            def stats(n, p, b, src, ready, parts=1):
                dve.wait_ge(ready, parts * b + parts)
                dve.bn_stats(bst[n][p][:], src).then_inc(s_bs[n], 1)
                dve.wait_ge(s_cstb, 8)
                dve.wait_ge(s_bs[n], b + 1)
                dve.bn_aggr(mv[n][p][:], bst[n][p][:]).then_inc(s_mv[n], 1)
                dve.wait_ge(s_mv[n], b + 1)
                if past(b, 2):
                    dve.wait_ge((s_ln0, s_x1, s_x2)[n], b - 1)
                dve.tensor_scalar(veps[n][p][:], mv[n][p][:, 1:2], EPS, None, ALU.add).then_inc(s_ve[n], 1)
                dve.tensor_scalar(nmu[n][p][:], mv[n][p][:, 0:1], -1.0, None, ALU.mult).then_inc(s_nm[n], 1)

            def emit(step, b, p, half):
                if step == "XTl":
                    low(XTl[p][:], chunks(bank[0], KC), XTh[p][:], s_xTh, s_xTl, b)
                if step == "qvsb":
                    dve.wait_ge(s_qv_ps, b + 1)
                    if past(b, 2):
                        dve.wait_ge(s_qs, b - 1)
                    if past(b, 2):
                        dve.wait_ge(s_st_ps, b - 1)
                    dve.scalar_tensor_tensor(QV[p][:], bank[0][:, :], 1.0 / PSCALE, rowb[:, RQV:RQV + 2 * D],
                                             ALU.mult, ALU.add).then_inc(s_qv_sb, 1)
                if step == "kmax":
                    dve.wait_ge(s_k_ps, b + 1)
                    dve.tensor_reduce(kmax[p][:], chunks(bank[2], KC), AX.X, ALU.max).then_inc(s_km, 1)
                    dve.wait_ge(s_km, 2 * b + 1)
                    dve.scalar_tensor_tensor(kmax[p][:], kmax[p][:], 1.0 / PSCALE, vec[:, VK:VK + KC],
                                             ALU.mult, ALU.add).then_inc(s_km, 1)
                    dve.wait_ge(s_km, 2 * b + 2)
                    if past(b, 2):
                        dve.wait_ge(s_ke, 2 * b - 2)
                    dve.tensor_tensor(knb[p][:], vec[:, VK:VK + KC], kmax[p][:], ALU.subtract).then_inc(s_knb, 1)
                if step == "qmax":
                    dve.wait_ge(s_qv_sb, b + 1)
                    dve.tensor_reduce(qmax[p][:], QV[p][:, 0:D].rearrange("p (h d) -> p h d", h=NH), AX.X,
                                      ALU.max).then_inc(s_qmax, 1)
                if step == "krec":
                    dve.wait_ge(s_ke, 2 * b + 2)
                    dve.reciprocal(krec[p][:], ksum[p][:]).then_inc(s_krec, 1)
                if step == "ST":
                    dve.wait_ge(s_st_ps, b + 1)
                    dve.wait_ge(s_krec, b + 1)
                    if past(b, 2):
                        dve.wait_ge(s_o_ps, b - 1)
                    for c in range(KC):
                        dve.scalar_tensor_tensor(ST[p][:, c, 0:P], bank[1][:, c * P:(c + 1) * P],
                                                 krec[p][:, c:c + 1], blockmask[:], ALU.mult, ALU.mult)\
                           .then_inc(s_st, 1)
                if step == "on":
                    dve.wait_ge(s_o_ps, b + 1)
                    o = chunks(bank[2], KC, P + 8)
                    dve.reciprocal(qrec[p][:].rearrange("p (c h) -> p c h", c=KC), o[:, :, P:P + 8])\
                       .then_inc(s_qrec, 1)
                    dve.wait_ge(s_qrec, b + 1)
                    if past(b, 2):
                        dve.wait_ge(s_ln0, b - 1)
                    for c in range(KC):
                        dve.tensor_tensor(ON[p][:, c * P:(c + 1) * P].rearrange("p (h d) -> p h d", d=DH),
                                          o[:, c, 0:P].rearrange("p (h d) -> p h d", d=DH),
                                          qrec[p][:, 8 * c:8 * c + 8].unsqueeze(2).to_broadcast([P, 8, DH]),
                                          ALU.mult).then_inc(s_on, 1)
                if step == "stats0":
                    stats(0, p, b, ON[p][:], s_on, 2)
                if step == "OTl":
                    low(OTl[p][:], chunks(bank[3], KC), OTh[p][:], s_onTh, s_onTl, b)
                if step == "CTl":
                    low(CTl[p][:], chunks(bank[6], KC), CTh[p][:], s_cTh, s_cTl, b)
                if step == "R1":
                    dve.wait_ge(s_ao_ps, b + 1)
                    dve.wait_ge(s_xb, b + 1)
                    if past(b, 2):
                        dve.wait_ge(s_x1, b - 1)
                    dve.scalar_tensor_tensor(R1[p][:], bank[3][:, 0:D], 1.0 / PSCALE, XB[p][:], ALU.mult, ALU.add)\
                       .then_inc(s_r1, 1)
                    stats(1, p, b, R1[p][:], s_r1)
                if step == "X1Tl":
                    low(X1Tl[p][:], chunks(bank[2], KC), X1Th[p][:], s_x1Th, s_x1Tl, b)
                if step == "v2sb":
                    dve.wait_ge(s_v2_ps, b + 1)
                    if past(b, 2):
                        dve.wait_ge(s_v2l, b - 1)
                    dve.scalar_tensor_tensor(V2[p][:, :, 0:DH], bank[0][:, 0:D].rearrange("p (h d) -> p h d", h=NH),
                                             1.0 / PSCALE, rowb[:, RV2:RV2 + D].rearrange("p (h d) -> p h d", h=NH),
                                             ALU.mult, ALU.add).then_inc(s_v2, 1)
                if step == "k2l":
                    if past(b, 2):
                        dve.wait_ge(s_sc, 4 * b - 4)
                    dve.wait_ge(s_k2h, 2 * b + 2)
                    for c in range(KC):
                        dve.scalar_tensor_tensor(K2l[p][:, c, :], bank[6][:, c * P:(c + 1) * P], bk2s[:, c:c + 1],
                                                 K2h[p][:, c, :], ALU.add, ALU.subtract).then_inc(s_k2l, 1)
                if step == "qmh":
                    dve.wait_ge(s_q2h, 2 * b + 2)
                    if past(b, 2):
                        dve.wait_ge(s_sc, 4 * b - 4)
                    for j in range(4):
                        dve.tensor_scalar(QMh[p][:, :, j, :], Q2h[p][:], mask4[:, j:j + 1], None, ALU.mult)\
                           .then_inc(s_qmh, 1)
                if step == "q2l":
                    dve.wait_ge(s_q2h, 2 * b + 2)
                    if past(b, 2):
                        dve.wait_ge(s_qml, 4 * b - 4)
                    for c in range(KC):
                        dve.scalar_tensor_tensor(Q2l[p][:, c, :], bank[1][:, c * P:(c + 1) * P], bq2s[:, c:c + 1],
                                                 Q2h[p][:, c, :], ALU.add, ALU.subtract).then_inc(s_q2l, 1)
                if step == "v2l":
                    dve.wait_ge(s_v2h, b + 1)
                    if past(b, 2):
                        dve.wait_ge(s_pv, 4 * b - 4)
                    dve.tensor_tensor(V2l[p][:], V2[p][:], V2h[p][:], ALU.subtract).then_inc(s_v2l, 1)
                if step == "mx":
                    if past(b, 2):
                        dve.wait_ge(s_mT_ps, b - 1)
                    for u in range(4):
                        dve.wait_ge(s_nat, 4 * b + u + 1)
                        dve.tensor_reduce(NM[p][:, u % 2, 4 * (u // 2):4 * (u // 2) + 4], chunks(bank[NAT_BANK[u]], 4), AX.X, ALU.max,
                                          negate=True).then_inc(s_mx, 1)
                if step == "o2":
                    dve.wait_ge(s_pv, 4 * b + 4)
                    pv = chunks(bank[6], NH, DH + 1)
                    dve.reciprocal(r2[p][:], pv[:, :, DH]).then_inc(s_r2, 1)
                    dve.wait_ge(s_r2, b + 1)
                    if past(b, 2):
                        dve.wait_ge(s_o2T, b - 1)
                    dve.tensor_tensor(O2[p][:].rearrange("p (h d) -> p h d", h=NH), pv[:, :, 0:DH],
                                      r2[p][:].unsqueeze(2).to_broadcast([P, NH, DH]), ALU.mult).then_inc(s_o2, 1)
                if step == "O2Tl":
                    low(O2Tl[p][:], chunks(bank[5], KC), O2Th[p][:], s_o2Th, s_o2Tl, b)
                if step == "R2":
                    dve.wait_ge(s_ao2, b + 1)
                    dve.wait_ge(s_x1b, b + 1)
                    if past(b, 2):
                        dve.wait_ge(s_x2, b - 1)
                    dve.scalar_tensor_tensor(R2[p][:], bank[3][:, 0:D], 1.0 / PSCALE, rows_v[:, half, p, :], ALU.mult, ALU.add)\
                       .then_inc(s_r2x, 1)
                    stats(2, p, b, R2[p][:], s_r2x)
                if step == "ewl" and not isinstance(b, int):
                    dve.wait_ge(s_ewh, b - 5)
                    dve.scalar_tensor_tensor(EW_v[:, half - 3, 1, p, :], EWF[p], WSCALE, EW_v[:, half - 3, 0, p, :],
                                             ALU.mult, ALU.subtract).then_inc(s_ewl, 1)
                if step == "X2Tl":
                    low(X2Tl[p][:], chunks(bank[4], KC), X2Th[p][:], s_x2Th, s_x2Tl, b)
                if step == "gcp":
                    dve.wait_ge(s_gh, b + 1)
                    dve.tensor_copy(GG_v[:, half, p, :], bank[4][0:G, 0:P]).then_inc(s_gcp, 1)
            pipeline(dve, "X1Tl/1 XTl/0 gcp/4 qmh/1 qvsb/0 kmax/0 qmax/0 q2l/1 mx/1 krec/0 o2/2 ST/0 ewl/0 "
                          "on/0 stats0/0 R2/3 OTl/0 O2Tl/2 CTl/0 R1/0 v2sb/0 k2l/0 v2l/0 X2Tl/3", emit)

            dve.wait_ge(s_l_ps, 4)
            logits = bank[0][:, 0:NB * NE].rearrange("p (b e) -> p b e", b=NB)
            dve.tensor_reduce(lmax[:], logits, AX.X, ALU.max).then_inc(s_lsb, 1)
            dve.wait_ge(s_lsb, 1)
            dve.tensor_tensor(L[:], logits, lmax[:].unsqueeze(2).to_broadcast([P, NB, NE]), ALU.subtract)\
               .then_inc(s_lsb, 1)
            dve.wait_ge(s_lsb, 3)
            small(dve.tensor_reduce(lsum[:], LE[:], AX.X, ALU.add))
            small(dve.reciprocal(lrec[:], lsum[:]))
            small(dve.tensor_tensor(PR[:], LE[:], lrec[:].unsqueeze(2).to_broadcast([P, NB, NE]), ALU.mult))
            for k, pr in enumerate((PR, rest)):
                small(dve.tensor_reduce(top[:, k, :], pr[:], AX.X, ALU.max))
                small(dve.tensor_tensor(score[:], pr[:], top[:, k, :].unsqueeze(2).to_broadcast([P, NB, NE]), ALU.is_equal))
                small(dve.tensor_tensor(score[:], score[:], down8[:].unsqueeze(1).to_broadcast([P, NB, NE]), ALU.mult))
                small(dve.tensor_reduce(best[:], score[:], AX.X, ALU.max))
                small(dve.tensor_tensor(sel[:, k, :, :], score[:], best[:].unsqueeze(2).to_broadcast([P, NB, NE]),
                                        ALU.is_equal))
                if k == 0:
                    small(dve.scalar_tensor_tensor(rest[:], sel[:, 0, :, :], -4.0, PR[:], ALU.mult, ALU.add))
            dve.tensor_tensor(selh[:, 0:NB, :], sel[:, 0, :, :], sel[:, 1, :, :], ALU.add).then_inc(s_cnt_sel, 1)
            dve.wait_ge(s_cnt_ps, 1)
            place = bank[5][:, 0:NB * NE].rearrange("p (b e) -> p b e", b=NB)
            small(dve.tensor_scalar(counts[:], bank[5][:, NB * NE:NB * NE + NE], 1.0 / TW, None, ALU.mult))
            small(dve.tensor_tensor(over[:], counts[:].unsqueeze(2).to_broadcast([P, NE, NB]),
                                    along[:, 0:NB].unsqueeze(1).to_broadcast([P, NE, NB]), ALU.is_gt))
            small(dve.tensor_reduce(ntile[:], over[:], AX.X, ALU.add))
            small(dve.tensor_tensor(ahead[:], lower[:], ntile[:].unsqueeze(1).to_broadcast([P, NE, NE]), ALU.mult))
            small(dve.tensor_reduce(start[:], ahead[:], AX.X, ALU.add))
            small(dve.scalar_tensor_tensor(SL[:], start[:].unsqueeze(1).to_broadcast([P, NB, NE]), float(TW), place,
                                           ALU.mult, ALU.add))
            for k in range(2):
                small(dve.tensor_tensor(spick[:, k, :, :], sel[:, k, :, :], SL[:], ALU.mult))
                small(dve.tensor_reduce(slot_f[:, k, :], spick[:, k, :, :], AX.X, ALU.add))
            small(dve.tensor_scalar(column[:], slot_f[:], 1.0 / P, -(P - 1) / 2 / P, ALU.mult, ALU.add))
            small(dve.tensor_scalar(column[:], column[:], MAGIC, None, ALU.add))
            small(dve.tensor_scalar(column[:], column[:], MAGIC, None, ALU.subtract))
            dve.scalar_tensor_tensor(place_in[:], column[:], -float(P), slot_f[:], ALU.mult, ALU.add).then_inc(s_slot, 1)
            small(dve.tensor_scalar(odd_col[:], column[:], 0.5, -0.25, ALU.mult, ALU.add))
            small(dve.tensor_scalar(odd_col[:], odd_col[:], MAGIC, None, ALU.add))
            small(dve.tensor_scalar(odd_col[:], odd_col[:], MAGIC, None, ALU.subtract))
            small(dve.scalar_tensor_tensor(odd_col[:], odd_col[:], -2.0, column[:], ALU.mult, ALU.add))
            dve.wait_ge(s_slot, 1)
            small(dve.scalar_tensor_tensor(shift[:], odd_col[:], -float(P), place_in[:], ALU.mult, ALU.subtract))
            small(dve.scalar_tensor_tensor(shift[:], shift[:], -float(NB * S),
                                           number_f[:].unsqueeze(1).to_broadcast([P, 2, NB]), ALU.add, ALU.add))
            small(dve.tensor_scalar(top[:], top[:], 1.0 / WSCALE, None, ALU.mult))
            dve.wait_ge(s_ao2, NB)
            dve.wait_ge(s_gg, 4)
            dve.wait_ge(s_l_ps, 4)
            for g in range(4):
                rows = slice(4 * g, 4 * g + 4)
                for k in range(2):
                    dve.tensor_tensor(HOT[k][:, rows, :], along[:].unsqueeze(1).to_broadcast([P, 4, P]),
                                      place_in[:, k, rows].unsqueeze(2).to_broadcast([P, 4, P]), ALU.is_equal)\
                       .then_inc(s_hot, 1)
                    small(dve.tensor_tensor(HOTC[:, k, rows, :],
                                            along[:, 0:MAXC].unsqueeze(1).to_broadcast([P, 4, MAXC]),
                                            column[:, k, rows].unsqueeze(2).to_broadcast([P, 4, MAXC]), ALU.is_equal))
                    for v, value in enumerate((shift, top)):
                        dve.tensor_tensor(COLS[:, k, rows, v, :], HOTC[:, k, rows, :],
                                          value[:, k, rows].unsqueeze(2).to_broadcast([P, 4, MAXC]), ALU.mult)\
                           .then_inc(s_cols, 1)
            dve.wait_ge(s_tab_ps, 1)
            small(dve.tensor_tensor(table[:], bank[6][:, 0:MAXC], spare_f[:], ALU.add))
            dve.tensor_copy(home[:], table[:]).then_inc(s_table, 1)
            dve.tensor_copy(gate[:], bank[6][:, MAXC:2 * MAXC]).then_inc(s_table, 1)
            small(dve.tensor_tensor(end[:], start[:], ntile[:], ALU.add))
            small(dve.tensor_tensor(passed[:], end[:].unsqueeze(1).to_broadcast([P, MAXI * TR, NE]),
                                    along[:, 0:MAXI * TR].unsqueeze(2).to_broadcast([P, MAXI * TR, NE]), ALU.is_le))
            small(dve.tensor_reduce(texp_f[:], passed[:], AX.X, ALU.add))
            small(dve.tensor_scalar(texp_f[:], texp_f[:], float(NE - 1), None, ALU.min))
            dve.tensor_copy(texp[:], texp_f[:]).then_inc(s_texp, 1)
            for piece in range(10, 2 * NE):
                e, p = piece // 2, piece % 2
                dve.wait_ge(s_ewh, piece + 1)
                dve.scalar_tensor_tensor(EW_v[:, e, 1, p, :], EWF[p], WSCALE, EW_v[:, e, 0, p, :],
                                         ALU.mult, ALU.subtract).then_inc(s_ewl, 1)

            def tile_low(t, k):
                dve.wait_ge(s_tTh, t + 1)
                if past(t, 2):
                    dve.wait_ge(s_up, t - 1)
                dve.tensor_tensor(TXl[k % 2][:], bank[6 + k % 2][:, :].rearrange("p (c t) -> p c t", c=KC),
                                  TXh[k % 2][:], ALU.subtract).then_inc(s_tTl, 1)

            def split_hidden(t, k):
                for g in range(2):
                    part = slice(2 * g, 2 * g + 2)
                    dve.wait_ge(s_cstb, 8)
                    dve.wait_ge(s_hf, 2 * t + g + 1)
                    if past(t, 2):
                        dve.wait_ge(s_dn, t - 1)
                    dve.tensor_copy(HH[k % 2][:, part, :], HF[k % 2][:, part, :]).then_inc(s_hh, 1)
                    dve.wait_ge(s_hh, 2 * t + g + 1)
                    dve.tensor_tensor(HL[k % 2][:, part, :], HF[k % 2][:, part, :], HH[k % 2][:, part, :], ALU.subtract)\
                       .then_inc(s_hl, 1)
            tile_low(0, 0)
            tile_low(1, 1)
            split_hidden(0, 0)

            def tiles(i, n=TR):
                for k in range(n):
                    if within(TR * i + k + 2):
                        tile_low(TR * i + k + 2, k + 2)
                    if within(TR * i + k + 1):
                        split_hidden(TR * i + k + 1, k + 1)
            tiles(0)
            with dve.Fori(1, MAXI - 1) as i:
                tiles(i)
            tiles(MAXI - 1, MAXT - TR * (MAXI - 1))

            for g in range(NB // GT):
                rows4 = range(GT * g, GT * g + GT)
                for b in rows4:
                    if b % GT == 0:
                        dve.wait_ge(s_yld4[g], 16)
                    dve.bn_stats(fst[:, b, :], rows_all[:, b, :]).then_inc(s_fbs, 1)
                for b in rows4:
                    dve.wait_ge(s_fbs, b + 1)
                    dve.bn_aggr(fmv[:, b, :], fst[:, b, :]).then_inc(s_fmv, 1)
                dve.wait_ge(s_fmv, GT * (g + 1))
                dve.tensor_scalar(fve[:, GT * g:GT * g + GT], fmv[:, GT * g:GT * g + GT, 1], EPS, None, ALU.add)\
                   .then_inc(s_fve, 1)
            for b in range(NB):
                if b % GT == 0:
                    dve.wait_ge(s_frs, b // GT + 1)
                dve.tensor_scalar(rows_all[:, b, :], rows_all[:, b, :], fmv[:, b, 0:1], frs[:, b:b + 1],
                                  ALU.subtract, ALU.mult).then_inc(s_fy, 1)

        @block.tensor
        def _(pe):
            pe.wait_ge(s_w_ld[1], 16)
            pe.wait_ge(s_lnb, KC)
            for c in range(KC):
                last = pe.matmul(bank[0][:, 0:D], lnb_rep[:, c, :], stage[:, c, CO:CO + D],
                                 start=(c == 0), stop=(c == KC - 1))
            last.then_inc(s_bo_ps, 1)
            pe.wait_ge(s_cstb, 8)
            pe.wait_ge(s_wsp_l, 4 * KC + 1)

            def w(t, col, width):
                return lambda c: t[:, c, col:col + width]

            def feature_major(dst, col, th, tl, signal):
                for f in range(KC):
                    last = split3(pe, dst[:, f * P:(f + 1) * P],
                                  w(wh, col + f * P, P), w(wl, col + f * P, P),
                                  lambda c: th[:, c, :], lambda c: tl[:, c, :])
                last.then_inc(signal, 1)

            def token_major(dst, col, width, th, tl, signal):
                split3(pe, dst, lambda c: th[:, c, :], lambda c: tl[:, c, :],
                       w(wh, col, width), w(wl, col, width)).then_inc(signal, 1)

            def turn(dst, src, n, signal):
                for c in range(n):
                    last = pe.transpose(dst[:, c * P:(c + 1) * P], src(c), ident[:])
                last.then_inc(signal, 1)

            def gate_logits(g):
                pe.wait_ge(s_exh, 4 * NB)
                pe.wait_ge(s_gg, g + 1)
                for b in range(4 * g, 4 * g + 4):
                    last = pe.matmul(bank[0][:, b * NE:(b + 1) * NE], GG[:, b * P:(b + 1) * P], wg2_f[:],
                                     start=True, stop=True)
                last.then_inc(s_l_ps, 1)

            def emit(step, b, p, half):
                if step == "xT":
                    pe.wait_ge(s_xld[p], 8 * b + 16 - 8 * p)
                    if past(b, 1):
                        pe.wait_ge(s_v2, b)
                    turn(bank[0], lambda c: X[p][:, c * P:(c + 1) * P], KC, s_xT)
                if step == "qv":
                    pe.wait_ge(s_xTl, b + 1)
                    token_major(bank[0][:, :], CQV, 2 * D, XTh[p], XTl[p], s_qv_ps)
                if step == "v2":
                    pe.wait_ge(s_cTl, b + 1)
                    pe.wait_ge(s_qv_sb, b + 1)
                    if past(b, 1):
                        pe.wait_ge(s_exh, 4 * b - 2)
                    token_major(bank[0][:, 0:D], CV2, D, CTh[p], CTl[p], s_v2_ps)
                if step == "kk":
                    pe.wait_ge(s_xTl, b + 1)
                    if past(b, 1):
                        pe.wait_ge(s_x1Tl, b)
                    feature_major(bank[2], CK, XTh[p], XTl[p], s_k_ps)
                if step == "qk":
                    pe.wait_ge(s_qe, b + 1)
                    pe.wait_ge(s_ke, 2 * b + 2)
                    for c in range(KC):
                        pe.transpose(bank[2][:, c * P:(c + 1) * P], QE[p][:, c * P:(c + 1) * P], ident[:])
                    turn(bank[2][:, D:2 * D], lambda c: KE[p][:, c, :], KC, s_qk_ps)
                if step == "o":
                    pe.wait_ge(s_qkT, b + 1)
                    pe.wait_ge(s_st, 2 * b + 2)
                    o = chunks(bank[2], KC, P + 8)
                    for c in range(KC):
                        last = pe.matmul(o[:, c, :], QKT[p][:, c, :], ST[p][:, c, :], start=True, stop=True)
                    last.then_inc(s_o_ps, 1)
                if step == "x1T":
                    pe.wait_ge(s_x1, b + 1)
                    pe.wait_ge(s_on, 2 * b + 2)
                    turn(bank[2], lambda c: X1[p][:, c * P:(c + 1) * P], KC, s_x1T)
                if step == "q2":
                    pe.wait_ge(s_x1Tl, b + 1)
                    pe.wait_ge(s_st, 2 * b + 2)
                    if past(b, 1):
                        pe.wait_ge(s_exh, 4 * b - 1)
                    feature_major(bank[1], CQ2, X1Th[p], X1Tl[p], s_q2_ps)
                if step == "st":
                    pe.wait_ge(s_qkT, b + 1)
                    if past(b, 1):
                        pe.wait_ge(s_q2l, 2 * b)
                    for c in range(KC):
                        last = pe.matmul(bank[1][:, c * P:(c + 1) * P], QKT[p][:, KC + c, :],
                                         QV[p][:, D + c * P:D + (c + 1) * P], start=True, stop=True)
                    last.then_inc(s_st_ps, 1)
                if step == "onT":
                    pe.wait_ge(s_ln0, b + 1)
                    if past(b, 3):
                        pe.wait_ge(s_r2x, b - 2)
                    elif past(b, 1):
                        pe.wait_ge(s_mx, 4 * b - 1)
                    turn(bank[3], lambda c: OL[p][:, c * P:(c + 1) * P], KC, s_onT)
                if step == "ao":
                    pe.wait_ge(s_onTl, b + 1)
                    token_major(bank[3][:, 0:D], CO, D, OTh[p], OTl[p], s_ao_ps)
                if step == "ao2":
                    pe.wait_ge(s_o2Tl, b + 1)
                    pe.wait_ge(s_mx, 4 * upto(b + 3) - 1)
                    token_major(bank[3][:, 0:D], CO2, D, O2Th[p], O2Tl[p], s_ao2)
                    if isinstance(b, int) and b == NB - 1:
                        for g in range(3):
                            gate_logits(g)
                if step == "cT":
                    pe.wait_ge(s_cld[p], 8 * b + 16 - 8 * p)
                    if past(b, 1):
                        pe.wait_ge(s_exh, 4 * b - 3)
                    turn(bank[6], lambda c: C[p][:, c * P:(c + 1) * P], KC, s_cT)
                if step == "k2":
                    pe.wait_ge(s_cTl, b + 1)
                    feature_major(bank[6], CK2, CTh[p], CTl[p], s_k2_ps)
                if step == "pv":
                    pe.wait_ge(s_v2l, b + 1)
                    pe.wait_ge(s_k2l, 2 * upto(b + 2))
                    for u in range(4):
                        pe.wait_ge(s_exl, 4 * b + u + 1)
                        for j in range(4):
                            h = 4 * u + j
                            last = split3(pe, bank[6][:, h * (DH + 1):(h + 1) * (DH + 1)],
                                          lambda c: EXh[p][:, u, j, :], lambda c: EXl[p][:, u, j, :],
                                          lambda c: V2h[p][:, h, :], lambda c: V2l[p][:, h, :], 1)
                        last.then_inc(s_pv, 1)
                if step == "mT":
                    pe.wait_ge(s_mx, 4 * b + 4)
                    pe.transpose(bank[7][:, 0:P // 2].bitcast(bf16), NM[p][:].rearrange("p s m -> p (s m)"),
                                 identb[:]).then_inc(s_mT_ps, 1)
                if step == "o2T":
                    pe.wait_ge(s_o2, b + 1)
                    pe.wait_ge(s_mx, 4 * upto(b + 2) - 2)
                    turn(bank[5], lambda c: O2[p][:, c * P:(c + 1) * P], KC, s_o2T)
                if step == "gh":
                    pe.wait_ge(s_x2Tl, b + 1)
                    split3(pe, bank[4][0:G, 0:P], lambda c: wg1h[:, c, :], lambda c: wg1l[:, c, :],
                           lambda c: X2Th[p][:, c, :], lambda c: X2Tl[p][:, c, :]).then_inc(s_gh, 1)
                if step == "x2T":
                    pe.wait_ge(s_x2, b + 1)
                    pe.wait_ge(s_mx, 4 * upto(b + 3) - 3)
                    if past(b, 1):
                        pe.wait_ge(s_gcp, b)
                    turn(bank[4], lambda c: X2[p][:, c * P:(c + 1) * P], KC, s_x2T)
                if step == "nat":
                    pe.wait_ge(s_k2h, 2 * b + 2)
                    pe.wait_ge(s_qmh, 4 * b + 4)
                    for u in range(4):
                        c, rows64 = u // 2, slice(64 * (u % 2), 64 * (u % 2) + 64)
                        if u == 0 and past(b, 3):
                            pe.wait_ge(s_gcp, b - 2)
                        if u == 1 and past(b, 1):
                            pe.wait_ge(s_exh, 4 * b)
                        if u == 2:
                            pe.wait_ge(s_r1, b + 1)
                        if u == 3 and past(b, 1):
                            pe.wait_ge(s_mT, b)
                        for j in range(4):
                            last = pe.matmul(bank[NAT_BANK[u]][:, j * P:(j + 1) * P], QMh[p][rows64, c, j, :],
                                             K2h[p][rows64, c, :], start=True, stop=True)
                        last.then_inc(s_nat, 1)
                if step[:-1] == "sc":
                    u = int(step[-1])
                    c, rows64 = u // 2, slice(64 * (u % 2), 64 * (u % 2) + 64)
                    pe.wait_ge(s_mT, b + 1)
                    pe.wait_ge(s_k2l, 2 * b + 2)
                    pe.wait_ge(s_qml, 4 * b + 4)
                    if u == 0 and past(b, 1):
                        pe.wait_ge(s_o2, b)
                    if u == 1:
                        pe.wait_ge(s_v2, b + 1)
                        pe.wait_ge(s_qv_sb, upto(b + 2))
                    if u == 2:
                        pe.wait_ge(s_st, 2 * upto(b + 2))
                    if u == 3 and past(b, 1):
                        pe.wait_ge(s_o2Tl, b)
                    dst = bank[SC_BANK[u]]
                    for j in range(4):
                        pe.matmul(dst[:, j * P:(j + 1) * P], pick[rows64, 4 * c + j, :], MT[p][rows64, :],
                                  start=(j == 0), stop=False)
                    for k, q in ((K2h, QMh), (K2h, QMl), (K2l, QMh)):
                        last = pe.matmul(dst[:, :], k[p][rows64, c, :],
                                         q[p][rows64, c, :, :].rearrange("p j t -> p (j t)"),
                                         start=False, stop=(k is K2l))
                    last.then_inc(s_sc, 1)
            pipeline(pe, "gh/4 xT/0 q2/1 qv/0 kk/0 nat/1 pv/2 qk/0 st/0 mT/1 ao2/3 o/0 o2T/2 sc0/1 sc1/1 "
                         "sc2/1 onT/0 cT/0 ao/0 k2/0 v2/0 sc3/1 x2T/3 x1T/0", emit)

            gate_logits(3)

            pe.wait_ge(s_cnt_sel, 1)
            pe.wait_ge(s_o2Tl, NB)
            pe.matmul(bank[5][:, 0:(NB + 1) * NE], before[:], selh[:].rearrange("p b e -> p (b e)"), start=True, stop=False)
            for b in range(NB):
                dst = bank[5][:, (b + 1) * NE:(NB + 1) * NE].rearrange("p (r e) -> p r e", e=NE)
                last = pe.matmul(dst, ones[:], selh[:, b, :].unsqueeze(1).to_broadcast([P, NB - b, NE]),
                                 start=False, stop=(b == NB - 1))
            last.then_inc(s_cnt_ps, 1)

            for b in range(NB):
                for k in range(2):
                    n = 2 * b + k
                    pe.wait_ge(s_hot, 2 * (b // 4) + k + 1)
                    pe.wait_ge(s_cols, 4 * (b // 4) + 2 * k + 2)
                    last = pe.matmul(bank[6][:, 0:2 * MAXC], HOT[k][:, b, :],
                                     COLS[:, k, b, :, :].rearrange("p v c -> p (v c)"),
                                     start=(n == 0), stop=(n == 2 * NB - 1))
            last.then_inc(s_tab_ps, 1)

            def tile_turn(i, k):
                t = TR * i + k
                for f in range(HALVES):
                    pe.wait_ge(s_tld[k][f], 16 * i + 16)
                if past(t, 2):
                    pe.wait_ge(s_tTl, t - 1)
                for f in range(HALVES):
                    for c in range(KC):
                        last = pe.transpose(bank[6 + k % 2][:, c * TW + f * P:c * TW + (f + 1) * P],
                                            TX[k][:, f, c * P:(c + 1) * P], ident[:])
                last.then_inc(s_tT, 1)

            def expert_of(i, k):
                return pe.value_load(texp_v[:, i + k // TR, k % TR:k % TR + 1], min_val=0, max_val=NE - 1)

            def up(t, k, e):
                pe.wait_ge(s_tTl, t + 1)
                if past(t, 2):
                    pe.wait_ge(s_hf, 2 * (t - 1))
                wi_h, wi_l = (EW_v[:, e, lo, 0, :].rearrange("p (k h) -> p k h", k=KC) for lo in range(2))
                for h in range(HC):
                    last = split3(pe, bank[2 * (k % 2) + h // 2][:, h % 2 * TW:(h % 2 + 1) * TW],
                                  lambda c: wi_h[:, c, h * P:(h + 1) * P], lambda c: wi_l[:, c, h * P:(h + 1) * P],
                                  lambda c: TXh[k % 2][:, c, :], lambda c: TXl[k % 2][:, c, :])
                last.then_inc(s_up, 1)

            def down(t, k, e, following=None):
                loaded = None
                pe.wait_ge(s_hl, 2 * t + 2)
                if past(t, 2):
                    pe.wait_ge(s_y, 2 * (t - 1))
                wo_h, wo_l = (EW_v[:, e, lo, 1, :].rearrange("p (k d) -> p k d", k=HC) for lo in range(2))
                for h in range(HC):
                    for i, (a, b) in enumerate(((HH, wo_h), (HH, wo_l), (HL, wo_h))):
                        for f in range(HALVES):
                            last = pe.matmul(bank[4 + k % 2][:, f * D:(f + 1) * D], a[k % 2][:, h, f * P:(f + 1) * P],
                                             b[:, h, :], start=(h == 0 and i == 0 and f == 0),
                                             stop=(h == HC - 1 and i == 2 and f == HALVES - 1))
                    if h == 0 and following is not None:
                        loaded = expert_of(*following)
                last.then_inc(s_dn, 1)
                return loaded
            pe.wait_ge(s_texp, 1)
            pe.wait_ge(s_ewl, 2 * NE)
            pe.wait_ge(s_table, 2)
            tile_turn(0, 0)
            tile_turn(0, 1)
            up(0, 0, expert_of(0, 0))

            def tiles(i, n=TR):
                e, e_next = expert_of(i, 0), expert_of(i, 1)
                for k in range(n):
                    if within(TR * i + k + 2):
                        tile_turn(i + (k + 2) // TR, (k + 2) % TR)
                    if within(TR * i + k + 1):
                        up(TR * i + k + 1, k + 1, e_next)
                    e, e_next = e_next, down(TR * i + k, k, e, (i, k + 2) if k + 1 < n else None)
            tiles(0)
            with pe.Fori(1, MAXI - 1) as i:
                tiles(i)
            tiles(MAXI - 1, MAXT - TR * (MAXI - 1))


def kernel(**inputs):
    import concourse.bacc as bacc
    from concourse.bass_utils import run_bass_kernel_spmd

    a = {k: np.asarray(v) for k, v in inputs.items()}

    def chunked(m):
        return m.reshape(-1, P, m.shape[-1]).transpose(1, 0, 2)

    order = ["attn_Wq", "attn_Wv", "attn_Wk", "attn_Wo", "xattn_Wq", "xattn_Wk", "xattn_Wv", "xattn_Wo"]
    wpack = chunked(np.concatenate([a["L0_" + n].T for n in order], axis=1))
    rows = np.concatenate([a["L0_" + n] for n in ("attn_bq", "attn_bv", "attn_bo", "xattn_bv", "xattn_bo")])
    vecs = np.concatenate([a["L0_" + n].reshape(KC, P).T
                           for n in ("attn_bk", "xattn_bk", "xattn_bq", "attn_ln_g", "attn_ln_b")], axis=1)
    arrays = {
        "x": a["x"],
        "ctx": a["ctx_1024"],
        "wpack": wpack,
        "rows": rows,
        "vecs": vecs,
        "wg1": chunked(a["L0_ffn_wg1"]),
        "bg1": a["L0_ffn_bg1"].reshape(G, 1),
        "wg2": a["L0_ffn_wg2"],
        "w_in": a["L0_ffn_w_in"].reshape(NE, KC, P, HID).transpose(0, 2, 1, 3),
        "w_out": a["L0_ffn_w_out"].reshape(NE, HC, P, D).transpose(0, 2, 1, 3),
    }
    arrays = {k: np.ascontiguousarray(v) for k, v in arrays.items()}
    nc = bacc.Bacc("TRN2", target_bir_lowering=False, num_devices=1)
    args = [nc.dram_tensor(k, v.shape, mybir.dt.from_np(v.dtype), kind="ExternalInput").ap()
            for k, v in arrays.items()]
    out = nc.dram_tensor("out", (NB, S, D), f32, kind="ExternalOutput").ap()
    decoder_layer(nc, *args, out)
    r = run_bass_kernel_spmd(nc, [arrays], core_ids=[0])
    return r.results[0]["out"]
```
